# Optimizing a Trainium2 kernel written in Bass

```python
import numpy as np
import jax
import jax.numpy as jnp

def _softmax(x, axis=-1):
    return jax.nn.softmax(x, axis=axis)

def _gelu(x):
    return jax.nn.gelu(x, approximate=True)

def _silu(x):
    return jax.nn.silu(x)

def _sigmoid(x):
    return jax.nn.sigmoid(x)

def _layernorm(x, axis=-1, eps=1e-05):
    m = jnp.mean(x, axis=axis, keepdims=True)
    v = jnp.var(x, axis=axis, keepdims=True)
    return (x - m) / jnp.sqrt(v + eps)

def _scatter_add(tgt, idx, src, axis=0):
    return tgt.at[idx].add(src)

def _segment_sum(src, seg, n):
    return jax.ops.segment_sum(src, seg, n)
kernel_name = 'mk_vit_tower_cls_d2_tok_img1024_r4_e57fae'

def setup_inputs(seed: int=0):
    np.random.seed(seed)
    _w = jnp.asarray

    def _rec_inputs():
        import jax
        import jax.numpy as jnp
        _rk = jax.random.key(seed)
        x = -0.000392918 + 0.999932 * jax.random.normal(jax.random.fold_in(_rk, 1), (32, 256, 256, 1), jnp.float32)
        cls_tok = 0.02 * jax.random.normal(jax.random.fold_in(_rk, 5), (1, 1, 256), jnp.float32)
        return (x, cls_tok)
    x, cls_tok = _rec_inputs()

    def _L0_tok_setup():
        import jax, jax.numpy as jnp
        import numpy as np
        INV_SQRT2 = 0.7071067811865476
        LEVEL = 3

        def _split(x, axis):
            ax = axis % x.ndim
            sl0 = [slice(None)] * x.ndim
            sl0[ax] = slice(0, None, 2)
            sl1 = [slice(None)] * x.ndim
            sl1[ax] = slice(1, None, 2)
            x0, x1 = (x[tuple(sl0)], x[tuple(sl1)])
            return ((x0 + x1) * INV_SQRT2, (x0 - x1) * INV_SQRT2)

        def _merge(lo, hi, axis):
            ax = axis % lo.ndim
            e = (lo + hi) * INV_SQRT2
            o = (lo - hi) * INV_SQRT2
            s = jnp.stack([e, o], axis=ax + 1)
            shape = list(lo.shape)
            shape[ax] *= 2
            return s.reshape(shape)

        def _dwt2(x):
            lo, hi = _split(x, -1)
            a, h = _split(lo, -2)
            v, d = _split(hi, -2)
            return (a, h, v, d)

        def _idwt2(a, h, v, d):
            lo = _merge(a, h, -2)
            hi = _merge(v, d, -2)
            return _merge(lo, hi, -1)
        key = jax.random.key(seed)
        ks = jax.random.split(key, 8)
        B, H, W = (16, 256, 256)
        x = jax.random.normal(ks[0], (B, H, W, 1), dtype=jnp.float32)
        na = H // 8 * (W // 8)
        n2 = H // 4 * (W // 4)
        n1 = H // 2 * (W // 2)
        scale = 0.02
        Wa = jax.random.normal(ks[1], (na, 1), dtype=jnp.float32) * scale
        ba = jnp.zeros((1,), jnp.float32)
        Wd1 = jax.random.normal(ks[2], (3 * na, 3), dtype=jnp.float32) * scale
        bd1 = jnp.zeros((3,), jnp.float32)
        Wd2 = jax.random.normal(ks[3], (3 * n2, 3), dtype=jnp.float32) * scale
        bd2 = jnp.zeros((3,), jnp.float32)
        Wd3 = jax.random.normal(ks[4], (3 * n1, 3), dtype=jnp.float32) * scale
        bd3 = jnp.zeros((3,), jnp.float32)
        return {'x': x, 'Wa': Wa, 'ba': ba, 'Wd1': Wd1, 'bd1': bd1, 'Wd2': Wd2, 'bd2': bd2, 'Wd3': Wd3, 'bd3': bd3}
    _L0_tok_all = _L0_tok_setup()
    _L0_tok_in = {k: v for k, v in _L0_tok_all.items() if k in ('Wa', 'ba', 'Wd1', 'bd1', 'Wd2', 'bd2', 'Wd3', 'bd3')}
    del _L0_tok_all

    def _L0_attn_setup():
        import math
        import jax, jax.numpy as jnp
        import numpy as np
        DIM = 256
        N_HEADS = 16
        N_KV_HEADS = 4
        HEAD_DIM = 64
        WINDOW = 128
        EPS = 1e-06
        B, S = (2, 512)

        def _alibi_slopes(n_heads):

            def pow2(n):
                r = 2.0 ** (-8.0 / n)
                return np.array([r ** (i + 1) for i in range(n)], dtype=np.float32)
            if math.log2(n_heads).is_integer():
                return pow2(n_heads)
            m = 2 ** math.floor(math.log2(n_heads))
            return np.concatenate([pow2(m), pow2(2 * m)[::2][:n_heads - m]])

        def _rmsnorm(x, w, eps=EPS):
            var = jnp.mean(x * x, axis=-1, keepdims=True)
            return x * jax.lax.rsqrt(var + eps) * w
        key = jax.random.key(seed)
        ks = jax.random.split(key, 8)
        x = jax.random.normal(ks[0], (B, S, DIM), dtype=jnp.float32)
        wq = 0.02 * jax.random.normal(ks[1], (N_HEADS * HEAD_DIM, DIM), dtype=jnp.float32)
        wk = 0.02 * jax.random.normal(ks[2], (N_KV_HEADS * HEAD_DIM, DIM), dtype=jnp.float32)
        wv = 0.02 * jax.random.normal(ks[3], (N_KV_HEADS * HEAD_DIM, DIM), dtype=jnp.float32)
        wo = 0.02 * jax.random.normal(ks[4], (DIM, N_HEADS * HEAD_DIM), dtype=jnp.float32)
        q_norm_w = jnp.ones((N_HEADS * HEAD_DIM,), dtype=jnp.float32)
        k_norm_w = jnp.ones((N_KV_HEADS * HEAD_DIM,), dtype=jnp.float32)
        return {'x': x, 'wq': wq, 'wk': wk, 'wv': wv, 'wo': wo, 'q_norm_w': q_norm_w, 'k_norm_w': k_norm_w}
    _L0_attn_all = _L0_attn_setup()
    _L0_attn_in = {k: v for k, v in _L0_attn_all.items() if k in ('wq', 'wk', 'wv', 'wo', 'q_norm_w', 'k_norm_w')}
    del _L0_attn_all

    def _L0_ffn_setup():
        import jax, jax.numpy as jnp
        import numpy as np
        FP8_MAX = 448.0
        FP8 = jnp.float8_e4m3fn
        key = jax.random.key(seed)
        kx, kw, kb = jax.random.split(key, 3)
        B, S, D_in, D_out = (4, 2048, 256, 256)
        x = jax.random.normal(kx, (B, S, D_in), dtype=jnp.float32)
        w = jax.random.normal(kw, (D_out, D_in), dtype=jnp.float32) * 0.02
        weight_scale = jnp.maximum(jnp.max(jnp.abs(w)), 1e-12) / FP8_MAX
        weight = (w / weight_scale).astype(FP8)
        bias = jax.random.normal(kb, (D_out,), dtype=jnp.float32) * 0.01
        return {'x': x, 'weight': weight, 'weight_scale': weight_scale, 'bias': bias}
    _L0_ffn_all = _L0_ffn_setup()
    _L0_ffn_in = {k: v for k, v in _L0_ffn_all.items() if k in ('weight', 'weight_scale', 'bias')}
    del _L0_ffn_all

    def _L1_attn_setup():
        import jax, jax.numpy as jnp
        import numpy as np
        DIM = 256
        NUM_HEADS = 16
        HEAD_DIM = DIM // NUM_HEADS
        EPS = 1e-06

        def layer_norm(x, gamma, beta):
            mu = jnp.mean(x, axis=-1, keepdims=True)
            var = jnp.mean(jnp.square(x - mu), axis=-1, keepdims=True)
            return (x - mu) / jnp.sqrt(var + EPS) * gamma + beta

        def apply_rope(q, k):
            seq_len, head_dim = (q.shape[1], q.shape[3])
            half = head_dim // 2
            freq_range = jnp.arange(half, dtype=jnp.float32) / half
            inv_freq = 1.0 / 10000.0 ** freq_range
            t = jnp.arange(seq_len, dtype=jnp.float32)
            freqs = jnp.outer(t, inv_freq)
            emb = jnp.concatenate([freqs, freqs], axis=-1)
            cos = jnp.cos(emb)[None, :, None, :]
            sin = jnp.sin(emb)[None, :, None, :]

            def rotate_half(x):
                x1, x2 = (x[..., :half], x[..., half:])
                return jnp.concatenate([-x2, x1], axis=-1)
            return (q * cos + rotate_half(q) * sin, k * cos + rotate_half(k) * sin)
        key = jax.random.key(seed)
        ks = jax.random.split(key, 4)
        B, S = (2, 512)
        x = jax.random.normal(ks[0], (B, S, DIM), dtype=jnp.float32)
        lim_qkv = float(np.sqrt(6.0 / (DIM + 3 * DIM)))
        w_qkv = jax.random.uniform(ks[1], (3 * DIM, DIM), dtype=jnp.float32, minval=-lim_qkv, maxval=lim_qkv)
        lim_p = float(np.sqrt(6.0 / (DIM + DIM)))
        w_proj = jax.random.uniform(ks[2], (DIM, DIM), dtype=jnp.float32, minval=-lim_p, maxval=lim_p)
        b_proj = jnp.zeros((DIM,), dtype=jnp.float32)
        q_gamma = jnp.ones((HEAD_DIM,), dtype=jnp.float32)
        q_beta = jnp.zeros((HEAD_DIM,), dtype=jnp.float32)
        k_gamma = jnp.ones((HEAD_DIM,), dtype=jnp.float32)
        k_beta = jnp.zeros((HEAD_DIM,), dtype=jnp.float32)
        return {'x': x, 'w_qkv': w_qkv, 'w_proj': w_proj, 'b_proj': b_proj, 'q_gamma': q_gamma, 'q_beta': q_beta, 'k_gamma': k_gamma, 'k_beta': k_beta}
    _L1_attn_all = _L1_attn_setup()
    _L1_attn_in = {k: v for k, v in _L1_attn_all.items() if k in ('w_qkv', 'w_proj', 'b_proj', 'q_gamma', 'q_beta', 'k_gamma', 'k_beta')}
    del _L1_attn_all

    def _L1_ffn_setup():
        import jax, jax.numpy as jnp
        import numpy as np
        E = 8
        G = 4
        LG = 2
        TOPK = 2
        ROUTE_SCALE = 1.0

        def _grouped_mm(x, w, counts):
            counts = counts.astype(jnp.int32)
            if hasattr(jax.lax, 'ragged_dot'):
                return jax.lax.ragged_dot(x, w, counts)
            offs = jnp.cumsum(counts)
            eid = jnp.searchsorted(offs, jnp.arange(x.shape[0]), side='right')
            oh = jax.nn.one_hot(eid, w.shape[0], dtype=x.dtype)
            return jnp.einsum('nd,ne,edh->nh', x, oh, w)
        key = jax.random.key(seed)
        ks = jax.random.split(key, 8)
        bs, slen, dim, hid, shid = (2, 512, 256, 128, 256)
        std = 0.02
        return {'x': jax.random.normal(ks[0], (bs, slen, dim), jnp.float32), 'w_gate': jax.random.normal(ks[1], (E, dim), jnp.float32) * std, 'w1': jax.random.normal(ks[2], (E, dim, hid), jnp.float32) * std, 'w2': jax.random.normal(ks[3], (E, hid, dim), jnp.float32) * std, 'w3': jax.random.normal(ks[4], (E, dim, hid), jnp.float32) * std, 'sw1': jax.random.normal(ks[5], (shid, dim), jnp.float32) * std, 'sw2': jax.random.normal(ks[6], (dim, shid), jnp.float32) * std, 'sw3': jax.random.normal(ks[7], (shid, dim), jnp.float32) * std, 'expert_bias': jnp.zeros((E,), jnp.float32)}
    _L1_ffn_all = _L1_ffn_setup()
    _L1_ffn_in = {k: v for k, v in _L1_ffn_all.items() if k in ('w_gate', 'w1', 'w2', 'w3', 'sw1', 'sw2', 'sw3', 'expert_bias')}
    del _L1_ffn_all
    return {'x': x, 'cls_tok': cls_tok, 'L0_tok_Wa': _L0_tok_in['Wa'], 'L0_tok_ba': _L0_tok_in['ba'], 'L0_tok_Wd1': _L0_tok_in['Wd1'], 'L0_tok_bd1': _L0_tok_in['bd1'], 'L0_tok_Wd2': _L0_tok_in['Wd2'], 'L0_tok_bd2': _L0_tok_in['bd2'], 'L0_tok_Wd3': _L0_tok_in['Wd3'], 'L0_tok_bd3': _L0_tok_in['bd3'], 'L0_attn_wq': _L0_attn_in['wq'], 'L0_attn_wk': _L0_attn_in['wk'], 'L0_attn_wv': _L0_attn_in['wv'], 'L0_attn_wo': _L0_attn_in['wo'], 'L0_attn_q_norm_w': _L0_attn_in['q_norm_w'], 'L0_attn_k_norm_w': _L0_attn_in['k_norm_w'], 'L0_ffn_weight': _L0_ffn_in['weight'], 'L0_ffn_weight_scale': _L0_ffn_in['weight_scale'], 'L0_ffn_bias': _L0_ffn_in['bias'], 'L1_attn_w_qkv': _L1_attn_in['w_qkv'], 'L1_attn_w_proj': _L1_attn_in['w_proj'], 'L1_attn_b_proj': _L1_attn_in['b_proj'], 'L1_attn_q_gamma': _L1_attn_in['q_gamma'], 'L1_attn_q_beta': _L1_attn_in['q_beta'], 'L1_attn_k_gamma': _L1_attn_in['k_gamma'], 'L1_attn_k_beta': _L1_attn_in['k_beta'], 'L1_ffn_w_gate': _L1_ffn_in['w_gate'], 'L1_ffn_w1': _L1_ffn_in['w1'], 'L1_ffn_w2': _L1_ffn_in['w2'], 'L1_ffn_w3': _L1_ffn_in['w3'], 'L1_ffn_sw1': _L1_ffn_in['sw1'], 'L1_ffn_sw2': _L1_ffn_in['sw2'], 'L1_ffn_sw3': _L1_ffn_in['sw3'], 'L1_ffn_expert_bias': _L1_ffn_in['expert_bias']}

def reference(x, cls_tok, L0_tok_Wa, L0_tok_ba, L0_tok_Wd1, L0_tok_bd1, L0_tok_Wd2, L0_tok_bd2, L0_tok_Wd3, L0_tok_bd3, L0_attn_wq, L0_attn_wk, L0_attn_wv, L0_attn_wo, L0_attn_q_norm_w, L0_attn_k_norm_w, L0_ffn_weight, L0_ffn_weight_scale, L0_ffn_bias, L1_attn_w_qkv, L1_attn_w_proj, L1_attn_b_proj, L1_attn_q_gamma, L1_attn_q_beta, L1_attn_k_gamma, L1_attn_k_beta, L1_ffn_w_gate, L1_ffn_w1, L1_ffn_w2, L1_ffn_w3, L1_ffn_sw1, L1_ffn_sw2, L1_ffn_sw3, L1_ffn_expert_bias):
    import jax
    import jax.numpy as jnp

    def _L0_tok_ref(x, Wa, ba, Wd1, bd1, Wd2, bd2, Wd3, bd3):
        import jax, jax.numpy as jnp
        import numpy as np
        INV_SQRT2 = 0.7071067811865476
        LEVEL = 3

        def _split(x, axis):
            ax = axis % x.ndim
            sl0 = [slice(None)] * x.ndim
            sl0[ax] = slice(0, None, 2)
            sl1 = [slice(None)] * x.ndim
            sl1[ax] = slice(1, None, 2)
            x0, x1 = (x[tuple(sl0)], x[tuple(sl1)])
            return ((x0 + x1) * INV_SQRT2, (x0 - x1) * INV_SQRT2)

        def _merge(lo, hi, axis):
            ax = axis % lo.ndim
            e = (lo + hi) * INV_SQRT2
            o = (lo - hi) * INV_SQRT2
            s = jnp.stack([e, o], axis=ax + 1)
            shape = list(lo.shape)
            shape[ax] *= 2
            return s.reshape(shape)

        def _dwt2(x):
            lo, hi = _split(x, -1)
            a, h = _split(lo, -2)
            v, d = _split(hi, -2)
            return (a, h, v, d)

        def _idwt2(a, h, v, d):
            lo = _merge(a, h, -2)
            hi = _merge(v, d, -2)
            return _merge(lo, hi, -1)
        img = x[..., 0]
        B = img.shape[0]
        details = []
        cur = img
        for _ in range(LEVEL):
            cur, h, v, d = _dwt2(cur)
            details.append((h, v, d))
        aw = jax.nn.sigmoid(cur.reshape(B, -1) @ Wa + ba)
        rec = cur * aw[:, :, None]
        det_params = [(Wd1, bd1), (Wd2, bd2), (Wd3, bd3)]
        for (h, v, d), (Wd, bd) in zip(reversed(details), det_params):
            flat = jnp.stack([h, v, d], axis=1).reshape(B, -1)
            w = jax.nn.softmax(flat @ Wd + bd, axis=-1)
            rec = _idwt2(rec, h * w[:, 0, None, None], v * w[:, 1, None, None], d * w[:, 2, None, None])
        return rec

    def _L0_attn_ref(x, wq, wk, wv, wo, q_norm_w, k_norm_w):
        import math
        import jax, jax.numpy as jnp
        import numpy as np
        DIM = 256
        N_HEADS = 16
        N_KV_HEADS = 4
        HEAD_DIM = 64
        WINDOW = 128
        EPS = 1e-06
        B, S = (2, 512)

        def _alibi_slopes(n_heads):

            def pow2(n):
                r = 2.0 ** (-8.0 / n)
                return np.array([r ** (i + 1) for i in range(n)], dtype=np.float32)
            if math.log2(n_heads).is_integer():
                return pow2(n_heads)
            m = 2 ** math.floor(math.log2(n_heads))
            return np.concatenate([pow2(m), pow2(2 * m)[::2][:n_heads - m]])

        def _rmsnorm(x, w, eps=EPS):
            var = jnp.mean(x * x, axis=-1, keepdims=True)
            return x * jax.lax.rsqrt(var + eps) * w
        bsz, seqlen, _ = x.shape
        repeats = N_HEADS // N_KV_HEADS
        xq = _rmsnorm(x @ wq.T, q_norm_w)
        xk = _rmsnorm(x @ wk.T, k_norm_w)
        xv = x @ wv.T
        q = xq.reshape(bsz, seqlen, N_HEADS, HEAD_DIM).transpose(0, 2, 1, 3)
        k = xk.reshape(bsz, seqlen, N_KV_HEADS, HEAD_DIM).transpose(0, 2, 1, 3)
        v = xv.reshape(bsz, seqlen, N_KV_HEADS, HEAD_DIM).transpose(0, 2, 1, 3)
        k = jnp.repeat(k, repeats, axis=1)
        v = jnp.repeat(v, repeats, axis=1)
        pos = jnp.arange(seqlen)
        rel = pos[None, :] - pos[:, None]
        slopes = jnp.asarray(_alibi_slopes(N_HEADS))
        bias = slopes[:, None, None] * rel[None].astype(x.dtype)
        masked = (rel > 0) | (rel < -WINDOW)
        bias = jnp.where(masked[None], -jnp.inf, bias)
        scale = 1.0 / math.sqrt(HEAD_DIM)
        scores = jnp.einsum('bhqd,bhkd->bhqk', q, k) * scale + bias[None]
        probs = jax.nn.softmax(scores, axis=-1)
        y = jnp.einsum('bhqk,bhkd->bhqd', probs, v)
        y = y.transpose(0, 2, 1, 3).reshape(bsz, seqlen, N_HEADS * HEAD_DIM)
        return y @ wo.T

    def _L0_ffn_ref(x, weight, weight_scale, bias):
        import jax, jax.numpy as jnp
        import numpy as np
        FP8_MAX = 448.0
        FP8 = jnp.float8_e4m3fn
        amax = jnp.max(jnp.abs(x), axis=-1, keepdims=True)
        x_scale = jnp.maximum(amax, 1e-12) / FP8_MAX
        qinput = (x / x_scale).astype(FP8)
        A = qinput.astype(x.dtype) * x_scale
        Bm = weight.astype(x.dtype) * weight_scale
        out = jnp.einsum('bsk,nk->bsn', A, Bm) + bias
        return out.astype(x.dtype)

    def _L1_attn_ref(x, w_qkv, w_proj, b_proj, q_gamma, q_beta, k_gamma, k_beta):
        import jax, jax.numpy as jnp
        import numpy as np
        DIM = 256
        NUM_HEADS = 16
        HEAD_DIM = DIM // NUM_HEADS
        EPS = 1e-06

        def layer_norm(x, gamma, beta):
            mu = jnp.mean(x, axis=-1, keepdims=True)
            var = jnp.mean(jnp.square(x - mu), axis=-1, keepdims=True)
            return (x - mu) / jnp.sqrt(var + EPS) * gamma + beta

        def apply_rope(q, k):
            seq_len, head_dim = (q.shape[1], q.shape[3])
            half = head_dim // 2
            freq_range = jnp.arange(half, dtype=jnp.float32) / half
            inv_freq = 1.0 / 10000.0 ** freq_range
            t = jnp.arange(seq_len, dtype=jnp.float32)
            freqs = jnp.outer(t, inv_freq)
            emb = jnp.concatenate([freqs, freqs], axis=-1)
            cos = jnp.cos(emb)[None, :, None, :]
            sin = jnp.sin(emb)[None, :, None, :]

            def rotate_half(x):
                x1, x2 = (x[..., :half], x[..., half:])
                return jnp.concatenate([-x2, x1], axis=-1)
            return (q * cos + rotate_half(q) * sin, k * cos + rotate_half(k) * sin)
        B, S, C = x.shape
        H, D = (NUM_HEADS, HEAD_DIM)
        qkv = jnp.einsum('bsc,oc->bso', x, w_qkv).reshape(B, S, 3, H, D)
        q = layer_norm(qkv[:, :, 0], q_gamma, q_beta)
        k = layer_norm(qkv[:, :, 1], k_gamma, k_beta)
        v = qkv[:, :, 2]
        q, k = apply_rope(q, k)
        scale = D ** (-0.5)
        q = q.astype(jnp.float32) * scale
        k = k.astype(jnp.float32)
        v = v.astype(jnp.float32)
        attn = jnp.einsum('bqhd,bkhd->bhqk', q, k)
        attn = jax.nn.softmax(attn, axis=-1)
        out = jnp.einsum('bhqk,bkhd->bqhd', attn, v).reshape(B, S, C)
        out = jnp.einsum('bsc,oc->bso', out, w_proj) + b_proj
        return out

    def _L1_ffn_ref(x, w_gate, w1, w2, w3, sw1, sw2, sw3, expert_bias):
        import jax, jax.numpy as jnp
        import numpy as np
        E = 8
        G = 4
        LG = 2
        TOPK = 2
        ROUTE_SCALE = 1.0

        def _grouped_mm(x, w, counts):
            counts = counts.astype(jnp.int32)
            if hasattr(jax.lax, 'ragged_dot'):
                return jax.lax.ragged_dot(x, w, counts)
            offs = jnp.cumsum(counts)
            eid = jnp.searchsorted(offs, jnp.arange(x.shape[0]), side='right')
            oh = jax.nn.one_hot(eid, w.shape[0], dtype=x.dtype)
            return jnp.einsum('nd,ne,edh->nh', x, oh, w)
        bs, slen, dim = x.shape
        xf = x.reshape(-1, dim)
        N = xf.shape[0]
        logits = xf @ w_gate.T
        scores = jax.nn.softmax(logits.astype(jnp.float32), axis=-1)
        original = scores
        s = (scores + expert_bias).reshape(N, G, E // G)
        group_scores = jax.lax.top_k(s, 2)[0].sum(-1)
        top_groups = jax.lax.top_k(group_scores, LG)[1]
        keep = jnp.zeros((N, G), bool).at[jnp.arange(N)[:, None], top_groups].set(True)
        masked = jnp.where(keep[:, :, None], s, -jnp.inf).reshape(N, E)
        topk_idx = jax.lax.top_k(masked, TOPK)[1]
        weights = (jnp.take_along_axis(original, topk_idx, axis=1) * ROUTE_SCALE).astype(x.dtype)
        counts = jnp.bincount(topk_idx.reshape(-1), length=E)
        flat_idx = topk_idx.reshape(-1)
        routed_in = xf[flat_idx]
        routed_in = (routed_in.astype(jnp.float32) * weights.reshape(-1, 1)).astype(x.dtype)
        h = jax.nn.silu(_grouped_mm(routed_in, w1, counts)) * _grouped_mm(routed_in, w3, counts)
        routed_out = _grouped_mm(h, w2, counts)
        shared = jax.nn.silu(xf @ sw1.T) * (xf @ sw3.T) @ sw2.T
        out = shared.at[flat_idx].add(routed_out)
        return out.reshape(bs, slen, dim)
    h = _L0_tok_ref(x, L0_tok_Wa, L0_tok_ba, L0_tok_Wd1, L0_tok_bd1, L0_tok_Wd2, L0_tok_bd2, L0_tok_Wd3, L0_tok_bd3)
    h = jnp.concatenate([jnp.broadcast_to(cls_tok, (h.shape[0], 1, h.shape[2])), h], axis=1)
    h = h + _L0_attn_ref(_layernorm(h, axis=-1), L0_attn_wq, L0_attn_wk, L0_attn_wv, L0_attn_wo, L0_attn_q_norm_w, L0_attn_k_norm_w)
    h = h + _L0_ffn_ref(_layernorm(h, axis=-1), L0_ffn_weight, L0_ffn_weight_scale, L0_ffn_bias)
    h = h + _L1_attn_ref(_layernorm(h, axis=-1), L1_attn_w_qkv, L1_attn_w_proj, L1_attn_b_proj, L1_attn_q_gamma, L1_attn_q_beta, L1_attn_k_gamma, L1_attn_k_beta)
    h = h + _L1_ffn_ref(_layernorm(h, axis=-1), L1_ffn_w_gate, L1_ffn_w1, L1_ffn_w2, L1_ffn_w3, L1_ffn_sw1, L1_ffn_sw2, L1_ffn_sw3, L1_ffn_expert_bias)
    return h

_drawn_inputs = setup_inputs


def setup_inputs(seed=0):
    import zlib

    import numpy as np

    out = dict(_drawn_inputs(seed))
    spreads = {'L0_tok_bd1': (0.0, 0.392),
     'L0_tok_bd2': (0.0, 0.535),
     'L0_tok_bd3': (0.0, 0.536),
     'L0_attn_q_norm_w': (1.0, 0.536),
     'L0_attn_k_norm_w': (1.0, 0.2),
     'L1_attn_b_proj': (0.0, 0.1),
     'L1_attn_q_gamma': (1.0, 0.2),
     'L1_attn_q_beta': (0.0, 0.785),
     'L1_attn_k_gamma': (1.0, 0.6),
     'L1_attn_k_beta': (0.0, 0.772),
     'L1_ffn_expert_bias': (0.0, 0.423)}
    factors = {'L1_ffn_w_gate': 8.0}
    for name, (base, spread) in spreads.items():
        noise = np.random.default_rng([zlib.crc32(name.encode()), seed]).standard_normal(out[name].shape)
        drawn = base * np.exp(spread * noise) if base else spread * noise
        out[name] = jnp.asarray(drawn.astype(out[name].dtype))
    for name, factor in factors.items():
        out[name] = (out[name] * factor).astype(out[name].dtype)
    return out
```

```python
from contextlib import ExitStack

import numpy as np

import concourse.bass as bass
from concourse import mybir

ALU = mybir.AluOpType
ACT = mybir.ActivationFunctionType
F32 = mybir.dt.float32
BF16 = mybir.dt.bfloat16
U8 = mybir.dt.uint8
I32 = mybir.dt.int32
AX_X = mybir.AxisListType.X
ABSMAX = bass.bass_isa.ReduceOp.absmax

P = 128
NB = 32
T = 257
TP = T + 1
C = 2
TT = 86
TILES = [(0, 86), (86, 86), (172, 85)]
H = 16
KV = 4
WINDOW = 128
NE = 8
HID = 128
NCOL = NB * 3

QR0 = [(0, 214), (86, 171), (172, 85)]
QC0 = [0, 214, 385]
W0 = 470
KR0 = [(0, 86), (0, 172), (44, 213)]
KC0 = [0, 86, 258]
W2 = 471
MASKED = -1e30
SLOPES = [float(np.float32(np.float32(2.0 ** (-8.0 / H)) ** np.float32(n + 1))) for n in range(H)]


class Signal:

    def __init__(self, sem, per):
        self.sem, self.per = sem, per

    def wait(self, eng, i, k):
        eng.wait_ge(self.sem, i * self.per + k)


class Chain:

    def __init__(self, eng, sem, per, i):
        self.eng, self.sem, self.per, self.i, self.n = eng, sem, per, i, 0

    def mark(self, ins):
        self.n += 1
        ins.then_inc(self.sem, 1)

    def sync(self):
        self.eng.wait_ge(self.sem, self.i * self.per + self.n)

    def step(self, ins):
        self.mark(ins)
        self.sync()

    def end(self):
        assert self.n == self.per, (self.n, self.per)


def build_tower(nc, a, out):
    with ExitStack() as ctx:
        def sb(name, shape, dt=F32):
            return ctx.enter_context(nc.sbuf_tensor("t_" + name, shape, dt))

        def sem(name):
            return ctx.enter_context(nc.semaphore(name))

        def signal(name, per):
            return Signal(sem(name), per)

        PS = ctx.enter_context(nc.psum_tensor("PS", [P, 8, 512], F32))

        loads = []

        def table(name, shape, dt=F32):
            t = sb(name, shape, dt)
            loads.append((t, a[name]))
            return t

        wq0 = table("wq0", [P, C, 1024])
        wk0 = table("wk0", [P, C, 512])
        wv0 = table("wv0", [P, C, 256])
        wo0 = table("wo0", [P, 8, 256])
        qkw0 = table("qkw0", [P, 12])
        w8 = table("w8", [P, C, 256], U8)
        w8s = table("w8s", [P, 1])
        b8 = table("b8", [P, C])
        wqk1 = table("wqk1", [P, C, 512])
        wv1 = table("wv1", [P, C, 256])
        wp1 = table("wp1", [P, 4, 256])
        gb1 = table("gb1", [P, 4])
        wg = table("wg", [P, C, NE])
        sw13 = table("sw13", [P, C, 512])
        sw2 = table("sw2", [P, C, 256])
        ebias = table("ebias", [P, NE])
        clst = table("clst", [P, C])
        wdet = table("wdet", [P, 3, 512])
        dbias = table("dbias", [P, 10])
        dscale = table("dscale", [P, 10])
        wscale = table("wscale", [P, 10])
        ident = table("ident", [P, P])
        block16 = table("block16", [P, P])
        rotate = table("rotate", [P, P])
        spread = table("spread", [P, P])
        cosT = table("cosT", [P, T])
        sinT = table("sinT", [P, T])
        parity = table("parity", [P, 2])
        relm = table("relm", [TT, W0])
        biasf = sb("biasq", [P, H * W2], BF16)
        biasq = biasf[:, :].rearrange("p (h n) -> p h n", h=H)
        pick = sb("pick", [P, H, TT], BF16)
        pos = table("pos", [TT, NCOL, 2])
        valid = table("valid", [TT, NCOL])

        ones = sb("ones", [P, P])
        ones256 = sb("ones256", [P, P])
        ones1024 = sb("ones1024", [P, P])
        ones512 = sb("ones512", [P, P])
        eps = sb("eps", [P, 2])
        w8b = sb("w8b", [P, C, 256], BF16)
        wmean = sb("wmean", [P, C, 32])

        img = sb("img", [P, 512])
        lohi = sb("lohi", [P, 2, 256])
        coef = sb("coef", [P, 504])
        avg = sb("avg", [P, 128 + 32 + 8])
        dots = sb("dots", [P, 10])
        dotx = sb("dotx", [P, 384])
        z10 = sb("z10", [P, 10])
        mx3 = sb("mx3", [P, 3])
        e10 = sb("e10", [P, 10])
        s4 = sb("s4", [P, 4])
        w10 = sb("w10", [P, 2, 10])
        syn = sb("syn", [P, 3, 256])
        rec = sb("rec", [P, 8 + 32 + 128 + 512])
        relq = rec[0:TT, 0:W2]
        loads.append((relq, a["relq"]))
        h0 = sb("h0", [P, C, T])
        h1 = sb("h1", [P, C, T])
        h2 = sb("h2", [P, C, T])
        h3 = sb("h3", [P, C, T])
        cen = sb("cen", [P, C, T])
        csq = sb("csq", [P, C, T])
        rs = sb("rs", [P, 4, T])
        nt = sb("nt", [P, 4, T])
        xn = sb("xn", [P, C, T])
        qk = sb("qk", [P, 12, TP])
        sq = sb("sq", [P, 12, T])
        pr1 = sb("pr1", [P, 8, 3, T])
        p1f = pr1[:, :, :, :].rearrange("p h t n -> p (h t n)")
        y0 = p1f[:, 0:2056].rearrange("p (j t) -> p j t", j=8)
        qkb = p1f[:, 2056:3598].bitcast(BF16).rearrange("p (n t) -> p n t", n=12)
        pre = p1f[0:TT, 3598:4538].rearrange("p (b n) -> p b n", b=2)
        pr0 = p1f[0:TT, 4538:5948].rearrange("p (b n) -> p b n", b=3)
        vx = sb("vx", [TT, 3, KV, 192])
        mtok = sb("mtok", [TT, 3, H])
        shift = sb("shift", [P, T], BF16)
        rr = sb("rr", [P, T])
        fs = sb("fs", [P, 4, T])
        fy, fm = nt[:, 0:2, :], nt[:, 2:4, :]
        fq = sb("fq", [P, C, T], BF16)
        u1 = sb("u1", [P, 4, T])
        amax = u1[:, 0:2, :]
        qr = sb("qr", [P, 4, T])
        k1 = sb("k1", [P, 2, C, TP])
        q1b = sb("q1b", [P, C, TP], BF16)
        k1b = sb("k1b", [P, 2, C, T], BF16)
        v1x = sb("v1x", [TT, 3, H, 32])
        zz = sb("zz", [P, 4, T])
        osb = sb("osb", [TT, 3, 256])
        lg = sb("lg", [TT, NCOL, NE])

        tables_loaded = sem("tables_loaded")
        gates_zeroed = sem("gates_zeroed")
        dve_setup = sem("dve_setup")
        act_setup = sem("act_setup")
        image_loaded = sem("image_loaded")
        image_read = signal("image_read", 1)
        dots_ready = signal("dots_ready", 1)
        logits_summed = signal("logits_summed", 1)
        logits_shifted = signal("logits_shifted", 1)
        weights_exp = signal("weights_exp", 1)
        rec_ready = signal("rec_ready", 1)
        rec_turned = signal("rec_turned", 1)
        h_ready = signal("h_ready", 4)
        ln_mean = signal("ln_mean", 4)
        ln_centred = signal("ln_centred", 4)
        ln_squared = signal("ln_squared", 4)
        ln_var = signal("ln_var", 4)
        ln_guess = signal("ln_guess", 4)
        ln_done = [signal(f"ln{n}_done", 1) for n in range(4)]
        qk0_proj = signal("qk0_proj", 12)
        qk0_copied = signal("qk0_copied", 12)
        qk0_squared = signal("qk0_squared", 12)
        qk0_sums = signal("qk0_sums", 1)
        qk0_guess = signal("qk0_guess", 1)
        qk0_ready = signal("qk0_ready", 12)
        qk0_bf16 = signal("qk0_bf16", 2)
        v0_proj = signal("v0_proj", 3)
        v0_ready = signal("v0_ready", 3)
        rough0 = signal("rough0", H)
        rowmax0 = signal("rowmax0", H)
        max0_turned = signal("max0_turned", 1)
        shift0_ready = signal("shift0_ready", 1)
        scores0 = signal("scores0", H)
        biased0 = signal("biased0", H)
        probs0 = signal("probs0", H)
        pv0 = signal("pv0", H)
        y0_ready = signal("y0_ready", H)
        wo0_done = signal("wo0_done", 1)
        absmax_done = signal("absmax_done", 1)
        fq_ready = signal("fq_ready", 1)
        ffn0_done = signal("ffn0_done", 1)
        qk1_proj = signal("qk1_proj", 1)
        qk1_squared = signal("qk1_squared", 1)
        qk1_var = signal("qk1_var", 1)
        qk1_guess = signal("qk1_guess", 1)
        qk1_normed = signal("qk1_normed", 1)
        qk1_beta = signal("qk1_beta", 2)
        qk1_turned = signal("qk1_turned", 1)
        rope_done = signal("rope_done", 1)
        k1_ready = signal("k1_ready", 5)
        v1_proj = signal("v1_proj", 3)
        v1_ready = signal("v1_ready", 3)
        rough1 = signal("rough1", H)
        rowmax1 = signal("rowmax1", H)
        max1_turned = signal("max1_turned", 1)
        shift1_ready = signal("shift1_ready", 1)
        scores1 = signal("scores1", H)
        probs1 = signal("probs1", H)
        pv1 = signal("pv1", 4)
        z_ready = signal("z_ready", 4)
        sums_spread = signal("sums_spread", 1)
        y1_ready = signal("y1_ready", 1)
        proj1_done = signal("proj1_done", 1)
        gates = signal("gates", 1)
        gates_kept = signal("gates_kept", 2)
        up_done = signal("up_done", 1)
        silu_exp = signal("silu_exp", 1)
        hh_ready = signal("hh_ready", 1)
        out_tok = signal("out_tok", 3)
        out_copied = signal("out_copied", 3)
        out_stored = sem("out_stored")
        dve_chain = sem("dve_chain")
        act_chain = sem("act_chain")

        def inside(host, at, shape):
            names = " ".join("abcd"[:len(shape)])
            sizes = {"abcd"[n]: shape[n] for n in range(len(shape))}
            return host[0:TT, at:at + int(np.prod(shape))].rearrange(f"p ({names}) -> p {names}", **sizes)

        qkf = qk[:, :, :].rearrange("p n t -> p (n t)")
        sqf = sq[:, :, :].rearrange("p n t -> p (n t)")
        N8 = NCOL * NE
        prob = inside(p1f, 0, [NCOL, NE])
        rt = inside(p1f, N8, [NCOL, NE])
        rk = inside(p1f, 2 * N8, [NCOL, NE])
        onehot = inside(p1f, 3 * N8, [NCOL, 2, NE])
        group = inside(p1f, 5 * N8, [NCOL, 2, NE])
        ge = inside(qkf, 0, [NCOL * 2, NE])
        g4 = inside(qkf, 2 * N8, [3, NCOL, 4])
        oh = inside(sqf, 0, [8, 64])
        ohw = inside(sqf, 512, [8, 64])
        he = inside(sqf, 1024, [8, HID])
        hs = inside(sqf, 2048, [8, HID])
        r1 = sb("r1", [TT, NCOL])
        weight = sb("weight", [TT, NCOL, 2])
        cnt = sb("cnt", [P, NE])
        offs = sb("offs", [TT, NE])
        u8sb = vx[0:NE, :, :, :].rearrange("p t g n -> p (t g n)")[:, 0:NE * 2 * HID]\
            .rearrange("p (g s n) -> p g s n", s=2, n=HID)
        ew1 = wq0
        ew3 = wo0[:, :, :].rearrange("p (c a) n -> p c (a n)", c=C)
        ew2 = biasf[:, :].bitcast(F32)[:, 0:NE * 256]\
            .rearrange("p (g n) -> p g n", g=NE)
        images_done = sem("images_done")
        experts_loaded = sem("experts_loaded")
        u64 = sb("u64", [64, 2 * HID])
        oht = p1f[0:64, 7 * N8:7 * N8 + 8 * TT]
        acct = sb("acct", [64, HID])
        accT = sb("accT", [P, 64])
        r8 = osb[0:8, 0, :]

        table_hidden = signal("table_hidden", 1)
        hidden_copied = sem("hidden_copied")
        u64_loaded = sem("u64_loaded")
        pairs_stored = sem("pairs_stored")
        pair_dram = nc.dram_tensor("pair_hidden", (NE, NE, 2, HID), F32, kind="Internal").ap()
        counts_ready = sem("counts_ready")
        counts_summed = sem("counts_summed")
        onehots_ready = signal("onehots_ready", 1)
        onehots_turned = signal("onehots_turned", 1)
        turned_copied = signal("turned_copied", 1)
        routed_up = signal("routed_up", 1)
        routed_exp = signal("routed_exp", 1)
        routed_h = signal("routed_h", 1)
        routed_added = signal("routed_added", 1)
        acc_copied = sem("acc_copied")
        acc_turned = sem("acc_turned")
        accT_ready = sem("accT_ready")
        routed_out = sem("routed_out")
        rows_loaded = sem("rows_loaded")
        rows_ready = sem("rows_ready")
        rows_stored = sem("rows_stored")
        tail_chain = sem("tail_chain")

        SETUP_DVE = 46
        SETUP_ACT = 4
        DVE_STEPS = 113
        ACT_STEPS = 6
        ROUNDS = NCOL // 4

        def wait_next(eng, count, signal):
            eng.reg_add(count, count, 1)
            eng.wait_ge(tables_loaded, 16 * len(loads))
            eng.wait_ge(signal.sem, count)

        block = ctx.enter_context(nc.Block())

        @block.sync
        def _(sp):
            for t, src in loads:
                sp.dma_start(t if isinstance(t, bass.AP) else t[:], src).then_inc(tables_loaded, 16)
            with sp.Fori(0, NB) as i:
                image_read.wait(sp, i, 1)
                sp.dma_start(img[:, :], a["x"][bass.ds(i, 1), :, :].rearrange("a p n -> (a p) n"))\
                    .then_inc(image_loaded, 16)
            sp.wait_ge(images_done, 1)
            sp.dma_start(ew1[:, :, :], a["ew1"]).then_inc(experts_loaded, 16)
            sp.dma_start(ew3, a["ew3"].rearrange("p c n -> p c n")).then_inc(experts_loaded, 16)
            sp.dma_start(ew2, a["ew2"]).then_inc(experts_loaded, 16)
            sp.wait_ge(hidden_copied, 2)
            sp.dma_start(pair_dram, u8sb).then_inc(pairs_stored, 16)
            sp.wait_ge(pairs_stored, 16)
            sp.dma_start(u64[:, :], pair_dram.rearrange("e g s n -> (e g) (s n)")).then_inc(u64_loaded, 16)
            sp.wait_ge(out_stored, 32 * NB + 32)
            sp.dma_start(r8, out[NB - 1, 0:8, :]).then_inc(rows_loaded, 16)
            sp.wait_ge(rows_ready, 1)
            sp.dma_start(out[NB - 1, 0:8, :], r8).then_inc(rows_stored, 16)
            sp.wait_ge(rows_stored, 16)

        @block.gpsimd
        def _(pool):
            n_ln = pool.alloc_register("n_ln")
            pool.reg_mov(n_ln, 0)
            with pool.Fori(0, NB) as i:
                wait_next(pool, n_ln, ln_done[1])
                pool.partition_all_reduce(amax[:, :, :], xn[:, :, :], P, ABSMAX).then_inc(absmax_done.sem, 1)

        @block.tensor
        def _(pe):
            def mm(o, l, r, start=True, stop=True, loose=False):
                return pe.matmul(o, l, r, start=start, stop=stop, skip_group_check=loose)

            pe.wait_ge(tables_loaded, 16 * len(loads))
            pe.wait_ge(dve_setup, SETUP_DVE)
            pe.wait_ge(act_setup, SETUP_ACT)

            n_rec = pe.alloc_register("n_rec")
            pe.reg_mov(n_rec, 0)
            with pe.Fori(0, NB) as i:
                def layernorm(n, src):
                    h_ready.wait(pe, i, n + 1)
                    for c in range(C):
                        m = mm(PS[:, 6, 0:T], ones256[:, :], src[:, c, :], c == 0, c == C - 1)
                    m.then_inc(ln_mean.sem, 1)
                    ln_squared.wait(pe, i, n + 1)
                    for c in range(C):
                        m = mm(PS[:, 7, 0:T], ones256[:, :], csq[:, c, :], c == 0, c == C - 1)
                    m.then_inc(ln_var.sem, 1)
                    ln_done[n].wait(pe, i, 1)

                dots_ready.wait(pe, i, 1)
                mm(PS[:, 0, 0:10], ones[:, :], dots[:, :]).then_inc(logits_summed.sem, 1)
                wait_next(pe, n_rec, rec_ready)
                for r in range(8):
                    m = pe.transpose(PS[0:64, 1 + r // 4, (r % 4) * P:(r % 4 + 1) * P],
                                     rec[:, 168 + 64 * r:168 + 64 * (r + 1)], ident[:, :])
                m.then_inc(rec_turned.sem, 1)

                layernorm(0, h0)
                for n in range(12):
                    w, j = (wq0, n) if n < 8 else (wk0, n - 8)
                    if n >= 6:
                        qk0_copied.wait(pe, i, n - 5)
                    for c in range(C):
                        m = mm(PS[:, n % 6, 0:T], w[:, c, j * P:(j + 1) * P], xn[:, c, :], c == 0, c == C - 1)
                    m.then_inc(qk0_proj.sem, 1)
                for t, (t0, tn) in enumerate(TILES):
                    qk0_copied.wait(pe, i, 7 + t)
                    for c in range(C):
                        m = mm(PS[0:tn, t, 0:256], xn[:, c, t0:t0 + tn], wv0[:, c, :], c == 0, c == C - 1)
                    m.then_inc(v0_proj.sem, 1)
                qk0_squared.wait(pe, i, 12)
                for n in range(12):
                    first, last = n in (0, 8), n in (7, 11)
                    m = mm(PS[:, 6 + n // 8, 0:T], (ones1024 if n < 8 else ones512)[:, :], sq[:, n, :], first, last)
                m.then_inc(qk0_sums.sem, 1)
                qk0_bf16.wait(pe, i, 2)
                v0_ready.wait(pe, i, 3)
                for h in range(H):
                    half, j, g = slice(64 * (h % 2), 64 * (h % 2) + 64), h // 2, h // 4
                    if h >= 4:
                        rowmax0.wait(pe, i, h - 3)
                    for (t0, tn), (k0, kn), kc in zip(TILES, KR0, KC0):
                        m = mm(PS[0:tn, h % 4, kc:kc + kn], qkb[half, j, t0:t0 + tn],
                               qkb[half, 8 + g, k0:k0 + kn])
                    m.then_inc(rough0.sem, 1)
                rowmax0.wait(pe, i, H)
                for t, (t0, tn) in enumerate(TILES):
                    m = pe.transpose(PS[0:H, 6, t0:t0 + tn], mtok[0:tn, t, :], ident[0:tn, 0:tn])
                m.then_inc(max0_turned.sem, 1)
                shift0_ready.wait(pe, i, 1)

                def score0(h):
                    half, j, g = slice(64 * (h % 2), 64 * (h % 2) + 64), h // 2, h // 4
                    if h >= 3:
                        biased0.wait(pe, i, h - 2)
                    for t in range(3):
                        (q0, qn), c0 = QR0[t], QC0[t]
                        mm(PS[0:TT, h % 3, c0:c0 + qn], qk[half, 8 + g, t * TT:(t + 1) * TT],
                           qk[half, j, q0:q0 + qn], True, False)
                        m = mm(PS[0:TT, h % 3, c0:c0 + qn], pick[:, h, :], shift[:, q0:q0 + qn], False, True)
                    m.then_inc(scores0.sem, 1)

                score0(0)
                score0(1)
                for h in range(H):
                    probs0.wait(pe, i, h + 1)
                    if h >= 3:
                        y0_ready.wait(pe, i, h - 2)
                    lo = 64 if h % 2 == 0 else 0
                    for t in range(3):
                        (q0, qn), c0 = QR0[t], QC0[t]
                        m = mm(PS[:, 3 + h % 3, q0:q0 + qn], vx[:, t, h // 4, lo:lo + P],
                               pr0[:, h % 3, c0:c0 + qn], t == 0, t == 2, loose=True)
                    m.then_inc(pv0.sem, 1)
                    if h + 2 < H:
                        score0(h + 2)
                y0_ready.wait(pe, i, H)
                for c in range(C):
                    for j in range(8):
                        m = mm(PS[:, 6 + c, 0:T], wo0[:, j, c * P:(c + 1) * P], y0[:, j, :], j == 0, j == 7)
                m.then_inc(wo0_done.sem, 1)

                layernorm(1, h1)
                fq_ready.wait(pe, i, 1)
                for o in range(C):
                    for c in range(C):
                        m = mm(PS[:, o, 0:T], w8b[:, c, o * P:(o + 1) * P], fq[:, c, :], c == 0, c == C - 1)
                m.then_inc(ffn0_done.sem, 1)

                layernorm(2, h2)
                for n in range(4):
                    for c in range(C):
                        m = mm(PS[:, n, 0:T], wqk1[:, c, n * P:(n + 1) * P], xn[:, c, :], c == 0, c == C - 1)
                m.then_inc(qk1_proj.sem, 1)
                qk1_squared.wait(pe, i, 1)
                for n in range(4):
                    m = mm(PS[:, 4 + n, 0:T], block16[:, :], sq[:, n, :])
                m.then_inc(qk1_var.sem, 1)
                qk1_beta.wait(pe, i, 2)
                for n in range(4):
                    m = mm(PS[:, n, 0:T], rotate[:, :], u1[:, n, :])
                m.then_inc(qk1_turned.sem, 1)
                for t, (t0, tn) in enumerate(TILES):
                    for c in range(C):
                        m = mm(PS[0:tn, 4 + t, 0:256], xn[:, c, t0:t0 + tn], wv1[:, c, :], c == 0, c == C - 1)
                    m.then_inc(v1_proj.sem, 1)
                k1_ready.wait(pe, i, 5)
                v1_ready.wait(pe, i, 3)
                for h in range(H):
                    c, r, par = h // 8, 32 * (h % 8 // 2), h % 2
                    if h >= 2:
                        rowmax1.wait(pe, i, h - 1)
                    for t in range(3):
                        m = mm(PS[0:TT, 3 * (h % 2) + t, 0:T], q1b[r:r + 32, c, t * TT:(t + 1) * TT],
                               k1b[r:r + 32, par, c, :])
                    m.then_inc(rough1.sem, 1)
                rowmax1.wait(pe, i, H)
                for t, (t0, tn) in enumerate(TILES):
                    m = pe.transpose(PS[0:H, 6, t0:t0 + tn], mtok[0:tn, t, :], ident[0:tn, 0:tn])
                m.then_inc(max1_turned.sem, 1)
                shift1_ready.wait(pe, i, 1)

                def score1(h):
                    c, r, par = h // 8, 32 * (h % 8 // 2), h % 2
                    if h >= 2:
                        probs1.wait(pe, i, h - 1)
                    for t in range(3):
                        bank = 3 * (h % 2) + t
                        mm(PS[0:TT, bank, 0:T], k1[r:r + 32, par, c, t * TT:(t + 1) * TT],
                           qr[r:r + 32, c, :], True, False)
                        m = mm(PS[0:TT, bank, 0:T], pick[:, h, :], shift[:, :], False, True)
                    m.then_inc(scores1.sem, 1)

                def context1(g):
                    probs1.wait(pe, i, 4 * g + 4)
                    if g >= 2:
                        z_ready.wait(pe, i, g - 1)
                    for t, (_, tn) in enumerate(TILES):
                        for k in range(4):
                            h = 4 * g + k
                            m = mm(PS[32 * k:32 * k + 32, 6 + g % 2, 0:T], v1x[0:tn, t, h, :],
                                   pr1[0:tn, h % 8, t, :], t == 0, t == 2)
                    m.then_inc(pv1.sem, 1)

                for h in range(H):
                    score1(h)
                    if h % 4 == 1 and h > 4:
                        context1(h // 4 - 1)
                context1(3)
                z_ready.wait(pe, i, 4)
                for n in range(4):
                    m = mm(PS[:, n, 0:T], spread[:, :], zz[:, n, :])
                m.then_inc(sums_spread.sem, 1)
                y1_ready.wait(pe, i, 1)
                for c in range(C):
                    for n in range(4):
                        m = mm(PS[:, 4 + c, 0:T], wp1[:, n, c * P:(c + 1) * P], zz[:, n, :], n == 0, n == 3)
                m.then_inc(proj1_done.sem, 1)

                layernorm(3, h3)
                for t, (t0, tn) in enumerate(TILES):
                    for c in range(C):
                        m = mm(PS[0:tn, 0, t * NE:(t + 1) * NE], xn[:, c, t0:t0 + tn], wg[:, c, :],
                               c == 0, c == C - 1)
                m.then_inc(gates.sem, 1)
                for n in range(4):
                    for c in range(C):
                        m = mm(PS[:, 1 + n, 0:T], sw13[:, c, n * P:(n + 1) * P], xn[:, c, :], c == 0, c == C - 1)
                m.then_inc(up_done.sem, 1)
                hh_ready.wait(pe, i, 1)
                for t, (t0, tn) in enumerate(TILES):
                    o = PS[0:tn, 5 + t, 0:256]
                    mm(o, cen[:, 0, t0:t0 + tn], sw2[:, 0, :], True, False, loose=True)
                    mm(o, cen[:, 1, t0:t0 + tn], sw2[:, 1, :], False, False, loose=True)
                    for c in range(C):
                        m = mm(PS[0:tn, 5 + t, c * P:(c + 1) * P], h3[:, c, t0:t0 + tn], ident[:, :],
                               False, c == C - 1, loose=True)
                    m.then_inc(out_tok.sem, 1)
                gates_kept.wait(pe, i, 2)
                out_copied.wait(pe, i, 3)
                m = None
            pe.transpose(PS[0:64, 0, 0:P], ident[:, 0:64], ident[:, :]).then_inc(images_done, 1)

            pe.wait_ge(experts_loaded, 48)
            for s, w in enumerate((ew1, ew3)):
                for b in range(2):
                    for c in range(C):
                        m = mm(PS[0:8, 2 * s + b, 0:512], xn[:, c, 0:8], w[:, c, 512 * b:512 * (b + 1)],
                               c == 0, c == C - 1)
            m.then_inc(table_hidden.sem, 1)
            pe.wait_ge(counts_ready, 1)
            mm(PS[:, 4, 0:NE], ones[0:TT, :], cnt[0:TT, :]).then_inc(counts_summed, 1)
            pe.wait_ge(u64_loaded, 16)
            pe.wait_ge(hidden_copied, 2)
            n_onehots = pe.alloc_register("n_onehots")
            pe.reg_mov(n_onehots, 0)
            with pe.Fori(0, ROUNDS) as r:
                wait_next(pe, n_onehots, onehots_ready)
                for n in range(8):
                    m = pe.transpose(PS[0:64, 4 + n // 4, (n % 4) * TT:(n % 4 + 1) * TT], ohw[:, n, :],
                                     ident[0:TT, 0:TT])
                m.then_inc(onehots_turned.sem, 1)
                turned_copied.wait(pe, r, 1)
                for n in range(8):
                    m = mm(PS[0:TT, n // 2, 256 * (n % 2):256 * (n % 2) + 256], oht[:, n * TT:(n + 1) * TT],
                           u64[:, :])
                m.then_inc(routed_up.sem, 1)
                routed_h.wait(pe, r, 1)
                for n in range(8):
                    m = mm(PS[0:64, 6, 0:HID], oh[:, n, :], hs[:, n, :], n == 0, n == 7)
                m.then_inc(routed_added.sem, 1)
            pe.wait_ge(acc_copied, ROUNDS + 1)
            pe.transpose(PS[:, 4, 0:64], acct[:, :], ident[0:64, 0:64]).then_inc(acc_turned, 1)
            pe.wait_ge(accT_ready, 1)
            turned = accT[:, :].rearrange("p (e g) -> p g e", g=NE)
            for g in range(NE):
                m = mm(PS[0:8, 5, 0:256], turned[:, g, :], ew2[:, g, :], g == 0, g == NE - 1)
            m.then_inc(routed_out, 1)

        @block.scalar
        def _(act):
            A = nc.scalar.activation
            act.wait_ge(tables_loaded, 16 * len(loads))
            A(h0[:, :, 0:1], clst[:, :].rearrange("p (c a) -> p c a", a=1), ACT.Copy).then_inc(act_setup, 1)
            A(osb[0:1, 0, 0:4], ident[0:1, 0:4], ACT.Copy).then_inc(out_stored, 32)
            A(gb1[:, 0:1], gb1[:, 0:1], ACT.Copy, scale=0.25).then_inc(act_setup, 1)
            A(gb1[:, 2:3], gb1[:, 2:3], ACT.Copy, scale=0.25).then_inc(act_setup, 1)
            A(qkw0[:, 0:8], qkw0[:, 0:8], ACT.Copy, scale=0.125).then_inc(act_setup, 1)
            act.wait_ge(act_setup, SETUP_ACT)
            act.wait_ge(dve_setup, SETUP_DVE)

            with act.Fori(0, NB) as i:
                ch = Chain(act, act_chain, ACT_STEPS, i)

                def layernorm(n):
                    ln_centred.wait(act, i, n + 1)
                    A(csq[:, :, :], cen[:, :, :], ACT.Square).then_inc(ln_squared.sem, 1)
                    ln_var.wait(act, i, n + 1)
                    ch.step(A(rs[:, 0, :], PS[:, 7, 0:T], ACT.Ln, bias=eps[:, 0:1]))
                    A(rs[:, 0, :], rs[:, 0, :], ACT.Exp, scale=-0.5).then_inc(ln_guess.sem, 1)

                logits_shifted.wait(act, i, 1)
                A(e10[:, :], z10[:, :], ACT.Exp).then_inc(weights_exp.sem, 1)
                layernorm(0)
                for n in range(12):
                    qk0_copied.wait(act, i, n + 1)
                    A(sq[:, n, :], qk[:, n, 0:T], ACT.Square).then_inc(qk0_squared.sem, 1)
                for t, (_, tn) in enumerate(TILES):
                    v0_proj.wait(act, i, t + 1)
                    A(vx[0:tn, t, :, 64:128], PS[0:tn, t, 0:256].rearrange("p (g d) -> p g d", g=KV), ACT.Copy)\
                        .then_inc(v0_ready.sem, 1)
                qk0_sums.wait(act, i, 1)
                ch.step(A(rs[:, 0:2, :], PS[:, 6:8, 0:T], ACT.Ln, bias=eps[:, 1:2]))
                A(rs[:, 0:2, :], rs[:, 0:2, :], ACT.Exp, scale=-0.5).then_inc(qk0_guess.sem, 1)
                qk0_ready.wait(act, i, 8)
                A(qkb[:, 0:8, :], qk[:, 0:8, 0:T], ACT.Copy).then_inc(qk0_bf16.sem, 1)
                qk0_ready.wait(act, i, 12)
                A(qkb[:, 8:12, :], qk[:, 8:12, 0:T], ACT.Copy).then_inc(qk0_bf16.sem, 1)
                max0_turned.wait(act, i, 1)
                A(shift[0:H, :], PS[0:H, 6, 0:T], ACT.Copy, scale=-1.0).then_inc(shift0_ready.sem, 1)
                for h in range(H):
                    biased0.wait(act, i, h + 1)
                    if h >= 3:
                        pv0.wait(act, i, h - 2)
                    A(pr0[:, h % 3, :], pre[:, h % 2, :], ACT.Exp).then_inc(probs0.sem, 1)

                layernorm(1)
                layernorm(2)
                qk1_proj.wait(act, i, 1)
                A(sq[:, 0:4, :], PS[:, 0:4, 0:T], ACT.Square).then_inc(qk1_squared.sem, 1)
                qk1_var.wait(act, i, 1)
                ch.step(A(rs[:, :, :], PS[:, 4:8, 0:T], ACT.Ln, bias=eps[:, 1:2]))
                A(rs[:, :, :], rs[:, :, :], ACT.Exp, scale=-0.5).then_inc(qk1_guess.sem, 1)
                qk1_normed.wait(act, i, 1)
                for n in range(2):
                    A(u1[:, 2 * n:2 * n + 2, :], u1[:, 2 * n:2 * n + 2, :], ACT.Identity,
                      bias=gb1[:, 2 + n:3 + n]).then_inc(qk1_beta.sem, 1)
                for t, (_, tn) in enumerate(TILES):
                    v1_proj.wait(act, i, t + 1)
                    A(v1x[0:tn, t, :, 0:16], PS[0:tn, 4 + t, 0:256].rearrange("p (h d) -> p h d", h=H), ACT.Copy)\
                        .then_inc(v1_ready.sem, 1)
                rope_done.wait(act, i, 1)
                A(q1b[:, :, 0:T], qr[:, 0:2, :], ACT.Copy).then_inc(k1_ready.sem, 1)
                for par in range(2):
                    A(k1b[:, par, :, :], qr[:, 2:4, :], ACT.Copy, scale=parity[:, par:par + 1])\
                        .then_inc(k1_ready.sem, 1)
                    A(k1[:, par, :, 0:T], qr[:, 2:4, :], ACT.Copy, scale=parity[:, par:par + 1])\
                        .then_inc(k1_ready.sem, 1)
                max1_turned.wait(act, i, 1)
                A(shift[0:H, :], PS[0:H, 6, 0:T], ACT.Copy, scale=-1.0).then_inc(shift1_ready.sem, 1)
                for h in range(H):
                    scores1.wait(act, i, h + 1)
                    if h >= 8:
                        pv1.wait(act, i, h // 4 - 1)
                    A(pr1[0:TT, h % 8, :, :], PS[0:TT, 3 * (h % 2):3 * (h % 2) + 3, 0:T], ACT.Exp)\
                        .then_inc(probs1.sem, 1)
                    if h % 4 == 2 and h > 4:
                        g = h // 4 - 1
                        pv1.wait(act, i, g + 1)
                        A(zz[:, g, :], PS[:, 6 + g % 2, 0:T], ACT.Copy).then_inc(z_ready.sem, 1)
                pv1.wait(act, i, 4)
                A(zz[:, 3, :], PS[:, 7, 0:T], ACT.Copy).then_inc(z_ready.sem, 1)

                layernorm(3)
                up_done.wait(act, i, 1)
                A(csq[:, :, :], PS[:, 1:3, 0:T], ACT.Exp, scale=-1.0).then_inc(silu_exp.sem, 1)
                act.wait_ge(out_stored, i * 32 + 32)
                for t, (_, tn) in enumerate(TILES):
                    out_tok.wait(act, i, t + 1)
                    A(osb[0:tn, t, :], PS[0:tn, 5 + t, 0:256], ACT.Copy).then_inc(out_copied.sem, 1)
                out_copied.wait(act, i, 3)
                o = out[bass.ds(i, 1), :, :]
                act.dma_start(o[:, 0:2 * TT, :].rearrange("a (t p) d -> p (a t) d", p=TT), osb[:, 0:2, :])\
                    .then_inc(out_stored, 16)
                act.dma_start(o[:, 2 * TT:T, :].rearrange("a p d -> p (a d)"), osb[0:85, 2, :])\
                    .then_inc(out_stored, 16)
                ch.end()

            table_hidden.wait(act, 0, 1)
            for s in range(2):
                A(u8sb[:, :, s, :], PS[0:8, 2 * s:2 * s + 2, :].rearrange("p b (g n) -> p (b g) n", n=HID),
                  ACT.Copy).then_inc(hidden_copied, 1)
            logits_shifted.wait(act, NB, 1)
            A(prob[:, :, :], rt[:, :, :], ACT.Exp).then_inc(weights_exp.sem, 1)
            with act.Fori(0, ROUNDS) as r:
                routed_up.wait(act, r, 1)
                A(he[:, :, :], PS[0:TT, 0:4, :].rearrange("p b (n s d) -> p (b n) s d", n=2, s=2)[:, :, 0, :],
                  ACT.Exp, scale=-1.0).then_inc(routed_exp.sem, 1)

        @block.vector
        def _(dve):
            V = nc.vector
            n_setup = [0]

            def setup(ins):
                n_setup[0] += 1
                ins.then_inc(dve_setup, 1)

            def settled():
                dve.wait_ge(dve_setup, n_setup[0])

            V.memset(img[:, :], 0.0).then_inc(image_read.sem, 1)
            setup(V.memset(ones[:, :], 1.0))
            setup(V.memset(ones256[:, :], 1.0 / 256))
            setup(V.memset(ones1024[:, :], 1.0 / 1024))
            setup(V.memset(ones512[:, :], 1.0 / 512))
            setup(V.memset(eps[:, 0:1], 1e-5))
            setup(V.memset(eps[:, 1:2], 1e-6))
            setup(V.memset(vx[:, :, :, :], 0.0))
            setup(V.memset(v1x[:, :, :, :], 1.0))
            setup(V.memset(shift[:, :], 0.0))
            setup(V.memset(qk[:, :, T:TP], 0.0))
            setup(V.memset(k1[:, :, :, T:TP], 0.0))
            setup(V.memset(q1b[:, :, T:TP], 0.0))
            setup(V.memset(lg[:, :, :], 0.0))
            settled()
            setup(V.memset(vx[:, :, :, 0:64], 1.0))
            setup(V.memset(vx[:, :, :, 128:192], 1.0))
            dve.wait_ge(tables_loaded, 16 * len(loads))
            w8x = [sq[:, 2 * n:2 * n + 2, 0:256] for n in range(4)]
            w8i, w8m, w8f, w8g = w8x[0].bitcast(I32), w8x[1].bitcast(I32), w8x[2], w8x[3]
            for h in range(H):
                setup(V.tensor_scalar(biasq[0:TT, h, :], relq, SLOPES[h], None, ALU.mult))
            setup(V.tensor_copy(pick[:, :, :], ident[:, 0:H].unsqueeze(2).broadcast_to([P, H, TT])))
            setup(V.tensor_copy(w8i[:, :, :], w8[:, :, :]))
            settled()
            setup(V.tensor_scalar(w8m[:, :, :], w8i[:, :, :], 127, None, ALU.bitwise_and))
            settled()
            setup(V.tensor_scalar(w8i[:, :, :], w8i[:, :, :], 128, 24, ALU.bitwise_and, ALU.logical_shift_left))
            setup(V.tensor_copy(w8f[:, :, :], w8m[:, :, :]))
            settled()
            setup(V.tensor_scalar(w8m[:, :, :], w8m[:, :, :], 20, None, ALU.logical_shift_left))
            setup(V.tensor_scalar(w8f[:, :, :], w8f[:, :, :], 8.0, 2.0 ** -9, ALU.min, ALU.mult))
            settled()
            setup(V.tensor_scalar(w8g[:, :, :], w8m[:, :, :].bitcast(F32), 2.0 ** 120, None, ALU.mult))
            settled()
            setup(V.tensor_tensor(w8f[:, :, :], w8f[:, :, :], w8g[:, :, :], op=ALU.max))
            settled()
            setup(V.tensor_tensor(w8m[:, :, :], w8f[:, :, :].bitcast(I32), w8i[:, :, :], op=ALU.bitwise_or))
            settled()
            setup(V.tensor_copy(w8b[:, :, :], w8m[:, :, :].bitcast(F32)))
            wh = wqk1[:, :, :].rearrange("p c (h d) -> p c h d", d=16)
            setup(V.tensor_reduce(wmean[:, :, :], wh, axis=AX_X, op=ALU.add))
            settled()
            setup(V.tensor_scalar(wmean[:, :, :], wmean[:, :, :], 1.0 / 16, None, ALU.mult))
            settled()
            for c in range(C):
                setup(V.tensor_tensor(wh[:, c], wh[:, c],
                                      wmean[:, c, :].unsqueeze(2).broadcast_to([P, 32, 16]), op=ALU.subtract))
            assert n_setup[0] == SETUP_DVE, n_setup
            settled()
            dve.wait_ge(act_setup, SETUP_ACT)

            def over(row, n):
                return row.unsqueeze(1).broadcast_to([P, n, T])

            n_rough = dve.alloc_register("n_rough")
            dve.reg_mov(n_rough, 0)
            with dve.Fori(0, NB) as i:
                ch = Chain(dve, dve_chain, DVE_STEPS, i)

                def newton(n, sums, which, last):
                    ch.step(V.scalar_tensor_tensor(nt[:, 0:n, :], sums, eps[:, which:which + 1], rs[:, 0:n, :],
                                                   ALU.add, ALU.mult))
                    ch.step(V.scalar_tensor_tensor(nt[:, 0:n, :], nt[:, 0:n, :], -0.5, rs[:, 0:n, :],
                                                   ALU.mult, ALU.mult))
                    ch.step(V.scalar_tensor_tensor(rs[:, 0:n, :], nt[:, 0:n, :], 1.5, rs[:, 0:n, :],
                                                   ALU.add, ALU.mult))

                def layernorm(n, src, done):
                    ln_mean.wait(dve, i, n + 1)
                    V.tensor_tensor(cen[:, :, :], src[:, :, :], over(PS[:, 6, 0:T], C), op=ALU.subtract)\
                        .then_inc(ln_centred.sem, 1)
                    ln_guess.wait(dve, i, n + 1)
                    newton(1, PS[:, 7:8, 0:T], 0, None)
                    V.tensor_tensor(xn[:, :, :], cen[:, :, :], over(rs[:, 0, :], C), op=ALU.mult)\
                        .then_inc(done.sem, 1)

                dve.wait_ge(image_loaded, i * 16 + 16)
                x0 = img[:, :]
                rows = 8
                for lev in range(3):
                    n = [128, 32, 8][lev]
                    half = rows // 2
                    v = x0.rearrange("p (n e) -> p n e", e=2)
                    lo, hi = lohi[:, 0, 0:2 * n], lohi[:, 1, 0:2 * n]
                    ch.mark(V.tensor_tensor(lo, v[:, :, 0], v[:, :, 1], op=ALU.add))
                    sub = V.tensor_tensor(hi, v[:, :, 0], v[:, :, 1], op=ALU.subtract)
                    if lev == 0:
                        sub.then_inc(image_read.sem, 1)
                        ch.sync()
                        image_read.wait(dve, i, 2)
                    else:
                        ch.step(sub)
                    c0 = [0, 384, 480][lev]
                    a0 = [0, 128, 160][lev]
                    lo = lo.rearrange("p (r e n) -> p r e n", r=half, e=2)
                    hi = hi.rearrange("p (r e n) -> p r e n", r=half, e=2)

                    def sub_of(t, at):
                        return t[:, at:at + n].rearrange("p (r n) -> p r n", r=half)

                    ch.mark(V.tensor_tensor(sub_of(avg, a0), lo[:, :, 0], lo[:, :, 1], op=ALU.add))
                    ch.mark(V.tensor_tensor(sub_of(coef, c0), lo[:, :, 0], lo[:, :, 1], op=ALU.subtract))
                    ch.mark(V.tensor_tensor(sub_of(coef, c0 + n), hi[:, :, 0], hi[:, :, 1], op=ALU.add))
                    ch.step(V.tensor_tensor(sub_of(coef, c0 + 2 * n), hi[:, :, 0], hi[:, :, 1], op=ALU.subtract))
                    x0 = avg[:, a0:a0 + n]
                    rows = half
                for k, (c0, n) in enumerate([(480, 24), (384, 96), (0, 384)]):
                    for o in range(3):
                        ch.step(V.tensor_tensor_reduce(
                            out=dotx[:, 0:n], in0=coef[:, c0:c0 + n], in1=wdet[:, o, c0:c0 + n], scale=1.0,
                            scalar=0.0, op0=ALU.mult, op1=ALU.add, accum_out=dots[:, 3 * k + o:3 * k + o + 1]))
                V.tensor_tensor_reduce(out=dotx[:, 0:8], in0=avg[:, 160:168], in1=wdet[:, 0, 504:512], scale=1.0,
                                       scalar=0.0, op0=ALU.mult, op1=ALU.add, accum_out=dots[:, 9:10])\
                    .then_inc(dots_ready.sem, 1)
                logits_summed.wait(dve, i, 1)
                ch.step(V.tensor_tensor(z10[:, :], PS[:, 0, 0:10], dscale[:, :], op=ALU.mult))
                ch.step(V.tensor_tensor(z10[:, :], z10[:, :], dbias[:, :], op=ALU.add))
                z9 = z10[:, 0:9].rearrange("p (l o) -> p l o", o=3)
                ch.mark(V.tensor_reduce(mx3[:, :], z9, axis=AX_X, op=ALU.max))
                ch.step(V.tensor_scalar(z10[:, 9:10], z10[:, 9:10], -1.0, None, ALU.mult))
                V.tensor_tensor(z9, z9, mx3[:, :].unsqueeze(2).broadcast_to([P, 3, 3]), op=ALU.subtract)\
                    .then_inc(logits_shifted.sem, 1)
                weights_exp.wait(dve, i, 1)
                e9 = e10[:, 0:9].rearrange("p (l o) -> p l o", o=3)
                ch.mark(V.tensor_reduce(s4[:, 0:3], e9, axis=AX_X, op=ALU.add))
                ch.step(V.tensor_scalar(s4[:, 3:4], e10[:, 9:10], 1.0, None, ALU.add))
                ch.step(V.reciprocal(s4[:, :], s4[:, :]))
                ch.mark(V.tensor_copy(e10[:, 9:10], s4[:, 3:4]))
                ch.step(V.tensor_tensor(e9, e9, s4[:, 0:3].unsqueeze(2).broadcast_to([P, 3, 3]), op=ALU.mult))
                ch.step(V.tensor_tensor(w10[:, 0, :], e10[:, :], wscale[:, :], op=ALU.mult))
                ch.step(V.tensor_scalar(w10[:, 1, :], w10[:, 0, :], -1.0, None, ALU.mult))
                ch.step(V.tensor_scalar(rec[:, 0:8], avg[:, 160:168], w10[:, 0, 9:10], None, ALU.mult))
                for k, (c0, n, rows, at) in enumerate([(480, 8, 1, 0), (384, 32, 2, 8), (0, 128, 4, 40)]):
                    cur = rec[:, at:at + n].rearrange("p (r n) -> p r n", r=rows)

                    def band(s):
                        return coef[:, c0 + s * n:c0 + (s + 1) * n].rearrange("p (r n) -> p r n", r=rows)

                    lo = syn[:, 0, 0:2 * n].rearrange("p (r e n) -> p r e n", r=rows, e=2)
                    hi = syn[:, 1, 0:2 * n].rearrange("p (r e n) -> p r e n", r=rows, e=2)
                    tv = syn[:, 2, 0:n].rearrange("p (r n) -> p r n", r=rows)
                    ch.mark(V.tensor_scalar(tv, band(1), w10[:, 0, 3 * k + 1:3 * k + 2], None, ALU.mult))
                    for s in range(2):
                        ch.mark(V.scalar_tensor_tensor(lo[:, :, s], band(0), w10[:, s, 3 * k:3 * k + 1], cur,
                                                       ALU.mult, ALU.add))
                    ch.sync()
                    for s in range(2):
                        ch.mark(V.scalar_tensor_tensor(hi[:, :, s], band(2), w10[:, s, 3 * k + 2:3 * k + 3], tv,
                                                       ALU.mult, ALU.add))
                    ch.sync()
                    o = rec[:, at + n:at + 5 * n].rearrange("p (n e) -> p n e", e=2)
                    ch.mark(V.tensor_tensor(o[:, :, 0], syn[:, 0, 0:2 * n], syn[:, 1, 0:2 * n], op=ALU.add))
                    odd = V.tensor_tensor(o[:, :, 1], syn[:, 0, 0:2 * n], syn[:, 1, 0:2 * n], op=ALU.subtract)
                    if k < 2:
                        ch.step(odd)
                    else:
                        odd.then_inc(rec_ready.sem, 1)
                rec_turned.wait(dve, i, 1)
                for cg in range(4):
                    src = PS[0:64, 1:3, :].rearrange("p b (r q n) -> p b r q n", r=4, q=4)[:, :, :, cg, :]
                    dst = h0[64 * (cg % 2):64 * (cg % 2) + 64, cg // 2, 1:T]\
                        .rearrange("p (n b r) -> p b r n", b=2, r=4)
                    cp = V.tensor_copy(dst, src)
                    if cg < 3:
                        ch.mark(cp)
                    else:
                        cp.then_inc(h_ready.sem, 1)

                layernorm(0, h0, ln_done[0])
                for n in range(12):
                    qk0_proj.wait(dve, i, n + 1)
                    V.tensor_copy(qk[:, n, 0:T], PS[:, n % 6, 0:T]).then_inc(qk0_copied.sem, 1)
                qk0_guess.wait(dve, i, 1)
                newton(2, PS[:, 6:8, 0:T], 1, None)
                qk0_squared.wait(dve, i, 12)
                for n in range(12):
                    V.scalar_tensor_tensor(qk[:, n, 0:T], qk[:, n, 0:T], qkw0[:, n:n + 1], rs[:, n // 8, :],
                                           ALU.mult, ALU.mult).then_inc(qk0_ready.sem, 1)
                for h in range(H):
                    wait_next(dve, n_rough, rough0)
                    for t, ((_, tn), (_, kn), kc) in enumerate(zip(TILES, KR0, KC0)):
                        o = PS[0:tn, h % 4, kc:kc + kn]
                        m = V.tensor_tensor_reduce(out=o, in0=o, in1=biasq[0:tn, h, kc:kc + kn], scale=1.0,
                                                   scalar=-3e38, op0=ALU.add, op1=ALU.max,
                                                   accum_out=mtok[0:tn, t, h:h + 1])
                    m.then_inc(rowmax0.sem, 1)

                def normalise0(h):
                    pv0.wait(dve, i, h + 1)
                    v0, s0 = (0, 64) if h % 2 == 0 else (64, 0)
                    b = 3 + h % 3
                    ch.step(V.reciprocal(rr[v0:v0 + 64, :], PS[s0:s0 + 64, b, 0:T]))
                    V.tensor_tensor(y0[v0:v0 + 64, h // 2, :], PS[v0:v0 + 64, b, 0:T], rr[v0:v0 + 64, :],
                                    op=ALU.mult).then_inc(y0_ready.sem, 1)

                for h in range(H):
                    scores0.wait(dve, i, h + 1)
                    if h >= 2:
                        probs0.wait(dve, i, h - 1)
                    V.scalar_tensor_tensor(pre[:, h % 2, :], relm[:, :], SLOPES[h], PS[0:TT, h % 3, 0:W0],
                                           ALU.mult, ALU.add).then_inc(biased0.sem, 1)
                    if h >= 2:
                        normalise0(h - 2)
                normalise0(H - 2)
                normalise0(H - 1)
                wo0_done.wait(dve, i, 1)
                V.tensor_tensor(h1[:, :, :], h0[:, :, :], PS[:, 6:8, 0:T], op=ALU.add).then_inc(h_ready.sem, 1)

                layernorm(1, h1, ln_done[1])
                absmax_done.wait(dve, i, 1)
                ch.step(V.tensor_tensor(fs[:, 0, :], amax[:, 0, :], amax[:, 1, :], op=ALU.max))
                ch.step(V.tensor_scalar(fs[:, 1, :], fs[:, 0, :], 1e-12, 1.0 / 448.0, ALU.max, ALU.mult))
                ch.mark(V.tensor_scalar(fs[:, 3, :], fs[:, 1, :], w8s[:, 0:1], None, ALU.mult))
                ch.step(V.reciprocal(fs[:, 2, :], fs[:, 1, :]))
                ch.step(V.tensor_tensor(fy[:, :, :], xn[:, :, :], over(fs[:, 2, :], C), op=ALU.mult))
                ch.step(V.tensor_scalar(fm[:, :, :].bitcast(I32), fy[:, :, :].bitcast(I32), 0x7F800000, None,
                                        ALU.bitwise_and))
                ch.step(V.tensor_scalar(fm[:, :, :], fm[:, :, :], 2.0 ** -6, 1.5 * 2.0 ** 20, ALU.max, ALU.mult))
                ch.step(V.tensor_tensor(fy[:, :, :], fy[:, :, :], fm[:, :, :], op=ALU.add))
                V.tensor_tensor(fq[:, :, :], fy[:, :, :], fm[:, :, :], op=ALU.subtract).then_inc(fq_ready.sem, 1)
                ffn0_done.wait(dve, i, 1)
                ch.step(V.tensor_tensor(fy[:, :, :], PS[:, 0:2, 0:T], over(fs[:, 3, :], C), op=ALU.mult))
                ch.mark(V.scalar_tensor_tensor(h2[:, 0, :], fy[:, 0, :], b8[:, 0:1], h1[:, 0, :], ALU.add, ALU.add))
                V.scalar_tensor_tensor(h2[:, 1, :], fy[:, 1, :], b8[:, 1:2], h1[:, 1, :], ALU.add, ALU.add)\
                    .then_inc(h_ready.sem, 1)

                layernorm(2, h2, ln_done[2])
                qk1_squared.wait(dve, i, 1)
                for n in range(2):
                    ch.mark(V.tensor_scalar(u1[:, 2 * n:2 * n + 2, :], PS[:, 2 * n:2 * n + 2, 0:T],
                                            gb1[:, n:n + 1], None, ALU.mult))
                qk1_guess.wait(dve, i, 1)
                newton(4, PS[:, 4:8, 0:T], 1, None)
                V.tensor_tensor(u1[:, :, :], u1[:, :, :], rs[:, :, :], op=ALU.mult).then_inc(qk1_normed.sem, 1)
                qk1_beta.wait(dve, i, 2)
                ch.mark(V.tensor_tensor(qr[:, :, :], u1[:, :, :], over(cosT[:, :], 4), op=ALU.mult))
                qk1_turned.wait(dve, i, 1)
                ch.step(V.tensor_tensor(nt[:, :, :], PS[:, 0:4, 0:T], over(sinT[:, :], 4), op=ALU.mult))
                V.tensor_tensor(qr[:, :, :], qr[:, :, :], nt[:, :, :], op=ALU.add).then_inc(rope_done.sem, 1)
                for h in range(H):
                    rough1.wait(dve, i, h + 1)
                    V.tensor_reduce(mtok[:, :, h:h + 1], PS[0:TT, 3 * (h % 2):3 * (h % 2) + 3, 0:T], axis=AX_X,
                                    op=ALU.max).then_inc(rowmax1.sem, 1)
                sums_spread.wait(dve, i, 1)
                ch.step(V.reciprocal(nt[:, :, :], PS[:, 0:4, 0:T]))
                V.tensor_tensor(zz[:, :, :], zz[:, :, :], nt[:, :, :], op=ALU.mult).then_inc(y1_ready.sem, 1)
                proj1_done.wait(dve, i, 1)
                V.tensor_tensor(h3[:, :, :], h2[:, :, :], PS[:, 4:6, 0:T], op=ALU.add).then_inc(h_ready.sem, 1)

                layernorm(3, h3, ln_done[3])
                gates.wait(dve, i, 1)
                V.tensor_copy(lg[:, bass.ds(i * 3, 2), :], PS[0:TT, 0, 0:2 * NE].rearrange("p (t e) -> p t e", e=NE))\
                    .then_inc(gates_kept.sem, 1)
                V.tensor_copy(lg[0:85, bass.ds(i * 3 + 2, 1), :],
                              PS[0:85, 0, 2 * NE:3 * NE].rearrange("p (t e) -> p t e", e=NE))\
                    .then_inc(gates_kept.sem, 1)
                silu_exp.wait(dve, i, 1)
                ch.step(V.tensor_scalar(csq[:, :, :], csq[:, :, :], 1.0, None, ALU.add))
                ch.step(V.reciprocal(csq[:, :, :], csq[:, :, :]))
                ch.step(V.tensor_tensor(csq[:, :, :], PS[:, 1:3, 0:T], csq[:, :, :], op=ALU.mult))
                V.tensor_tensor(cen[:, :, :], PS[:, 3:5, 0:T], csq[:, :, :], op=ALU.mult).then_inc(hh_ready.sem, 1)
                ch.end()

            steps = [0]

            def mark(ins):
                steps[0] += 1
                ins.then_inc(tail_chain, 1)

            def step(ins):
                mark(ins)
                dve.wait_ge(tail_chain, steps[0])

            def per_expert(x):
                return x.unsqueeze(2).broadcast_to([TT, NCOL, NE])

            gates_kept.wait(dve, NB - 1, 2)
            step(V.tensor_reduce(r1[:, :], lg[:, :, :], axis=AX_X, op=ALU.max))
            V.tensor_tensor(rt[:, :, :], lg[:, :, :], per_expert(r1[:, :]), op=ALU.subtract)\
                .then_inc(logits_shifted.sem, 1)
            weights_exp.wait(dve, NB, 1)
            step(V.tensor_reduce(r1[:, :], prob[:, :, :], axis=AX_X, op=ALU.add))
            step(V.reciprocal(r1[:, :], r1[:, :]))
            step(V.tensor_tensor(prob[:, :, :], prob[:, :, :], per_expert(r1[:, :]), op=ALU.mult))
            step(V.tensor_tensor(rt[:, :, :], prob[:, :, :], ebias[0:TT, :].unsqueeze(1)
                                 .broadcast_to([TT, NCOL, NE]), op=ALU.add))
            s2 = rt[:, :, :].rearrange("p n (g e) -> p n g e", e=2)
            gs, beat, tmp = g4[:, 0], g4[:, 1], g4[:, 2]
            step(V.tensor_tensor(gs, s2[:, :, :, 0], s2[:, :, :, 1], op=ALU.add))
            step(V.memset(beat, 0.0))

            def rank(score, count, scratch, width):
                for k in range(width):
                    for lo, hi, op in ((0, k, ALU.is_gt), (k + 1, width, ALU.is_ge)):
                        if lo < hi:
                            rival = score[:, :, k:k + 1].broadcast_to([TT, NCOL, hi - lo])
                            step(V.tensor_tensor(scratch[:, :, lo:hi], rival, score[:, :, lo:hi], op=op))
                            step(V.tensor_tensor(count[:, :, lo:hi], count[:, :, lo:hi], scratch[:, :, lo:hi],
                                                 op=ALU.add))

            rank(gs, beat, tmp, 4)
            step(V.tensor_scalar(tmp, beat, 1.5, None, ALU.is_lt))
            step(V.tensor_scalar(beat, tmp, -MASKED, MASKED, ALU.mult, ALU.add))
            for e in range(2):
                step(V.tensor_tensor(s2[:, :, :, e], s2[:, :, :, e], tmp, op=ALU.mult))
                step(V.tensor_tensor(s2[:, :, :, e], s2[:, :, :, e], beat, op=ALU.add))
            step(V.memset(rk[:, :, :], 0.0))
            scratch = ge[:, 0:NCOL, :]
            rank(rt, rk, scratch, NE)
            for s in range(2):
                step(V.tensor_scalar(onehot[:, :, s, :], rk[:, :, :], float(s), None, ALU.is_equal))
                step(V.tensor_tensor(scratch, onehot[:, :, s, :], prob[:, :, :], op=ALU.mult))
                step(V.tensor_reduce(weight[:, :, s:s + 1], scratch, axis=AX_X, op=ALU.add))
                step(V.tensor_tensor(onehot[:, :, s, :], onehot[:, :, s, :], per_expert(valid[:, :]), op=ALU.mult))
            step(V.tensor_tensor(scratch, onehot[:, :, 0, :], onehot[:, :, 1, :], op=ALU.add))
            V.tensor_reduce(cnt[0:TT, :], scratch.rearrange("p n e -> p e n"), axis=AX_X, op=ALU.add)\
                .then_inc(counts_ready, 1)
            dve.wait_ge(counts_summed, 1)
            step(V.tensor_copy(offs[:, :], PS[0:TT, 4, 0:NE]))
            for e in range(1, NE):
                step(V.tensor_tensor(offs[:, e:e + 1], offs[:, e:e + 1], offs[:, e - 1:e], op=ALU.add))
            flat = pos[:, :, :].rearrange("p n s -> p (n s)").unsqueeze(2).broadcast_to([TT, NCOL * 2, NE])
            step(V.tensor_tensor(ge[:, :, :], flat, offs[:, :].unsqueeze(1).broadcast_to([TT, NCOL * 2, NE]),
                                 op=ALU.is_lt))
            gr = group[:, :, :, :].rearrange("p n s g -> p (n s) g")
            step(V.tensor_copy(gr[:, :, 0:1], ge[:, :, 0:1]))
            step(V.tensor_tensor(gr[:, :, 1:NE], ge[:, :, 1:NE], ge[:, :, 0:NE - 1], op=ALU.subtract))

            V.memset(acct[:, :], 0.0).then_inc(acc_copied, 1)

            n_steps = steps[0]
            ONES = onehot[:, :, :, :].rearrange("p n s e -> p (n s) e")
            WGT = weight[:, :, :].rearrange("p n s -> p (n s)")
            with dve.Fori(0, ROUNDS) as r:
                tail = n_steps
                o4 = oh[:, :, :].rearrange("p n (e g) -> p n e g", g=NE)
                at = bass.ds(r * 8, 8)
                V.tensor_tensor(o4, ONES[:, at, :].unsqueeze(3).broadcast_to([TT, 8, NE, NE]),
                                gr[:, at, :].unsqueeze(2).broadcast_to([TT, 8, NE, NE]), op=ALU.mult)\
                    .then_inc(tail_chain, 1)
                dve.wait_ge(tail_chain, r * 4 + (tail + 1))
                V.tensor_tensor(ohw[:, :, :], oh[:, :, :], WGT[:, at].unsqueeze(2).broadcast_to([TT, 8, 64]),
                                op=ALU.mult).then_inc(onehots_ready.sem, 1)
                onehots_turned.wait(dve, r, 1)
                V.tensor_copy(oht[:, :].rearrange("p (b n) -> p b n", b=2), PS[0:64, 4:6, 0:4 * TT])\
                    .then_inc(turned_copied.sem, 1)
                routed_exp.wait(dve, r, 1)
                V.tensor_scalar(he[:, :, :], he[:, :, :], 1.0, None, ALU.add).then_inc(tail_chain, 1)
                dve.wait_ge(tail_chain, r * 4 + (tail + 2))
                V.reciprocal(he[:, :, :], he[:, :, :]).then_inc(tail_chain, 1)
                dve.wait_ge(tail_chain, r * 4 + (tail + 3))
                up = PS[0:TT, 0:4, :].rearrange("p b (n s d) -> p (b n) s d", n=2, s=2)
                V.tensor_tensor(he[:, :, :], up[:, :, 0, :], he[:, :, :], op=ALU.mult).then_inc(tail_chain, 1)
                dve.wait_ge(tail_chain, r * 4 + (tail + 4))
                V.tensor_tensor(hs[:, :, :], up[:, :, 1, :], he[:, :, :], op=ALU.mult).then_inc(routed_h.sem, 1)
                routed_added.wait(dve, r, 1)
                dve.wait_ge(acc_copied, r + 1)
                V.tensor_tensor(acct[:, :], acct[:, :], PS[0:64, 6, 0:HID], op=ALU.add).then_inc(acc_copied, 1)
            dve.wait_ge(acc_turned, 1)
            V.tensor_copy(accT[:, :], PS[:, 4, 0:64]).then_inc(accT_ready, 1)
            dve.wait_ge(routed_out, 1)
            dve.wait_ge(rows_loaded, 16)
            V.tensor_tensor(r8, r8, PS[0:8, 5, 0:256], op=ALU.add).then_inc(rows_ready, 1)


def tables():
    k = np.arange(P)
    t = {"ident": np.eye(P, dtype=np.float32)}
    t["block16"] = (k[:, None] // 16 == k[None, :] // 16).astype(np.float32) / 16
    rot = np.zeros((P, P), np.float32)
    for m in range(P):
        if m % 16 < 8:
            rot[m + 8, m] = -1.0
        else:
            rot[m - 8, m] = 1.0
    t["rotate"] = rot
    t["spread"] = (k[:, None] == 32 * (k[None, :] // 32) + 16).astype(np.float32)
    freq = np.float32(1.0) / np.float32(10000.0) ** (np.arange(8, dtype=np.float32) / np.float32(8))
    ang = (np.arange(T, dtype=np.float32)[None, :] * freq[k % 8][:, None]).astype(np.float32)
    t["cosT"], t["sinT"] = np.cos(ang).astype(np.float32), np.sin(ang).astype(np.float32)
    t["parity"] = np.stack([(k // 16) % 2 == 0, (k // 16) % 2 == 1], 1).astype(np.float32)
    relm = np.full((TT, W0), MASKED, np.float32)
    for n, ((q0, qn), c0) in enumerate(zip(QR0, QC0)):
        key, q = n * TT + np.arange(TT)[:, None], q0 + np.arange(qn)[None, :]
        ok = (key <= q) & (key >= q - WINDOW) & (key < T)
        relm[:, c0:c0 + qn] = np.where(ok, (key - q).astype(np.float32), MASKED)
    t["relm"] = relm
    relq = np.full((TT, W2), MASKED, np.float32)
    for n, ((k0, kn), c0) in enumerate(zip(KR0, KC0)):
        q, key = n * TT + np.arange(TT)[:, None], k0 + np.arange(kn)[None, :]
        ok = (key <= q) & (key >= q - WINDOW)
        relq[:, c0:c0 + kn] = np.where(ok, (key - q).astype(np.float32), MASKED)
    t["relq"] = relq
    p, col = np.arange(TT)[:, None], np.arange(NCOL)[None, :]
    token = (NB - 1 - col // 3) * T + (col % 3) * TT + p
    t["pos"] = np.stack([2 * token, 2 * token + 1], -1).astype(np.float32)
    t["valid"] = ((col % 3) * TT + p < T).astype(np.float32)
    level = np.array([8, 8, 8, 4, 4, 4, 2, 2, 2, 8], np.float32)
    t["dscale"] = np.tile(1 / level, (P, 1)).astype(np.float32)
    t["wscale"] = np.tile(1 / level ** 2, (P, 1)).astype(np.float32)
    return t


def blocks(x, rows, cols):
    lead = x.shape[:-2]
    n = len(lead)
    y = x.reshape(*lead, 32, rows, 4, cols)
    return y.transpose(*range(n), n + 2, n, n + 1, n + 3).reshape(*lead, P, rows * cols)


def halves(w):
    return w.reshape(C, P, -1).transpose(1, 0, 2)


def layout(d):
    r = {}
    r["x"] = blocks(d["x"][::-1, :, :, 0], 8, 64)
    r["wq0"] = halves(d["L0_attn_wq"].T)
    wk = d["L0_attn_wk"].T.reshape(256, KV, 1, 64)
    r["wk0"] = halves(np.repeat(wk, 2, axis=2).reshape(256, 512))
    r["wv0"] = halves(d["L0_attn_wv"].T)
    r["wo0"] = d["L0_attn_wo"].T.reshape(8, P, 256).transpose(1, 0, 2)
    kn = np.repeat(d["L0_attn_k_norm_w"].reshape(KV, 1, 64), 2, axis=1).reshape(KV, P)
    r["qkw0"] = np.concatenate([d["L0_attn_q_norm_w"].reshape(8, P), kn]).T
    r["w8"] = halves(d["L0_ffn_weight"].view(np.uint8).T)
    r["w8s"] = np.broadcast_to(d["L0_ffn_weight_scale"].reshape(1, 1), (P, 1))
    r["b8"] = d["L0_ffn_bias"].reshape(C, P).T
    r["wqk1"] = halves(d["L1_attn_w_qkv"][0:512].T)
    r["wv1"] = halves(d["L1_attn_w_qkv"][512:768].T)
    wp = np.zeros((H, 32, 256), np.float32)
    wp[:, 0:16] = d["L1_attn_w_proj"].T.reshape(H, 16, 256)
    wp[0, 16] = d["L1_attn_b_proj"]
    r["wp1"] = wp.reshape(4, P, 256).transpose(1, 0, 2)
    r["gb1"] = np.stack([np.tile(d["L1_attn_" + n], 8) for n in ("q_gamma", "k_gamma", "q_beta", "k_beta")], 1)
    r["wg"] = halves(d["L1_ffn_w_gate"].T)
    r["sw13"] = halves(np.concatenate([d["L1_ffn_sw1"].T, d["L1_ffn_sw3"].T], 1))
    r["sw2"] = halves(d["L1_ffn_sw2"].T)
    for n, name in (("ew1", "L1_ffn_w1"), ("ew3", "L1_ffn_w3")):
        r[n] = halves(d[name].transpose(1, 0, 2).reshape(256, NE * HID))
    r["ew2"] = d["L1_ffn_w2"].transpose(1, 0, 2)
    r["ebias"] = np.tile(d["L1_ffn_expert_bias"][None], (P, 1))
    r["clst"] = d["cls_tok"].reshape(C, P).T
    parts = []
    for name, n in (("L0_tok_Wd3", 128), ("L0_tok_Wd2", 64), ("L0_tok_Wd1", 32)):
        w = blocks(d[name].T.reshape(3, 3, n, n), n // 32, n // 4)
        parts.append(w.transpose(2, 0, 1, 3).reshape(P, 3, -1))
    wa = blocks(d["L0_tok_Wa"].reshape(32, 32), 1, 8)
    parts.append(np.broadcast_to(wa[:, None, :], (P, 3, 8)))
    r["wdet"] = np.concatenate(parts, 2)
    bias = np.concatenate([d["L0_tok_" + n] for n in ("bd1", "bd2", "bd3", "ba")])
    r["dbias"] = np.tile(bias[None], (P, 1))
    return r


def kernel(**inputs):
    import concourse.bacc as bacc
    from concourse.bass_utils import run_bass_kernel_spmd

    nc = bacc.Bacc("TRN2", target_bir_lowering=False, num_devices=1)
    data = layout({k: np.asarray(v) for k, v in inputs.items()})
    data.update(tables())
    arrays = {f"in_{k}": np.ascontiguousarray(v) for k, v in data.items()}
    aps = {k: nc.dram_tensor(f"in_{k}", arrays[f"in_{k}"].shape, mybir.dt.from_np(arrays[f"in_{k}"].dtype),
                             kind="ExternalInput").ap() for k in data}
    out = nc.dram_tensor("out_tokens", (NB, T, 256), F32, kind="ExternalOutput").ap()
    build_tower(nc, aps, out)
    result = run_bass_kernel_spmd(nc, [arrays], core_ids=[0])
    return result.results[0]["out_tokens"][::-1]
```

```python
from contextlib import ExitStack

import numpy as np

import concourse.bass as bass
from concourse import mybir

ALU = mybir.AluOpType
ACT = mybir.ActivationFunctionType
F32 = mybir.dt.float32
BF16 = mybir.dt.bfloat16
U8 = mybir.dt.uint8
I32 = mybir.dt.int32
AX_X = mybir.AxisListType.X
ABSMAX = bass.bass_isa.ReduceOp.absmax

P = 128
NB = 32
T = 257
TP = T + 1
C = 2
TT = 86
TILES = [(0, 86), (86, 86), (172, 85)]
H = 16
KV = 4
WINDOW = 128
NE = 8
HID = 128
NCOL = NB * 3

QR0 = [(0, 214), (86, 171), (172, 85)]
QC0 = [0, 214, 385]
W0 = 470
KR0 = [(0, 86), (0, 172), (44, 213)]
KC0 = [0, 86, 258]
W2 = 471
MASKED = -1e30
SLOPES = [float(np.float32(np.float32(2.0 ** (-8.0 / H)) ** np.float32(n + 1))) for n in range(H)]


class Signal:

    def __init__(self, sem, per):
        self.sem, self.per = sem, per

    def at(self, i, k):
        return i * self.per + k


class Chain:

    def __init__(self, eng, signal, i):
        self.eng, self.sem, self.per, self.i, self.n = eng, signal.sem, signal.per, i, 0

    def mark(self, ins):
        self.n += 1
        ins.then_inc(self.sem, 1)

    def sync(self):
        self.eng.wait_ge(self.sem, self.i * self.per + self.n)

    def step(self, ins):
        self.mark(ins)
        self.sync()

    def end(self):
        assert self.n == self.per, (self.n, self.per)


STRETCHES = {"first": 40, "att0": 28, "middle": 39, "att1": 24, "last": 13}


def stretches(name, part):
    n = 0
    for _ in part:
        n += 1
        yield
    assert n == STRETCHES[name], (name, n)


def weave(main, *sides):
    name, part = main
    rest = [[STRETCHES[n] * 1.06 / STRETCHES[name], 0.0, stretches(n, p)] for n, p in sides]
    for _ in stretches(name, part):
        for side in rest:
            side[1] += side[0]
            while side[1] >= 1:
                side[1] -= 1
                next(side[2], None)
    for side in rest:
        for _ in side[2]:
            pass


def schedule(eng, parts):
    def part(name, i):
        return name, parts[name](i)

    weave(part("first", 0))
    weave(part("att0", 0))
    weave(part("first", 1))
    weave(part("att0", 1), part("middle", 0))
    weave(part("att1", 0), part("first", 2))
    with eng.Fori(2, NB - 1) as i:
        weave(part("att0", i), part("middle", i - 1), part("last", i - 2))
        weave(part("att1", i - 1), part("first", i + 1))
    weave(part("att0", NB - 1), part("middle", NB - 2), part("last", NB - 3))
    weave(part("att1", NB - 2))
    weave(part("middle", NB - 1), part("last", NB - 2))
    weave(part("att1", NB - 1))
    weave(part("last", NB - 1))


class Norm:

    def __init__(self, n, src, work, banks, signal):
        self.src, (self.cen, self.csq, self.small, self.xn) = src, work
        self.mean_bank, self.var_bank = banks
        self.src_ready = signal(f"h{n}_ready", 1)
        self.mean_done = signal(f"mean{n}_done", 1)
        self.centred = signal(f"centred{n}", 1)
        self.squared = signal(f"squared{n}", 1)
        self.var_done = signal(f"var{n}_done", 1)
        self.root_done = signal(f"root{n}_done", 1)
        self.root_wide = signal(f"root{n}_wide", 1)
        self.done = signal(f"norm{n}_done", 1)


def build_tower(nc, a, out):
    with ExitStack() as ctx:
        def sb(name, shape, dt=F32):
            return ctx.enter_context(nc.sbuf_tensor("t_" + name, shape, dt))

        def sem(name):
            return ctx.enter_context(nc.semaphore(name))

        def signal(name, per):
            return Signal(sem(name), per)

        PS = ctx.enter_context(nc.psum_tensor("PS", [P, 8, 512], F32))

        loads = []

        def table(name, shape, dt=F32):
            t = sb(name, shape, dt)
            loads.append((t, a[name]))
            return t

        wq0 = table("wq0", [P, C, 1024])
        wk0 = table("wk0", [P, C, 512])
        wv0 = table("wv0", [P, C, 256])
        wo0 = table("wo0", [P, 8, 256])
        qkw0 = table("qkw0", [P, 12])
        w8 = table("w8", [P, C, 256], U8)
        w8s = table("w8s", [P, 1])
        b8 = table("b8", [P, C])
        wqk1 = table("wqk1", [P, C, 512])
        wv1 = table("wv1", [P, C, 256])
        wp1 = table("wp1", [P, 4, 256])
        gb1 = table("gb1", [P, 4])
        wg = table("wg", [P, C, NE])
        sw13 = table("sw13", [P, C, 512])
        sw2 = table("sw2", [P, C, 256])
        ebias = table("ebias", [P, NE])
        clst = table("clst", [P, C])
        wdet = table("wdet", [P, 3, 512])
        dbias = table("dbias", [P, 10])
        dscale = table("dscale", [P, 10])
        wscale = table("wscale", [P, 10])
        ident = table("ident", [P, P])
        block8 = table("block8", [P, 8])
        headmask = table("headmask", [P, C, H])
        collect = table("collect", [P, 4, H])
        spread = table("spread", [H, 4, P])
        sumsel = table("sumsel", [P, 4, 32])
        sumback = table("sumback", [P, 8, P])
        expand = table("expand", [32, 4, P])
        rotate = table("rotate", [P, P])
        cosT = table("cosT", [P, T])
        sinT = table("sinT", [P, T])
        parity = table("parity", [P, 2])
        relm = table("relm", [TT, W0])
        biasf = sb("biasq", [P, H * W2], BF16)
        biasq = biasf[:, :].rearrange("p (h n) -> p h n", h=H)
        pick = sb("pick", [P, H, P], BF16)
        pos = table("pos", [TT, NCOL, 2])
        valid = table("valid", [TT, NCOL])

        ones = sb("ones", [P, P])
        ones256 = sb("ones256", [P, P])
        ones1024 = sb("ones1024", [P, 1])
        ones512 = sb("ones512", [P, 1])
        onesb = sb("onesb", [P, P], BF16)
        identb = sb("identb", [P, H], BF16)
        w8b = sb("w8b", [P, C, 256], BF16)
        wmean = sb("wmean", [P, C, 32])

        img = sb("img", [P, 512])
        lohi = sb("lohi", [P, 2, 256])
        coef = sb("coef", [P, 504])
        avg = sb("avg", [P, 128 + 32 + 8])
        dots = sb("dots", [P, 10])
        z10 = sb("z10", [P, 10])
        mx3 = sb("mx3", [P, 3])
        e10 = sb("e10", [P, 10])
        s4 = sb("s4", [P, 4])
        w10 = sb("w10", [P, 2, 10])
        rec = sb("rec", [P, 8 + 32 + 128 + 512])
        relq = rec[0:TT, 0:W2]
        loads.append((relq, a["relq"]))
        dotx = rec[:, 0:384]
        h0 = sb("h0", [P, C, T])
        h1 = sb("h1", [P, C, T])
        h2 = sb("h2", [P, C, T])
        h3 = sb("h3", [P, C, T])

        def work(name):
            return (sb("cen" + name, [P, C, T]), sb("csq" + name, [P, C, TP]), sb("small" + name, [TT, 4, 3]),
                    sb("xn" + name, [P, C, T]))

        works = [work(name) for name in "ab"]
        norms = [Norm(0, h0, works[0], (7, 4), signal), Norm(1, h1, works[1], (4, 5), signal),
                 Norm(2, h2, works[1], (4, 5), signal), Norm(3, h3, works[0], (6, 7), signal)]
        n0, n1, n2, n3 = norms
        qk = sb("qk", [P, 12, TP])
        sq = sb("sq", [P, 12, TP])
        syn = qk[:, 0:3, 0:256]
        qks = sb("qks", [TT, 4, 6])
        qkb = sb("qkb", [P, 12, T], BF16)
        vx = sb("vx", [TT, 3, KV, 64])
        mtok = sb("mtok", [TT, 3, H])
        shift0 = sb("shift0", [P, T], BF16)
        att = sb("att", [P, 8 * 2 * 256])
        pre = att[0:TT, 0:2 * W0].rearrange("p (b n) -> p b n", b=2)
        pr0 = att[0:TT, 2 * W0:8 * W0].rearrange("p (b n) -> p b n", b=6)
        pr1 = att[:, :].rearrange("p (h t n) -> p h t n", h=8, t=2)
        y0 = sb("y0", [P, 8, T])
        zz = y0[:, 0:4, :]
        rsum = sb("rsum", [P, T])
        fs, fy, fm = sq[:, 0:4, 0:T], sq[:, 4:6, 0:T], sq[:, 6:8, 0:T]
        fq = sb("fq", [P, C, T], BF16)
        u1 = sb("u1", [P, 4, T])
        amax = u1[:, 0:2, :]
        sq1 = sb("sq1", [P, 4, TP])
        rsin = sq[:, 8:12, 0:T]
        root32 = sb("root32", [32, T])
        root1 = sb("root1", [TT, 4, 3, 32])
        qr = sb("qr", [P, 4, T])
        k1 = sb("k1", [P, 2, C, T])
        q1b = sb("q1b", [P, C, T], BF16)
        k1b = sb("k1b", [P, 2, C, T], BF16)
        v1x = sb("v1x", [P, 2, H, 32])
        vlast = sb("vlast", [H, H, 32])
        qlast = sb("qlast", [P, C, H])
        klast = sb("klast", [P, C, H])
        mlast = sb("mlast", [H, 1])
        mcol1 = sb("mcol1", [P, 2, H])
        mtok1 = sb("mtok1", [P, 2, H])
        shift1 = sb("shift1", [P, T], BF16)
        slast = sb("slast", [P, H], BF16)
        pklast = sb("pklast", [H, T])
        pqlast = sb("pqlast", [P, 2, H])
        rz = rsum[0:H, :]
        half_t = n3.csq
        gate_in = rec[:, 0:C * T].rearrange("p (c t) -> p c t", c=C)
        hh = n3.cen
        osb = sb("osb", [TT, 3, 256])
        lg = sb("lg", [TT, NCOL, NE])

        tables_loaded = sem("tables_loaded")
        dve_setup = sem("dve_setup")
        act_setup = sem("act_setup")
        chain_tok = signal("chain_tok", 41)
        chain_a = signal("chain_a", 20)
        chain_b = signal("chain_b", 45)
        chain_c = signal("chain_c", 12)
        chain_pool = signal("chain_pool", 16)
        image_loaded = sem("image_loaded")
        image_read = signal("image_read", 1)
        bands_ready = signal("bands_ready", 1)
        dots_ready = signal("dots_ready", 1)
        logits_summed = signal("logits_summed", 1)
        logits_shifted = signal("logits_shifted", 1)
        weights_exp = signal("weights_exp", 1)
        rec_ready = signal("rec_ready", 1)
        rec_turned = signal("rec_turned", 1)
        qk0_proj = signal("qk0_proj", 12)
        qk0_squared = signal("qk0_squared", 12)
        v0_proj = signal("v0_proj", 3)
        v0_ready = signal("v0_ready", 3)
        qk0_sums = signal("qk0_sums", 1)
        qk0_root = signal("qk0_root", 1)
        qk0_wide = signal("qk0_wide", 1)
        qk0_ready = signal("qk0_ready", 12)
        qk0_bf16 = signal("qk0_bf16", 3)
        rough0 = signal("rough0", H)
        rowmax0 = signal("rowmax0", H)
        max0_turned = signal("max0_turned", 1)
        shift0_ready = signal("shift0_ready", 1)
        scores0 = signal("scores0", H)
        biased0 = signal("biased0", H)
        probs0 = signal("probs0", H)
        pv0 = signal("pv0", 8)
        y0_copied = signal("y0_copied", 8)
        sums0 = signal("sums0", 4)
        rsum_ready = signal("rsum_ready", 1)
        rsum_wide = signal("rsum_wide", 8)
        y0_ready = signal("y0_ready", 8)
        wo0_done = signal("wo0_done", 1)
        absmax_done = signal("absmax_done", 1)
        fq_ready = signal("fq_ready", 1)
        ffn0_done = signal("ffn0_done", 1)
        qk1_proj = signal("qk1_proj", 4)
        qk1_squared = signal("qk1_squared", 4)
        v1_proj = signal("v1_proj", 3)
        v1_ready = signal("v1_ready", 2)
        vlast_ready = signal("vlast_ready", 1)
        qk1_var = signal("qk1_var", 1)
        qk1_root = signal("qk1_root", 1)
        root1_turned = signal("root1_turned", 1)
        root1_copied = signal("root1_copied", 1)
        qk1_wide = signal("qk1_wide", 4)
        qk1_normed = signal("qk1_normed", 4)
        qk1_beta = signal("qk1_beta", 4)
        qk1_turned = signal("qk1_turned", 4)
        sin_done = signal("sin_done", 4)
        rope_done = signal("rope_done", 4)
        last_ready = signal("last_ready", 1)
        k1_ready = signal("k1_ready", 5)
        rough_last = signal("rough_last", 2)
        last_max = signal("last_max", 2)
        rough1 = signal("rough1", H)
        rowmax1 = signal("rowmax1", H)
        max1_ready = signal("max1_ready", 1)
        max1_turned = signal("max1_turned", 1)
        shift1_ready = signal("shift1_ready", 2)
        slast_ready = signal("slast_ready", 1)
        last_scores = signal("last_scores", 1)
        last_probs = signal("last_probs", 2)
        scores1 = signal("scores1", H)
        probs1 = signal("probs1", H)
        pv1 = signal("pv1", 4)
        z_ready = signal("z_ready", 4)
        sums1 = signal("sums1", 1)
        rz_ready = signal("rz_ready", 1)
        rz_wide = signal("rz_wide", 4)
        y1_ready = signal("y1_ready", 4)
        proj1_done = signal("proj1_done", 1)
        gates = signal("gates", 1)
        gates_kept = signal("gates_kept", 2)
        gate_done = signal("gate_done", 2)
        gate_copied = signal("gate_copied", 2)
        value_done = signal("value_done", 2)
        hh_ready = signal("hh_ready", 2)
        out_tok = signal("out_tok", 3)
        out_copied = signal("out_copied", 3)
        out_stored = sem("out_stored")

        def inside(host, at, shape):
            names = " ".join("abcd"[:len(shape)])
            sizes = {"abcd"[n]: shape[n] for n in range(len(shape))}
            return host[0:TT, at:at + int(np.prod(shape))].rearrange(f"p ({names}) -> p {names}", **sizes)

        qkf = qk[:, :, :].rearrange("p n t -> p (n t)")
        sqf = sq[:, :, :].rearrange("p n t -> p (n t)")
        y0f = y0[:, :, :].rearrange("p n t -> p (n t)")
        N8 = NCOL * NE
        prob = inside(att, 0, [NCOL, NE])
        rt = inside(att, N8, [NCOL, NE])
        rk = inside(att, 2 * N8, [NCOL, NE])
        onehot = inside(att, 3 * N8, [NCOL, 2, NE])
        group = inside(sqf, 0, [NCOL, 2, NE])
        ge = inside(qkf, 0, [NCOL * 2, NE])
        g4 = inside(qkf, 2 * N8, [3, NCOL, 4])
        oh = inside(sqf, 2 * N8, [8, 64])
        ohw = inside(sqf, 2 * N8 + 512, [8, 64])
        he = inside(y0f, 0, [8, HID])
        hs = inside(y0f, 1024, [8, HID])
        u1f = u1[:, :, :].rearrange("p n t -> p (n t)")
        oht = u1f[0:64, 0:8 * TT]
        r1 = u1f[0:TT, 8 * TT:8 * TT + NCOL]
        weight = inside(u1f, 8 * TT + NCOL, [NCOL, 2])
        cnt = sb("cnt", [P, NE])
        offs = sb("offs", [TT, NE])
        u8sb = [t[0:NE, :, :].rearrange("p c n -> p (c n)").rearrange("p (g n) -> p g n", g=NE)
                for t in (wk0, sw13)]
        ew1 = wq0
        ew3 = wo0[:, :, :].rearrange("p (c a) n -> p c (a n)", c=C)
        ew2 = biasf[:, :].bitcast(F32)[:, 0:NE * 256]\
            .rearrange("p (g n) -> p g n", g=NE)
        images_done = sem("images_done")
        experts_loaded = sem("experts_loaded")
        u64 = h1[0:64, 0, 0:2 * HID]
        acct = h2[0:64, 0, 0:HID]
        accT = h0[:, 0, 0:64]
        r8 = osb[0:8, 0, :]

        table_hidden = signal("table_hidden", 1)
        hidden_copied = sem("hidden_copied")
        u64_loaded = sem("u64_loaded")
        pairs_stored = sem("pairs_stored")
        pair_dram = nc.dram_tensor("pair_hidden", (NE, NE, 2, HID), F32, kind="Internal").ap()
        counts_ready = sem("counts_ready")
        counts_summed = sem("counts_summed")
        onehots_ready = signal("onehots_ready", 1)
        onehots_turned = signal("onehots_turned", 1)
        turned_copied = signal("turned_copied", 1)
        routed_up = signal("routed_up", 1)
        routed_tanh = signal("routed_tanh", 1)
        routed_h = signal("routed_h", 1)
        routed_added = signal("routed_added", 1)
        acc_copied = sem("acc_copied")
        acc_turned = sem("acc_turned")
        accT_ready = sem("accT_ready")
        routed_out = sem("routed_out")
        rows_loaded = sem("rows_loaded")
        rows_ready = sem("rows_ready")
        rows_stored = sem("rows_stored")
        tail_chain = sem("tail_chain")

        SETUP_DVE = 48
        SETUP_ACT = 4
        ROUNDS = NCOL // 4

        def wait_next(eng, count, signal):
            eng.reg_add(count, count, 1)
            eng.wait_ge(tables_loaded, 16 * len(loads))
            eng.wait_ge(signal.sem, count)

        def head0(h):
            return slice(64 * (h % 2), 64 * (h % 2) + 64), h // 2, h // 4

        def head1(h):
            return h // 8, 32 * (h % 8 // 2), h % 2

        block = ctx.enter_context(nc.Block())

        @block.sync
        def _(sp):
            for t, src in loads:
                sp.dma_start(t if isinstance(t, bass.AP) else t[:], src).then_inc(tables_loaded, 16)
            with sp.Fori(0, NB) as i:
                sp.wait_ge(image_read.sem, image_read.at(i, 1))
                sp.dma_start(img[:, :], a["x"][bass.ds(i, 1), :, :].rearrange("a p n -> (a p) n"))\
                    .then_inc(image_loaded, 16)
            sp.wait_ge(images_done, 1)
            sp.dma_start(ew1[:, :, :], a["ew1"]).then_inc(experts_loaded, 16)
            sp.dma_start(ew3, a["ew3"].rearrange("p c n -> p c n")).then_inc(experts_loaded, 16)
            sp.dma_start(ew2, a["ew2"]).then_inc(experts_loaded, 16)
            sp.wait_ge(hidden_copied, 2)
            for s in range(2):
                sp.dma_start(pair_dram[:, :, s, :], u8sb[s]).then_inc(pairs_stored, 16)
            sp.wait_ge(pairs_stored, 32)
            sp.dma_start(u64[:, :], pair_dram.rearrange("e g s n -> (e g) (s n)")).then_inc(u64_loaded, 16)
            sp.wait_ge(out_stored, 32 * NB + 32)
            sp.dma_start(r8, out[NB - 1, 0:8, :]).then_inc(rows_loaded, 16)
            sp.wait_ge(rows_ready, 1)
            sp.dma_start(out[NB - 1, 0:8, :], r8).then_inc(rows_stored, 16)
            sp.wait_ge(rows_stored, 16)

        @block.gpsimd
        def _(pool):
            G = nc.gpsimd
            n_ln = pool.alloc_register("n_ln")
            pool.reg_mov(n_ln, 0)

            def nothing(name):
                def part(i):
                    for _ in range(STRETCHES[name]):
                        yield
                return part

            def first(i):
                ch = Chain(pool, chain_pool, i)
                pool.wait_ge(image_loaded, i * 16 + 16)
                pool.wait_ge(rec_ready.sem, rec_ready.at(i, 1))
                x0 = img[:, :]
                rows = 8
                for lev in range(3):
                    n = [128, 32, 8][lev]
                    half = rows // 2
                    v = x0.rearrange("p (n e) -> p n e", e=2)
                    lo, hi = lohi[:, 0, 0:2 * n], lohi[:, 1, 0:2 * n]
                    ch.mark(G.tensor_tensor(lo, v[:, :, 0], v[:, :, 1], op=ALU.add))
                    sub = G.tensor_tensor(hi, v[:, :, 0], v[:, :, 1], op=ALU.subtract)
                    if lev == 0:
                        sub.then_inc(image_read.sem, 1)
                        ch.sync()
                        pool.wait_ge(image_read.sem, image_read.at(i, 2))
                    else:
                        ch.step(sub)
                    c0 = [0, 384, 480][lev]
                    a0 = [0, 128, 160][lev]
                    lo = lo.rearrange("p (r e n) -> p r e n", r=half, e=2)
                    hi = hi.rearrange("p (r e n) -> p r e n", r=half, e=2)

                    def sub_of(t, at):
                        return t[:, at:at + n].rearrange("p (r n) -> p r n", r=half)

                    ch.mark(G.tensor_tensor(sub_of(coef, c0), lo[:, :, 0], lo[:, :, 1], op=ALU.subtract))
                    ch.mark(G.tensor_tensor(sub_of(coef, c0 + n), hi[:, :, 0], hi[:, :, 1], op=ALU.add))
                    ch.mark(G.tensor_tensor(sub_of(coef, c0 + 2 * n), hi[:, :, 0], hi[:, :, 1], op=ALU.subtract))
                    av = G.tensor_tensor(sub_of(avg, a0), lo[:, :, 0], lo[:, :, 1], op=ALU.add)
                    if lev < 2:
                        ch.step(av)
                    else:
                        av.then_inc(bands_ready.sem, 1)
                    x0 = avg[:, a0:a0 + n]
                    rows = half
                ch.end()
                for _ in range(STRETCHES["first"]):
                    yield

            def middle(i):
                for _ in range(4):
                    yield
                wait_next(pool, n_ln, n1.done)
                pool.partition_all_reduce(amax, n1.xn[:, :, :], P, ABSMAX).then_inc(absmax_done.sem, 1)
                for _ in range(STRETCHES["middle"] - 4):
                    yield

            schedule(pool, {"first": first, "att0": nothing("att0"), "middle": middle,
                            "att1": nothing("att1"), "last": nothing("last")})

        @block.tensor
        def _(pe):
            def mm(o, l, r, start=True, stop=True, loose=False):
                return pe.matmul(o, l, r, start=start, stop=stop, skip_group_check=loose)

            pe.wait_ge(tables_loaded, 16 * len(loads))
            pe.wait_ge(dve_setup, SETUP_DVE)
            pe.wait_ge(act_setup, SETUP_ACT)

            n_rec = pe.alloc_register("n_rec")
            pe.reg_mov(n_rec, 1)

            def layernorm(nm, i):
                pe.wait_ge(nm.src_ready.sem, nm.src_ready.at(i, 1))
                for c in range(C):
                    m = mm(PS[:, nm.mean_bank, 0:T], ones256[:, :], nm.src[:, c, :], c == 0, c == C - 1)
                m.then_inc(nm.mean_done.sem, 1)
                yield
                yield
                pe.wait_ge(nm.squared.sem, nm.squared.at(i, 1))
                for t in range(3):
                    for c in range(C):
                        m = mm(PS[0:TT, nm.var_bank, t:t + 1], nm.csq[:, c, t * TT:(t + 1) * TT],
                               ones256[:, 0:1], c == 0, c == C - 1)
                m.then_inc(nm.var_done.sem, 1)
                yield
                pe.wait_ge(nm.root_done.sem, nm.root_done.at(i, 1))
                for t, (t0, tn) in enumerate(TILES):
                    m = mm(PS[:, nm.mean_bank, t0:t0 + tn], nm.small[:, 0, t:t + 1].broadcast_to([TT, P]),
                           ident[0:TT, 0:tn])
                m.then_inc(nm.root_wide.sem, 1)
                yield
                pe.wait_ge(nm.done.sem, nm.done.at(i, 1))

            def first(i):
                yield
                pe.wait_ge(dots_ready.sem, dots_ready.at(i, 1))
                mm(PS[:, 4, 0:10], ones[:, :], dots[:, :]).then_inc(logits_summed.sem, 1)
                yield
                yield
                yield
                yield
                wait_next(pe, n_rec, rec_ready)
                for r in range(8):
                    m = pe.transpose(PS[0:64, 5 + r // 4, (r % 4) * P:(r % 4 + 1) * P],
                                     rec[:, 168 + 64 * r:168 + 64 * (r + 1)], ident[:, :])
                m.then_inc(rec_turned.sem, 1)
                yield
                yield
                yield from layernorm(n0, i)
                for n in range(12):
                    w, j = (wq0, n) if n < 8 else (wk0, n - 8)
                    if n >= 4:
                        pe.wait_ge(qk0_squared.sem, qk0_squared.at(i, n - 3))
                    for c in range(C):
                        m = mm(PS[:, 4 + n % 4, 0:T], w[:, c, j * P:(j + 1) * P], n0.xn[:, c, :],
                               c == 0, c == C - 1)
                    m.then_inc(qk0_proj.sem, 1)
                    yield
                for t, (t0, tn) in enumerate(TILES):
                    pe.wait_ge(qk0_squared.sem, qk0_squared.at(i, 9 + t))
                    for c in range(C):
                        m = mm(PS[0:tn, 4 + t, 0:256], n0.xn[:, c, t0:t0 + tn], wv0[:, c, :], c == 0, c == C - 1)
                    m.then_inc(v0_proj.sem, 1)
                    yield
                pe.wait_ge(qk0_squared.sem, qk0_squared.at(i, 12))
                for t in range(3):
                    for b, (lo, hi, col) in enumerate(((0, 8, ones1024), (8, 12, ones512))):
                        for n in range(lo, hi):
                            m = mm(PS[0:TT, 7, 2 * t + b:2 * t + b + 1], sq[:, n, t * TT:(t + 1) * TT],
                                   col[:, :], n == lo, n == hi - 1)
                m.then_inc(qk0_sums.sem, 1)
                yield
                pe.wait_ge(v0_ready.sem, v0_ready.at(i, 3))
                pe.wait_ge(qk0_root.sem, qk0_root.at(i, 1))
                for b in range(2):
                    for t, (t0, tn) in enumerate(TILES):
                        m = mm(PS[:, 4 + b, t0:t0 + tn],
                               qks[:, 0, 2 * t + b:2 * t + b + 1].broadcast_to([TT, P]), ident[0:TT, 0:tn])
                m.then_inc(qk0_wide.sem, 1)
                yield
                yield
                yield
                pe.wait_ge(qk0_bf16.sem, qk0_bf16.at(i, 3))
                for h in range(H):
                    rows, j, g = head0(h)
                    if h >= 4:
                        pe.wait_ge(rowmax0.sem, rowmax0.at(i, h - 3))
                    for (t0, tn), (k0, kn), kc in zip(TILES, KR0, KC0):
                        m = mm(PS[0:tn, 4 + h % 4, kc:kc + kn], qkb[rows, j, t0:t0 + tn],
                               qkb[rows, 8 + g, k0:k0 + kn])
                    m.then_inc(rough0.sem, 1)
                    if h % 2:
                        yield
                pe.wait_ge(rowmax0.sem, rowmax0.at(i, H))
                for t, (t0, tn) in enumerate(TILES):
                    m = pe.transpose(PS[0:H, 4, t0:t0 + tn], mtok[0:tn, t, :], ident[0:tn, 0:tn])
                m.then_inc(max0_turned.sem, 1)
                yield
                pe.wait_ge(shift0_ready.sem, shift0_ready.at(i, 1))
                yield

            def att0(i):
                def score(h):
                    rows, j, g = head0(h)
                    if h >= 2:
                        pe.wait_ge(biased0.sem, biased0.at(i, h - 1))
                    for t in range(3):
                        (q0, qn), c0 = QR0[t], QC0[t]
                        mm(PS[0:TT, h % 2, c0:c0 + qn], qk[rows, 8 + g, t * TT:(t + 1) * TT],
                           qk[rows, j, q0:q0 + qn], True, False)
                        m = mm(PS[0:TT, h % 2, c0:c0 + qn], pick[:, h, 0:TT], shift0[:, q0:q0 + qn], False, True)
                    m.then_inc(scores0.sem, 1)

                score(0)
                score(1)
                yield
                for j in range(8):
                    if j < 7:
                        score(2 * j + 2)
                    yield
                    if j < 7:
                        score(2 * j + 3)
                    pe.wait_ge(probs0.sem, probs0.at(i, 2 * j + 2))
                    if j:
                        pe.wait_ge(y0_copied.sem, y0_copied.at(i, j))
                    for t in range(3):
                        (q0, qn), c0 = QR0[t], QC0[t]
                        for h in (2 * j, 2 * j + 1):
                            k = 64 * (h % 2)
                            m = mm(PS[k:k + 64, 2, q0:q0 + qn], vx[:, t, h // 4, :], pr0[:, h % 6, c0:c0 + qn],
                                   t == 0, t == 2, loose=True)
                    m.then_inc(pv0.sem, 1)
                    if j % 2:
                        g = j // 2
                        for t in range(3):
                            (q0, qn), c0 = QR0[t], QC0[t]
                            for k in range(4):
                                h = 4 * g + k
                                m = mm(PS[32 * k:32 * k + 32, 3, q0:q0 + qn], sumsel[0:TT, g, :],
                                       pr0[:, h % 6, c0:c0 + qn], t == 0 and g == 0, t == 2 and g == 3,
                                       loose=True)
                        m.then_inc(sums0.sem, 1)
                    yield
                pe.wait_ge(y0_copied.sem, y0_copied.at(i, 8))
                yield
                pe.wait_ge(rsum_ready.sem, rsum_ready.at(i, 1))
                for j in range(8):
                    if j >= 2:
                        pe.wait_ge(y0_ready.sem, y0_ready.at(i, j - 1))
                    mm(PS[:, j % 2, 0:T], sumback[:, j, :], rsum[:, :]).then_inc(rsum_wide.sem, 1)
                    if j >= 1:
                        yield
                        pe.wait_ge(y0_ready.sem, y0_ready.at(i, j))
                        for c in range(C):
                            mm(PS[:, 2 + c, 0:T], wo0[:, j - 1, c * P:(c + 1) * P], y0[:, j - 1, :], j == 1,
                               False, loose=True)
                yield
                pe.wait_ge(y0_ready.sem, y0_ready.at(i, 8))
                for c in range(C):
                    m = mm(PS[:, 2 + c, 0:T], wo0[:, 7, c * P:(c + 1) * P], y0[:, 7, :], False, True, loose=True)
                m.then_inc(wo0_done.sem, 1)
                yield
                pe.wait_ge(n1.src_ready.sem, n1.src_ready.at(i, 1))
                yield

            def middle(i):
                yield from layernorm(n1, i)
                yield
                yield
                pe.wait_ge(fq_ready.sem, fq_ready.at(i, 1))
                for o in range(C):
                    for c in range(C):
                        m = mm(PS[:, 4 + o, 0:T], w8b[:, c, o * P:(o + 1) * P], fq[:, c, :], c == 0, c == C - 1)
                m.then_inc(ffn0_done.sem, 1)
                yield
                yield from layernorm(n2, i)
                for n in range(4):
                    if n >= 2:
                        pe.wait_ge(qk1_squared.sem, qk1_squared.at(i, n - 1))
                    for c in range(C):
                        m = mm(PS[:, 4 + n % 2, 0:T], wqk1[:, c, n * P:(n + 1) * P], n2.xn[:, c, :],
                               c == 0, c == C - 1)
                    m.then_inc(qk1_proj.sem, 1)
                    yield
                for t in range(2):
                    pe.wait_ge(qk1_squared.sem, qk1_squared.at(i, 3 + t))
                    for c in range(C):
                        m = mm(PS[:, 4 + t, 0:256], n2.xn[:, c, t * P:(t + 1) * P], wv1[:, c, :],
                               c == 0, c == C - 1)
                    m.then_inc(v1_proj.sem, 1)
                yield
                pe.wait_ge(v1_ready.sem, v1_ready.at(i, 1))
                for c in range(C):
                    m = mm(PS[0:H, 4, 0:256], n2.xn[:, c, 256:257].broadcast_to([P, H]), wv1[:, c, :],
                           c == 0, c == C - 1)
                m.then_inc(v1_proj.sem, 1)
                pe.wait_ge(v1_ready.sem, v1_ready.at(i, 2))
                for t in range(3):
                    for n in range(4):
                        m = mm(PS[0:TT, 5, 32 * t + 8 * n:32 * t + 8 * n + 8], sq1[:, n, t * TT:(t + 1) * TT],
                               block8[:, :])
                m.then_inc(qk1_var.sem, 1)
                yield
                pe.wait_ge(qk1_root.sem, qk1_root.at(i, 1))
                pe.wait_ge(vlast_ready.sem, vlast_ready.at(i, 1))
                for t, (t0, tn) in enumerate(TILES):
                    m = mm(PS[0:32, 4, t0:t0 + tn], root1[:, 0, t, :], ident[0:TT, 0:tn])
                m.then_inc(root1_turned.sem, 1)
                yield
                pe.wait_ge(root1_copied.sem, root1_copied.at(i, 1))
                for n in range(4):
                    if n >= 2:
                        pe.wait_ge(qk1_normed.sem, qk1_normed.at(i, n - 1))
                    mm(PS[:, 4 + n % 2, 0:T], expand[:, n, :], root32[:, :]).then_inc(qk1_wide.sem, 1)
                    yield
                for n in range(4):
                    pe.wait_ge(qk1_beta.sem, qk1_beta.at(i, n + 1))
                    if n >= 2:
                        pe.wait_ge(sin_done.sem, sin_done.at(i, n - 1))
                    else:
                        pe.wait_ge(qk1_normed.sem, qk1_normed.at(i, n + 3))
                    mm(PS[:, 4 + n % 2, 0:T], rotate[:, :], u1[:, n, :]).then_inc(qk1_turned.sem, 1)
                    yield
                yield
                pe.wait_ge(sin_done.sem, sin_done.at(i, 4))
                pe.wait_ge(last_ready.sem, last_ready.at(i, 1))
                for c in range(C):
                    m = mm(PS[0:H, 4, 0:T], qlast[:, c, :], qr[:, 2 + c, :], c == 0, c == C - 1)
                m.then_inc(rough_last.sem, 1)
                for t in range(2):
                    for c in range(C):
                        m = mm(PS[:, 5, H * t:H * t + H], qr[:, c, t * P:(t + 1) * P], klast[:, c, :],
                               c == 0, c == C - 1)
                m.then_inc(rough_last.sem, 1)
                yield
                pe.wait_ge(k1_ready.sem, k1_ready.at(i, 5))
                for h in range(H):
                    c, r, par = head1(h)
                    if h >= 2:
                        pe.wait_ge(rowmax1.sem, rowmax1.at(i, h - 1))
                    else:
                        pe.wait_ge(last_max.sem, last_max.at(i, h + 1))
                    for t in range(2):
                        m = mm(PS[:, 4 + h % 2, 256 * t:256 * t + 256], q1b[r:r + 32, c, t * P:(t + 1) * P],
                               k1b[r:r + 32, par, c, 0:256])
                    m.then_inc(rough1.sem, 1)
                    if h % 2:
                        yield
                pe.wait_ge(max1_ready.sem, max1_ready.at(i, 1))
                for t in range(2):
                    m = mm(PS[0:H, 4, t * P:(t + 1) * P], mtok1[:, t, :], ident[:, :])
                m.then_inc(max1_turned.sem, 1)
                yield
                pe.wait_ge(shift1_ready.sem, shift1_ready.at(i, 2))
                for c in range(C):
                    mm(PS[0:H, 5, 0:T], klast[:, c, :], qr[:, c, :], c == 0, False)
                mm(PS[0:H, 5, 0:T], identb[:, :], shift1[:, :], False, True)
                pe.wait_ge(slast_ready.sem, slast_ready.at(i, 1))
                for t in range(2):
                    for c in range(C):
                        mm(PS[:, 4, H * t:H * t + H], qr[:, 2 + c, t * P:(t + 1) * P], qlast[:, c, :],
                           c == 0, False)
                    m = mm(PS[:, 4, H * t:H * t + H], onesb[:, :], slast[:, :], False, True)
                m.then_inc(last_scores.sem, 1)
                yield
                pe.wait_ge(last_probs.sem, last_probs.at(i, 2))
                yield

            def att1(i):
                def context(g):
                    pe.wait_ge(probs1.sem, probs1.at(i, 4 * g + 4))
                    if g >= 2:
                        pe.wait_ge(z_ready.sem, z_ready.at(i, g - 1))
                    heads = range(4 * g, 4 * g + 4)
                    for t in range(2):
                        for h in heads:
                            k = 32 * (h % 4)
                            mm(PS[k:k + 32, 2 + g % 2, 0:256], v1x[:, t, h, :], pr1[:, h % 8, t, :], t == 0,
                               False, loose=True)
                        for h in heads:
                            k = 32 * (h % 4)
                            mm(PS[k:k + 32, 2 + g % 2, 256:257], v1x[:, t, h, :], pqlast[:, t, h:h + 1], False,
                               False, loose=True)
                    mm(PS[:, 2 + g % 2, 0:T], vlast[:, 4 * g:4 * g + 4, :], pklast[:, :], False, True,
                       loose=True).then_inc(pv1.sem, 1)

                for h in range(H):
                    c, r, par = head1(h)
                    if h >= 2:
                        pe.wait_ge(probs1.sem, probs1.at(i, h - 1))
                    for t in range(2):
                        o = PS[:, h % 2, 256 * t:256 * t + 256]
                        mm(o, k1[r:r + 32, par, c, t * P:(t + 1) * P], qr[r:r + 32, c, 0:256], True, False)
                        m = mm(o, pick[:, h, :], shift1[:, 0:256], False, True)
                    m.then_inc(scores1.sem, 1)
                    if h % 4 == 1 and h > 4:
                        context(h // 4 - 1)
                    yield
                context(3)
                yield
                pe.wait_ge(z_ready.sem, z_ready.at(i, 4))
                for g in range(4):
                    m = mm(PS[0:H, 0, 0:T], collect[:, g, :], zz[:, g, :], g == 0, g == 3)
                m.then_inc(sums1.sem, 1)
                yield
                pe.wait_ge(rz_ready.sem, rz_ready.at(i, 1))
                for n in range(4):
                    if n >= 2:
                        pe.wait_ge(y1_ready.sem, y1_ready.at(i, n - 1))
                    mm(PS[:, n % 2, 0:T], spread[:, n, :], rz[:, :]).then_inc(rz_wide.sem, 1)
                    if n >= 1:
                        yield
                        pe.wait_ge(y1_ready.sem, y1_ready.at(i, n))
                        for c in range(C):
                            mm(PS[:, 2 + c, 0:T], wp1[:, n - 1, c * P:(c + 1) * P], zz[:, n - 1, :], n == 1,
                               False, loose=True)
                yield
                pe.wait_ge(y1_ready.sem, y1_ready.at(i, 4))
                for c in range(C):
                    m = mm(PS[:, 2 + c, 0:T], wp1[:, 3, c * P:(c + 1) * P], zz[:, 3, :], False, True, loose=True)
                m.then_inc(proj1_done.sem, 1)
                yield
                pe.wait_ge(n3.src_ready.sem, n3.src_ready.at(i, 1))
                yield

            def last(i):
                yield from layernorm(n3, i)
                for t, (t0, tn) in enumerate(TILES):
                    for c in range(C):
                        m = mm(PS[0:tn, 7, t * NE:(t + 1) * NE], n3.xn[:, c, t0:t0 + tn], wg[:, c, :],
                               c == 0, c == C - 1)
                m.then_inc(gates.sem, 1)
                yield
                for n in range(2):
                    if n:
                        pe.wait_ge(gate_copied.sem, gate_copied.at(i, 1))
                        pe.wait_ge(hh_ready.sem, hh_ready.at(i, 1))
                    for c in range(C):
                        m = mm(PS[:, 6, 0:T], sw13[:, c, n * P:(n + 1) * P], n3.xn[:, c, :], c == 0, c == C - 1)
                    m.then_inc(gate_done.sem, 1)
                    yield
                    if not n:
                        pe.wait_ge(gates_kept.sem, gates_kept.at(i, 2))
                    for c in range(C):
                        m = mm(PS[:, 7, 0:T], sw13[:, c, (2 + n) * P:(3 + n) * P], n3.xn[:, c, :],
                               c == 0, c == C - 1)
                    m.then_inc(value_done.sem, 1)
                    yield
                pe.wait_ge(gate_copied.sem, gate_copied.at(i, 2))
                pe.wait_ge(hh_ready.sem, hh_ready.at(i, 2))
                for t, (t0, tn) in enumerate(TILES):
                    bank = 6 + t % 2
                    if t == 2:
                        pe.wait_ge(out_copied.sem, out_copied.at(i, 1))
                    for c in range(C):
                        mm(PS[0:tn, bank, 0:256], hh[:, c, t0:t0 + tn], sw2[:, c, :], c == 0, False, loose=True)
                    for c in range(C):
                        m = mm(PS[0:tn, bank, c * P:(c + 1) * P], h3[:, c, t0:t0 + tn], ident[:, :],
                               False, c == C - 1, loose=True)
                    m.then_inc(out_tok.sem, 1)
                    yield
                pe.wait_ge(out_copied.sem, out_copied.at(i, 3))
                yield

            schedule(pe, {"first": first, "att0": att0, "middle": middle, "att1": att1, "last": last})
            pe.wait_ge(gates_kept.sem, gates_kept.at(NB - 1, 2))
            pe.transpose(PS[0:64, 0, 0:P], ident[:, 0:64], ident[:, :]).then_inc(images_done, 1)

            pe.wait_ge(experts_loaded, 48)
            for s, w in enumerate((ew1, ew3)):
                for b in range(2):
                    for c in range(C):
                        m = mm(PS[0:8, 2 * s + b, 0:512], n3.xn[:, c, 0:8], w[:, c, 512 * b:512 * (b + 1)],
                               c == 0, c == C - 1)
            m.then_inc(table_hidden.sem, 1)
            pe.wait_ge(counts_ready, 1)
            mm(PS[:, 4, 0:NE], ones[0:TT, :], cnt[0:TT, :]).then_inc(counts_summed, 1)
            pe.wait_ge(u64_loaded, 16)
            pe.wait_ge(hidden_copied, 2)
            n_onehots = pe.alloc_register("n_onehots")
            pe.reg_mov(n_onehots, 0)
            with pe.Fori(0, ROUNDS) as r:
                wait_next(pe, n_onehots, onehots_ready)
                for n in range(8):
                    m = pe.transpose(PS[0:64, 4 + n // 4, (n % 4) * TT:(n % 4 + 1) * TT], ohw[:, n, :],
                                     ident[0:TT, 0:TT])
                m.then_inc(onehots_turned.sem, 1)
                pe.wait_ge(turned_copied.sem, turned_copied.at(r, 1))
                for n in range(8):
                    m = mm(PS[0:TT, n // 2, 256 * (n % 2):256 * (n % 2) + 256], oht[:, n * TT:(n + 1) * TT],
                           u64[:, :])
                m.then_inc(routed_up.sem, 1)
                pe.wait_ge(routed_h.sem, routed_h.at(r, 1))
                for n in range(8):
                    m = mm(PS[0:64, 6, 0:HID], oh[:, n, :], hs[:, n, :], n == 0, n == 7)
                m.then_inc(routed_added.sem, 1)
            pe.wait_ge(acc_copied, ROUNDS + 1)
            pe.transpose(PS[:, 4, 0:64], acct[:, :], ident[0:64, 0:64]).then_inc(acc_turned, 1)
            pe.wait_ge(accT_ready, 1)
            turned = accT[:, :].rearrange("p (e g) -> p g e", g=NE)
            for g in range(NE):
                m = mm(PS[0:8, 5, 0:256], turned[:, g, :], ew2[:, g, :], g == 0, g == NE - 1)
            m.then_inc(routed_out, 1)

        @block.scalar
        def _(act):
            A = nc.scalar.activation
            act.wait_ge(tables_loaded, 16 * len(loads))
            A(h0[:, :, 0:1], clst[:, :].rearrange("p (c a) -> p c a", a=1), ACT.Copy).then_inc(act_setup, 1)
            A(osb[0:1, 0, 0:4], ident[0:1, 0:4], ACT.Copy).then_inc(out_stored, 32)
            A(gb1[:, 0:1], gb1[:, 0:1], ACT.Copy, scale=0.25).then_inc(act_setup, 1)
            A(gb1[:, 2:3], gb1[:, 2:3], ACT.Copy, scale=0.25).then_inc(act_setup, 1)
            A(qkw0[:, 0:8], qkw0[:, 0:8], ACT.Copy, scale=0.125).then_inc(act_setup, 1)
            act.wait_ge(act_setup, SETUP_ACT)
            act.wait_ge(dve_setup, SETUP_DVE)

            def idle(n):
                for _ in range(n):
                    yield

            def layernorm(nm, i):
                yield
                act.wait_ge(nm.centred.sem, nm.centred.at(i, 1))
                A(nm.csq[:, :, 0:T], nm.cen[:, :, :], ACT.Square).then_inc(nm.squared.sem, 1)
                yield
                yield
                yield

            def first(i):
                yield
                yield
                act.wait_ge(logits_shifted.sem, logits_shifted.at(i, 1))
                A(e10[:, :], z10[:, :], ACT.Exp).then_inc(weights_exp.sem, 1)
                yield from idle(4)
                act.wait_ge(rec_turned.sem, rec_turned.at(i, 1))
                for cg in range(4):
                    src = PS[0:64, 5:7, :].rearrange("p b (r q n) -> p b r q n", r=4, q=4)[:, :, :, cg, :]
                    dst = h0[64 * (cg % 2):64 * (cg % 2) + 64, cg // 2, 1:T]\
                        .rearrange("p (n b r) -> p b r n", b=2, r=4)
                    cp = A(dst, src, ACT.Copy)
                cp.then_inc(n0.src_ready.sem, 1)
                yield
                yield from layernorm(n0, i)
                for n in range(12):
                    act.wait_ge(qk0_proj.sem, qk0_proj.at(i, n + 1))
                    A(qk[:, n, 0:T], PS[:, 4 + n % 4, 0:T], ACT.Copy)
                    A(sq[:, n, 0:T], PS[:, 4 + n % 4, 0:T], ACT.Square).then_inc(qk0_squared.sem, 1)
                    yield
                for t, (_, tn) in enumerate(TILES):
                    act.wait_ge(v0_proj.sem, v0_proj.at(i, t + 1))
                    A(vx[0:tn, t, :, :], PS[0:tn, 4 + t, 0:256].rearrange("p (g d) -> p g d", g=KV), ACT.Copy)\
                        .then_inc(v0_ready.sem, 1)
                    yield
                yield
                for n in range(3):
                    act.wait_ge(qk0_ready.sem, qk0_ready.at(i, 4 * n + 4))
                    A(qkb[:, 4 * n:4 * n + 4, :], qk[:, 4 * n:4 * n + 4, 0:T], ACT.Copy).then_inc(qk0_bf16.sem, 1)
                    yield
                yield from idle(8)
                act.wait_ge(max0_turned.sem, max0_turned.at(i, 1))
                A(shift0[0:H, :], PS[0:H, 4, 0:T], ACT.Copy, scale=-1.0).then_inc(shift0_ready.sem, 1)
                yield
                yield

            def att0(i):
                def prob0(h):
                    act.wait_ge(biased0.sem, biased0.at(i, h + 1))
                    if h >= 6:
                        act.wait_ge(sums0.sem, sums0.at(i, (h - 6) // 4 + 1))
                    A(pr0[:, h % 6, :], pre[:, h % 2, :], ACT.Exp).then_inc(probs0.sem, 1)

                prob0(0)
                prob0(1)
                yield
                for j in range(8):
                    if j < 7:
                        prob0(2 * j + 2)
                    yield
                    act.wait_ge(pv0.sem, pv0.at(i, j + 1))
                    A(y0[:, j, :], PS[:, 2, 0:T], ACT.Copy).then_inc(y0_copied.sem, 1)
                    if j < 7:
                        prob0(2 * j + 3)
                    yield
                yield from idle(11)

            def middle(i):
                yield from layernorm(n1, i)
                yield from idle(3)
                yield from layernorm(n2, i)
                for n in range(4):
                    act.wait_ge(qk1_proj.sem, qk1_proj.at(i, n + 1))
                    A(u1[:, n, :], PS[:, 4 + n % 2, 0:T], ACT.Copy, scale=gb1[:, n // 2:n // 2 + 1])
                    A(sq1[:, n, 0:T], PS[:, 4 + n % 2, 0:T], ACT.Square).then_inc(qk1_squared.sem, 1)
                    yield
                for t in range(2):
                    act.wait_ge(v1_proj.sem, v1_proj.at(i, t + 1))
                    A(v1x[:, t, :, 0:16], PS[:, 4 + t, 0:256].rearrange("p (h d) -> p h d", h=H), ACT.Copy)\
                        .then_inc(v1_ready.sem, 1)
                yield
                yield
                yield from idle(5)
                for n in range(4):
                    act.wait_ge(qk1_normed.sem, qk1_normed.at(i, n + 1))
                    A(u1[:, n, :], u1[:, n, :], ACT.Identity, bias=gb1[:, 2 + n // 2:3 + n // 2])\
                        .then_inc(qk1_beta.sem, 1)
                    yield
                act.wait_ge(rope_done.sem, rope_done.at(i, 4))
                A(q1b[:, :, :], qr[:, 0:2, :], ACT.Copy).then_inc(k1_ready.sem, 1)
                for par in range(2):
                    A(k1b[:, par, :, :], qr[:, 2:4, :], ACT.Copy, scale=parity[:, par:par + 1])\
                        .then_inc(k1_ready.sem, 1)
                    A(k1[:, par, :, :], qr[:, 2:4, :], ACT.Copy, scale=parity[:, par:par + 1])\
                        .then_inc(k1_ready.sem, 1)
                yield
                yield
                yield from idle(8)
                act.wait_ge(max1_turned.sem, max1_turned.at(i, 1))
                A(shift1[0:H, 0:256], PS[0:H, 4, 0:256], ACT.Copy, scale=-1.0).then_inc(shift1_ready.sem, 1)
                yield
                act.wait_ge(last_scores.sem, last_scores.at(i, 1))
                A(pklast[:, :], PS[0:H, 5, 0:T], ACT.Exp).then_inc(last_probs.sem, 1)
                A(pqlast[:, :, :], PS[:, 4, 0:2 * H].rearrange("p (t h) -> p t h", t=2), ACT.Exp)\
                    .then_inc(last_probs.sem, 1)
                yield
                yield

            def att1(i):
                def keep(g):
                    act.wait_ge(pv1.sem, pv1.at(i, g + 1))
                    A(zz[:, g, :], PS[:, 2 + g % 2, 0:T], ACT.Copy).then_inc(z_ready.sem, 1)

                for h in range(H):
                    act.wait_ge(scores1.sem, scores1.at(i, h + 1))
                    if h >= 8:
                        act.wait_ge(pv1.sem, pv1.at(i, h // 4 - 1))
                    A(pr1[:, h % 8, :, :], PS[:, h % 2, :].rearrange("p (t n) -> p t n", t=2), ACT.Exp)\
                        .then_inc(probs1.sem, 1)
                    if h % 4 == 2 and h > 4:
                        keep(h // 4 - 1)
                    yield
                keep(3)
                yield
                yield from idle(7)

            def last(i):
                yield from layernorm(n3, i)
                yield
                for n in range(2):
                    act.wait_ge(gate_done.sem, gate_done.at(i, n + 1))
                    A(half_t[:, n, 0:T], PS[:, 6, 0:T], ACT.Tanh, scale=0.5)
                    A(gate_in[:, n, :], PS[:, 6, 0:T], ACT.Copy, scale=0.5).then_inc(gate_copied.sem, 1)
                    yield
                    yield
                act.wait_ge(out_stored, i * 32 + 32)
                for t, (_, tn) in enumerate(TILES):
                    act.wait_ge(out_tok.sem, out_tok.at(i, t + 1))
                    A(osb[0:tn, t, :], PS[0:tn, 6 + t % 2, 0:256], ACT.Copy).then_inc(out_copied.sem, 1)
                    yield
                act.wait_ge(out_copied.sem, out_copied.at(i, 3))
                o = out[bass.ds(i, 1), :, :]
                act.dma_start(o[:, 0:2 * TT, :].rearrange("a (t p) d -> p (a t) d", p=TT), osb[:, 0:2, :])\
                    .then_inc(out_stored, 16)
                act.dma_start(o[:, 2 * TT:T, :].rearrange("a p d -> p (a d)"), osb[0:85, 2, :])\
                    .then_inc(out_stored, 16)
                yield

            schedule(act, {"first": first, "att0": att0, "middle": middle, "att1": att1, "last": last})

            act.wait_ge(table_hidden.sem, table_hidden.at(0, 1))
            for s in range(2):
                A(u8sb[s], PS[0:8, 2 * s:2 * s + 2, :].rearrange("p b (g n) -> p (b g) n", n=HID), ACT.Copy)\
                    .then_inc(hidden_copied, 1)
            act.wait_ge(logits_shifted.sem, logits_shifted.at(NB, 1))
            A(prob[:, :, :], rt[:, :, :], ACT.Exp).then_inc(weights_exp.sem, 1)
            with act.Fori(0, ROUNDS) as r:
                act.wait_ge(routed_up.sem, routed_up.at(r, 1))
                A(he[:, :, :], PS[0:TT, 0:4, :].rearrange("p b (n s d) -> p (b n) s d", n=2, s=2)[:, :, 0, :],
                  ACT.Tanh, scale=0.5).then_inc(routed_tanh.sem, 1)

        @block.vector
        def _(dve):
            V = nc.vector
            n_setup = [0]

            def setup(ins):
                n_setup[0] += 1
                ins.then_inc(dve_setup, 1)

            def settled():
                dve.wait_ge(dve_setup, n_setup[0])

            V.memset(img[:, :], 0.0).then_inc(image_read.sem, 1)
            V.memset(coef[:, :], 0.0).then_inc(rec_ready.sem, 1)
            setup(V.memset(ones[:, :], 1.0))
            setup(V.memset(onesb[:, :], 1.0))
            setup(V.memset(ones256[:, :], 1.0 / 256))
            setup(V.memset(ones1024[:, :], 1.0 / 1024))
            setup(V.memset(ones512[:, :], 1.0 / 512))
            setup(V.memset(vx[:, :, :, :], 0.0))
            setup(V.memset(v1x[:, :, :, :], 1.0))
            setup(V.memset(shift0[:, :], 0.0))
            setup(V.memset(shift1[:, :], 0.0))
            setup(V.memset(qk[:, :, T:TP], 0.0))
            setup(V.memset(sq[:, :, T:TP], 0.0))
            setup(V.memset(sq1[:, :, T:TP], 0.0))
            for w in works:
                setup(V.memset(w[1][:, :, T:TP], 0.0))
            setup(V.memset(lg[:, :, :], 0.0))
            settled()
            dve.wait_ge(tables_loaded, 16 * len(loads))
            w8x = [sq[:, 2 * n:2 * n + 2, 0:256] for n in range(4)]
            w8i, w8m, w8f, w8g = w8x[0].bitcast(I32), w8x[1].bitcast(I32), w8x[2], w8x[3]
            for h in range(H):
                setup(V.tensor_scalar(biasq[0:TT, h, :], relq, SLOPES[h], None, ALU.mult))
            setup(V.tensor_copy(pick[:, :, :], ident[:, 0:H].unsqueeze(2).broadcast_to([P, H, P])))
            setup(V.tensor_copy(identb[:, :], ident[:, 0:H]))
            setup(V.tensor_copy(vlast[:, :, 16:32], ident[0:H, 0:H].unsqueeze(2).broadcast_to([H, H, 16])))
            setup(V.tensor_copy(w8i[:, :, :], w8[:, :, :]))
            settled()
            setup(V.tensor_scalar(w8m[:, :, :], w8i[:, :, :], 127, None, ALU.bitwise_and))
            settled()
            setup(V.tensor_scalar(w8i[:, :, :], w8i[:, :, :], 128, 24, ALU.bitwise_and, ALU.logical_shift_left))
            setup(V.tensor_copy(w8f[:, :, :], w8m[:, :, :]))
            settled()
            setup(V.tensor_scalar(w8m[:, :, :], w8m[:, :, :], 20, None, ALU.logical_shift_left))
            setup(V.tensor_scalar(w8f[:, :, :], w8f[:, :, :], 8.0, 2.0 ** -9, ALU.min, ALU.mult))
            settled()
            setup(V.tensor_scalar(w8g[:, :, :], w8m[:, :, :].bitcast(F32), 2.0 ** 120, None, ALU.mult))
            settled()
            setup(V.tensor_tensor(w8f[:, :, :], w8f[:, :, :], w8g[:, :, :], op=ALU.max))
            settled()
            setup(V.tensor_tensor(w8m[:, :, :], w8f[:, :, :].bitcast(I32), w8i[:, :, :], op=ALU.bitwise_or))
            settled()
            setup(V.tensor_copy(w8b[:, :, :], w8m[:, :, :].bitcast(F32)))
            wh = wqk1[:, :, :].rearrange("p c (h d) -> p c h d", d=16)
            setup(V.tensor_reduce(wmean[:, :, :], wh, axis=AX_X, op=ALU.add))
            settled()
            setup(V.tensor_scalar(wmean[:, :, :], wmean[:, :, :], 1.0 / 16, None, ALU.mult))
            settled()
            for c in range(C):
                setup(V.tensor_tensor(wh[:, c], wh[:, c],
                                      wmean[:, c, :].unsqueeze(2).broadcast_to([P, 32, 16]), op=ALU.subtract))
            assert n_setup[0] == SETUP_DVE, n_setup
            settled()
            dve.wait_ge(act_setup, SETUP_ACT)

            n_rough = dve.alloc_register("n_rough")
            dve.reg_mov(n_rough, 0)

            def over(row, n):
                return row.unsqueeze(1).broadcast_to([P, n, T])

            def idle(n):
                for _ in range(n):
                    yield

            def root(ch, y, v, w, x, sums, eps, done):
                ch.step(V.tensor_scalar(v, sums, eps, None, ALU.add))
                ch.step(V.tensor_scalar(y.bitcast(I32), v.bitcast(I32), -0.5, 1597463007.0, ALU.mult, ALU.add))
                for n in range(3):
                    ch.step(V.scalar_tensor_tensor(w, v, -0.5, y, ALU.mult, ALU.mult))
                    ch.step(V.tensor_tensor(x, w, y, op=ALU.mult))
                    y_next = V.scalar_tensor_tensor(y, x, 1.5, y, ALU.add, ALU.mult)
                    if n < 2:
                        ch.step(y_next)
                    else:
                        y_next.then_inc(done.sem, 1)

            def layernorm(nm, i, ch):
                dve.wait_ge(nm.mean_done.sem, nm.mean_done.at(i, 1))
                V.tensor_tensor(nm.cen[:, :, :], nm.src[:, :, :], over(PS[:, nm.mean_bank, 0:T], C),
                                op=ALU.subtract).then_inc(nm.centred.sem, 1)
                yield
                yield
                dve.wait_ge(nm.var_done.sem, nm.var_done.at(i, 1))
                s = [nm.small[:, k, :] for k in range(4)]
                root(ch, *s, PS[0:TT, nm.var_bank, 0:3], 1e-5, nm.root_done)
                yield
                dve.wait_ge(nm.root_wide.sem, nm.root_wide.at(i, 1))
                V.tensor_tensor(nm.xn[:, :, :], nm.cen[:, :, :], over(PS[:, nm.mean_bank, 0:T], C),
                                op=ALU.mult).then_inc(nm.done.sem, 1)
                yield

            def first(i):
                ch = Chain(dve, chain_tok, i)
                dve.wait_ge(bands_ready.sem, bands_ready.at(i, 1))
                for k, (c0, n) in enumerate([(480, 24), (384, 96), (0, 384)]):
                    for o in range(3):
                        ch.step(V.tensor_tensor_reduce(
                            out=dotx[:, 0:n], in0=coef[:, c0:c0 + n], in1=wdet[:, o, c0:c0 + n], scale=1.0,
                            scalar=0.0, op0=ALU.mult, op1=ALU.add, accum_out=dots[:, 3 * k + o:3 * k + o + 1]))
                V.tensor_tensor_reduce(out=dotx[:, 0:8], in0=avg[:, 160:168], in1=wdet[:, 0, 504:512], scale=1.0,
                                       scalar=0.0, op0=ALU.mult, op1=ALU.add, accum_out=dots[:, 9:10])\
                    .then_inc(dots_ready.sem, 1)
                yield
                yield
                dve.wait_ge(logits_summed.sem, logits_summed.at(i, 1))
                ch.step(V.tensor_tensor(z10[:, :], PS[:, 4, 0:10], dscale[:, :], op=ALU.mult))
                ch.step(V.tensor_tensor(z10[:, :], z10[:, :], dbias[:, :], op=ALU.add))
                z9 = z10[:, 0:9].rearrange("p (l o) -> p l o", o=3)
                ch.mark(V.tensor_reduce(mx3[:, :], z9, axis=AX_X, op=ALU.max))
                ch.step(V.tensor_scalar(z10[:, 9:10], z10[:, 9:10], -1.0, None, ALU.mult))
                V.tensor_tensor(z9, z9, mx3[:, :].unsqueeze(2).broadcast_to([P, 3, 3]), op=ALU.subtract)\
                    .then_inc(logits_shifted.sem, 1)
                yield
                dve.wait_ge(weights_exp.sem, weights_exp.at(i, 1))
                e9 = e10[:, 0:9].rearrange("p (l o) -> p l o", o=3)
                ch.mark(V.tensor_reduce(s4[:, 0:3], e9, axis=AX_X, op=ALU.add))
                ch.step(V.tensor_scalar(s4[:, 3:4], e10[:, 9:10], 1.0, None, ALU.add))
                ch.step(V.reciprocal(s4[:, :], s4[:, :]))
                ch.mark(V.tensor_copy(e10[:, 9:10], s4[:, 3:4]))
                ch.step(V.tensor_tensor(e9, e9, s4[:, 0:3].unsqueeze(2).broadcast_to([P, 3, 3]), op=ALU.mult))
                ch.step(V.tensor_tensor(w10[:, 0, :], e10[:, :], wscale[:, :], op=ALU.mult))
                ch.step(V.tensor_scalar(w10[:, 1, :], w10[:, 0, :], -1.0, None, ALU.mult))
                ch.step(V.tensor_scalar(rec[:, 0:8], avg[:, 160:168], w10[:, 0, 9:10], None, ALU.mult))
                for k, (c0, n, rows, at) in enumerate([(480, 8, 1, 0), (384, 32, 2, 8), (0, 128, 4, 40)]):
                    cur = rec[:, at:at + n].rearrange("p (r n) -> p r n", r=rows)

                    def band(s):
                        return coef[:, c0 + s * n:c0 + (s + 1) * n].rearrange("p (r n) -> p r n", r=rows)

                    lo = syn[:, 0, 0:2 * n].rearrange("p (r e n) -> p r e n", r=rows, e=2)
                    hi = syn[:, 1, 0:2 * n].rearrange("p (r e n) -> p r e n", r=rows, e=2)
                    tv = syn[:, 2, 0:n].rearrange("p (r n) -> p r n", r=rows)
                    ch.mark(V.tensor_scalar(tv, band(1), w10[:, 0, 3 * k + 1:3 * k + 2], None, ALU.mult))
                    for s in range(2):
                        ch.mark(V.scalar_tensor_tensor(lo[:, :, s], band(0), w10[:, s, 3 * k:3 * k + 1], cur,
                                                       ALU.mult, ALU.add))
                    ch.sync()
                    for s in range(2):
                        ch.mark(V.scalar_tensor_tensor(hi[:, :, s], band(2), w10[:, s, 3 * k + 2:3 * k + 3], tv,
                                                       ALU.mult, ALU.add))
                    ch.sync()
                    o = rec[:, at + n:at + 5 * n].rearrange("p (n e) -> p n e", e=2)
                    ch.mark(V.tensor_tensor(o[:, :, 0], syn[:, 0, 0:2 * n], syn[:, 1, 0:2 * n], op=ALU.add))
                    odd = V.tensor_tensor(o[:, :, 1], syn[:, 0, 0:2 * n], syn[:, 1, 0:2 * n], op=ALU.subtract)
                    if k < 2:
                        ch.step(odd)
                    else:
                        odd.then_inc(rec_ready.sem, 1)
                    if k:
                        yield
                ch.end()
                yield from idle(2)
                ch = Chain(dve, chain_a, i)
                yield from layernorm(n0, i, ch)
                yield from idle(15)
                dve.wait_ge(qk0_sums.sem, qk0_sums.at(i, 1))
                root(ch, *[qks[:, k, :] for k in range(4)], PS[0:TT, 7, 0:6], 1e-6, qk0_root)
                yield
                dve.wait_ge(qk0_wide.sem, qk0_wide.at(i, 1))
                for n in range(12):
                    V.scalar_tensor_tensor(qk[:, n, 0:T], qk[:, n, 0:T], qkw0[:, n:n + 1],
                                           PS[:, 4 + n // 8, 0:T], ALU.mult, ALU.mult)\
                        .then_inc(qk0_ready.sem, 1)
                    if n % 4 == 3:
                        yield
                for h in range(H):
                    wait_next(dve, n_rough, rough0)
                    for t, ((_, tn), (_, kn), kc) in enumerate(zip(TILES, KR0, KC0)):
                        o = PS[0:tn, 4 + h % 4, kc:kc + kn]
                        m = V.tensor_tensor_reduce(out=o, in0=o, in1=biasq[0:tn, h, kc:kc + kn], scale=1.0,
                                                   scalar=-3e38, op0=ALU.add, op1=ALU.max,
                                                   accum_out=mtok[0:tn, t, h:h + 1])
                    m.then_inc(rowmax0.sem, 1)
                    if h % 2:
                        yield
                ch.end()
                yield
                yield

            def att0(i):
                def bias(h):
                    dve.wait_ge(scores0.sem, scores0.at(i, h + 1))
                    if h >= 2:
                        dve.wait_ge(probs0.sem, probs0.at(i, h - 1))
                    V.scalar_tensor_tensor(pre[:, h % 2, :], relm[:, :], SLOPES[h], PS[0:TT, h % 2, 0:W0],
                                           ALU.mult, ALU.add).then_inc(biased0.sem, 1)

                def scale(j):
                    dve.wait_ge(rsum_wide.sem, rsum_wide.at(i, j + 1))
                    V.tensor_tensor(y0[:, j, :], y0[:, j, :], PS[:, j % 2, 0:T], op=ALU.mult)\
                        .then_inc(y0_ready.sem, 1)

                bias(0)
                bias(1)
                yield
                for h in range(2, 18):
                    if h < H:
                        bias(h)
                    yield
                dve.wait_ge(sums0.sem, sums0.at(i, 4))
                dve.wait_ge(y0_copied.sem, y0_copied.at(i, 8))
                V.reciprocal(rsum[:, :], PS[:, 3, 0:T]).then_inc(rsum_ready.sem, 1)
                yield
                for j in range(8):
                    scale(j)
                    yield
                dve.wait_ge(wo0_done.sem, wo0_done.at(i, 1))
                V.tensor_tensor(h1[:, :, :], h0[:, :, :], PS[:, 2:4, 0:T], op=ALU.add).then_inc(n1.src_ready.sem, 1)
                yield
                yield

            def middle(i):
                ch = Chain(dve, chain_b, i)
                yield from layernorm(n1, i, ch)
                dve.wait_ge(absmax_done.sem, absmax_done.at(i, 1))
                ch.step(V.tensor_tensor(fs[:, 0, :], amax[:, 0, :], amax[:, 1, :], op=ALU.max))
                ch.step(V.tensor_scalar(fs[:, 1, :], fs[:, 0, :], 1e-12, 1.0 / 448.0, ALU.max, ALU.mult))
                ch.mark(V.tensor_scalar(fs[:, 3, :], fs[:, 1, :], w8s[:, 0:1], None, ALU.mult))
                ch.step(V.reciprocal(fs[:, 2, :], fs[:, 1, :]))
                ch.step(V.tensor_tensor(fy[:, :, :], n1.xn[:, :, :], over(fs[:, 2, :], C), op=ALU.mult))
                yield
                ch.step(V.tensor_scalar(fm[:, :, :].bitcast(I32), fy[:, :, :].bitcast(I32), 0x7F800000, None,
                                        ALU.bitwise_and))
                ch.step(V.tensor_scalar(fm[:, :, :], fm[:, :, :], 2.0 ** -6, 1.5 * 2.0 ** 20, ALU.max, ALU.mult))
                ch.step(V.tensor_tensor(fy[:, :, :], fy[:, :, :], fm[:, :, :], op=ALU.add))
                V.tensor_tensor(fq[:, :, :], fy[:, :, :], fm[:, :, :], op=ALU.subtract).then_inc(fq_ready.sem, 1)
                yield
                dve.wait_ge(ffn0_done.sem, ffn0_done.at(i, 1))
                ch.step(V.tensor_tensor(fy[:, :, :], PS[:, 4:6, 0:T], over(fs[:, 3, :], C), op=ALU.mult))
                ch.mark(V.scalar_tensor_tensor(h2[:, 0, :], fy[:, 0, :], b8[:, 0:1], h1[:, 0, :], ALU.add, ALU.add))
                V.scalar_tensor_tensor(h2[:, 1, :], fy[:, 1, :], b8[:, 1:2], h1[:, 1, :], ALU.add, ALU.add)\
                    .then_inc(n2.src_ready.sem, 1)
                yield

                yield from layernorm(n2, i, ch)
                yield from idle(5)
                dve.wait_ge(v1_proj.sem, v1_proj.at(i, 3))
                V.tensor_tensor(vlast[:, :, 0:16], PS[0:H, 4, 0:256].rearrange("p (h d) -> p h d", h=H),
                                ident[0:H, 0:H].unsqueeze(2).broadcast_to([H, H, 16]), op=ALU.mult)\
                    .then_inc(vlast_ready.sem, 1)
                dve.wait_ge(qk1_var.sem, qk1_var.at(i, 1))
                root(ch, *[root1[:, k, :, :] for k in range(4)],
                     PS[0:TT, 5, 0:96].rearrange("p (t n) -> p t n", t=3), 1e-6, qk1_root)
                yield
                dve.wait_ge(root1_turned.sem, root1_turned.at(i, 1))
                V.tensor_copy(root32[:, :], PS[0:32, 4, 0:T]).then_inc(root1_copied.sem, 1)
                yield
                for n in range(4):
                    dve.wait_ge(qk1_wide.sem, qk1_wide.at(i, n + 1))
                    V.tensor_tensor(u1[:, n, :], u1[:, n, :], PS[:, 4 + n % 2, 0:T], op=ALU.mult)\
                        .then_inc(qk1_normed.sem, 1)
                    yield
                for n in range(4):
                    dve.wait_ge(qk1_turned.sem, qk1_turned.at(i, n + 1))
                    V.tensor_tensor(rsin[:, n, :], PS[:, 4 + n % 2, 0:T], sinT[:, :], op=ALU.mult)\
                        .then_inc(sin_done.sem, 1)
                    ch.step(V.tensor_tensor(qr[:, n, :], u1[:, n, :], cosT[:, :], op=ALU.mult))
                    dve.wait_ge(sin_done.sem, sin_done.at(i, n + 1))
                    V.tensor_tensor(qr[:, n, :], qr[:, n, :], rsin[:, n, :], op=ALU.add).then_inc(rope_done.sem, 1)
                    yield
                dve.wait_ge(rope_done.sem, rope_done.at(i, 4))
                ch.mark(V.tensor_tensor(qlast[:, :, :], headmask[:, :, :],
                                        qr[:, 0:2, 256:257].broadcast_to([P, C, H]), op=ALU.mult))
                V.tensor_tensor(klast[:, :, :], headmask[:, :, :], qr[:, 2:4, 256:257].broadcast_to([P, C, H]),
                                op=ALU.mult).then_inc(last_ready.sem, 1)
                yield
                dve.wait_ge(rough_last.sem, rough_last.at(i, 1))
                V.tensor_reduce(mlast[:, :], PS[0:H, 4, 0:T], axis=AX_X, op=ALU.max).then_inc(last_max.sem, 1)
                dve.wait_ge(rough_last.sem, rough_last.at(i, 2))
                V.tensor_copy(mcol1[:, :, :], PS[:, 5, 0:2 * H].rearrange("p (t h) -> p t h", t=2))\
                    .then_inc(last_max.sem, 1)
                yield
                for h in range(H):
                    dve.wait_ge(rough1.sem, rough1.at(i, h + 1))
                    V.tensor_reduce(mtok1[:, :, h:h + 1], PS[:, 4 + h % 2, :].rearrange("p (t n) -> p t n", t=2),
                                    axis=AX_X, op=ALU.max).then_inc(rowmax1.sem, 1)
                    if h % 2:
                        yield
                dve.wait_ge(rowmax1.sem, rowmax1.at(i, H))
                V.tensor_tensor(mtok1[:, :, :], mtok1[:, :, :], mcol1[:, :, :], op=ALU.max)\
                    .then_inc(max1_ready.sem, 1)
                V.tensor_scalar(shift1[0:H, 256:257], mlast[:, :], -1.0, None, ALU.mult)\
                    .then_inc(shift1_ready.sem, 1)
                dve.wait_ge(shift1_ready.sem, shift1_ready.at(i, 2))
                V.tensor_tensor(slast[:, :], identb[:, :], shift1[:, 256:257].broadcast_to([P, H]), op=ALU.mult)\
                    .then_inc(slast_ready.sem, 1)
                yield
                yield
                yield
                ch.end()

            def att1(i):
                def scale(n):
                    dve.wait_ge(rz_wide.sem, rz_wide.at(i, n + 1))
                    V.tensor_tensor(zz[:, n, :], zz[:, n, :], PS[:, n % 2, 0:T], op=ALU.mult)\
                        .then_inc(y1_ready.sem, 1)

                yield from idle(17)
                dve.wait_ge(sums1.sem, sums1.at(i, 1))
                V.reciprocal(rz[:, :], PS[0:H, 0, 0:T]).then_inc(rz_ready.sem, 1)
                yield
                for n in range(4):
                    scale(n)
                    yield
                dve.wait_ge(proj1_done.sem, proj1_done.at(i, 1))
                V.tensor_tensor(h3[:, :, :], h2[:, :, :], PS[:, 2:4, 0:T], op=ALU.add).then_inc(n3.src_ready.sem, 1)
                yield
                yield

            def last(i):
                ch = Chain(dve, chain_c, i)
                yield from layernorm(n3, i, ch)
                dve.wait_ge(gates.sem, gates.at(i, 1))
                V.tensor_copy(lg[:, bass.ds(i * 3, 2), :], PS[0:TT, 7, 0:2 * NE].rearrange("p (t e) -> p t e", e=NE))\
                    .then_inc(gates_kept.sem, 1)
                V.tensor_copy(lg[0:85, bass.ds(i * 3 + 2, 1), :],
                              PS[0:85, 7, 2 * NE:3 * NE].rearrange("p (t e) -> p t e", e=NE))\
                    .then_inc(gates_kept.sem, 1)
                yield
                for n in range(2):
                    dve.wait_ge(gate_copied.sem, gate_copied.at(i, n + 1))
                    ch.step(V.scalar_tensor_tensor(gate_in[:, n, :], half_t[:, n, 0:T], 1.0, gate_in[:, n, :],
                                                   ALU.add, ALU.mult))
                    yield
                    dve.wait_ge(value_done.sem, value_done.at(i, n + 1))
                    V.tensor_tensor(hh[:, n, :], gate_in[:, n, :], PS[:, 7, 0:T], op=ALU.mult)\
                        .then_inc(hh_ready.sem, 1)
                    yield
                ch.end()
                yield from idle(4)

            schedule(dve, {"first": first, "att0": att0, "middle": middle, "att1": att1, "last": last})

            steps = [0]

            def mark(ins):
                steps[0] += 1
                ins.then_inc(tail_chain, 1)

            def step(ins):
                mark(ins)
                dve.wait_ge(tail_chain, steps[0])

            def per_expert(x):
                return x.unsqueeze(2).broadcast_to([TT, NCOL, NE])

            dve.wait_ge(gates_kept.sem, gates_kept.at(NB - 1, 2))
            step(V.tensor_reduce(r1[:, :], lg[:, :, :], axis=AX_X, op=ALU.max))
            V.tensor_tensor(rt[:, :, :], lg[:, :, :], per_expert(r1[:, :]), op=ALU.subtract)\
                .then_inc(logits_shifted.sem, 1)
            dve.wait_ge(weights_exp.sem, weights_exp.at(NB, 1))
            step(V.tensor_reduce(r1[:, :], prob[:, :, :], axis=AX_X, op=ALU.add))
            step(V.reciprocal(r1[:, :], r1[:, :]))
            step(V.tensor_tensor(prob[:, :, :], prob[:, :, :], per_expert(r1[:, :]), op=ALU.mult))
            step(V.tensor_tensor(rt[:, :, :], prob[:, :, :], ebias[0:TT, :].unsqueeze(1)
                                 .broadcast_to([TT, NCOL, NE]), op=ALU.add))
            s2 = rt[:, :, :].rearrange("p n (g e) -> p n g e", e=2)
            gs, beat, tmp = g4[:, 0], g4[:, 1], g4[:, 2]
            step(V.tensor_tensor(gs, s2[:, :, :, 0], s2[:, :, :, 1], op=ALU.add))
            step(V.memset(beat, 0.0))

            def rank(score, count, scratch, width):
                for k in range(width):
                    for lo, hi, op in ((0, k, ALU.is_gt), (k + 1, width, ALU.is_ge)):
                        if lo < hi:
                            rival = score[:, :, k:k + 1].broadcast_to([TT, NCOL, hi - lo])
                            step(V.tensor_tensor(scratch[:, :, lo:hi], rival, score[:, :, lo:hi], op=op))
                            step(V.tensor_tensor(count[:, :, lo:hi], count[:, :, lo:hi], scratch[:, :, lo:hi],
                                                 op=ALU.add))

            rank(gs, beat, tmp, 4)
            step(V.tensor_scalar(tmp, beat, 1.5, None, ALU.is_lt))
            step(V.tensor_scalar(beat, tmp, -MASKED, MASKED, ALU.mult, ALU.add))
            for e in range(2):
                step(V.tensor_tensor(s2[:, :, :, e], s2[:, :, :, e], tmp, op=ALU.mult))
                step(V.tensor_tensor(s2[:, :, :, e], s2[:, :, :, e], beat, op=ALU.add))
            step(V.memset(rk[:, :, :], 0.0))
            scratch = ge[:, 0:NCOL, :]
            rank(rt, rk, scratch, NE)
            for s in range(2):
                step(V.tensor_scalar(onehot[:, :, s, :], rk[:, :, :], float(s), None, ALU.is_equal))
                step(V.tensor_tensor(scratch, onehot[:, :, s, :], prob[:, :, :], op=ALU.mult))
                step(V.tensor_reduce(weight[:, :, s:s + 1], scratch, axis=AX_X, op=ALU.add))
                step(V.tensor_tensor(onehot[:, :, s, :], onehot[:, :, s, :], per_expert(valid[:, :]), op=ALU.mult))
            step(V.tensor_tensor(scratch, onehot[:, :, 0, :], onehot[:, :, 1, :], op=ALU.add))
            V.tensor_reduce(cnt[0:TT, :], scratch.rearrange("p n e -> p e n"), axis=AX_X, op=ALU.add)\
                .then_inc(counts_ready, 1)
            dve.wait_ge(counts_summed, 1)
            step(V.tensor_copy(offs[:, :], PS[0:TT, 4, 0:NE]))
            for e in range(1, NE):
                step(V.tensor_tensor(offs[:, e:e + 1], offs[:, e:e + 1], offs[:, e - 1:e], op=ALU.add))
            flat = pos[:, :, :].rearrange("p n s -> p (n s)").unsqueeze(2).broadcast_to([TT, NCOL * 2, NE])
            step(V.tensor_tensor(ge[:, :, :], flat, offs[:, :].unsqueeze(1).broadcast_to([TT, NCOL * 2, NE]),
                                 op=ALU.is_lt))
            gr = group[:, :, :, :].rearrange("p n s g -> p (n s) g")
            step(V.tensor_copy(gr[:, :, 0:1], ge[:, :, 0:1]))
            step(V.tensor_tensor(gr[:, :, 1:NE], ge[:, :, 1:NE], ge[:, :, 0:NE - 1], op=ALU.subtract))

            V.memset(acct[:, :], 0.0).then_inc(acc_copied, 1)

            n_steps = steps[0]
            ONES = onehot[:, :, :, :].rearrange("p n s e -> p (n s) e")
            WGT = weight[:, :, :].rearrange("p n s -> p (n s)")
            with dve.Fori(0, ROUNDS) as r:
                tail = n_steps
                o4 = oh[:, :, :].rearrange("p n (e g) -> p n e g", g=NE)
                at = bass.ds(r * 8, 8)
                V.tensor_tensor(o4, ONES[:, at, :].unsqueeze(3).broadcast_to([TT, 8, NE, NE]),
                                gr[:, at, :].unsqueeze(2).broadcast_to([TT, 8, NE, NE]), op=ALU.mult)\
                    .then_inc(tail_chain, 1)
                dve.wait_ge(tail_chain, r * 2 + (tail + 1))
                V.tensor_tensor(ohw[:, :, :], oh[:, :, :], WGT[:, at].unsqueeze(2).broadcast_to([TT, 8, 64]),
                                op=ALU.mult).then_inc(onehots_ready.sem, 1)
                dve.wait_ge(onehots_turned.sem, onehots_turned.at(r, 1))
                V.tensor_copy(oht[:, :].rearrange("p (b n) -> p b n", b=2), PS[0:64, 4:6, 0:4 * TT])\
                    .then_inc(turned_copied.sem, 1)
                dve.wait_ge(routed_tanh.sem, routed_tanh.at(r, 1))
                up = PS[0:TT, 0:4, :].rearrange("p b (n s d) -> p (b n) s d", n=2, s=2)
                V.scalar_tensor_tensor(he[:, :, :], he[:, :, :], 1.0, up[:, :, 0, :], ALU.add, ALU.mult)\
                    .then_inc(tail_chain, 1)
                dve.wait_ge(tail_chain, r * 2 + (tail + 2))
                V.scalar_tensor_tensor(hs[:, :, :], he[:, :, :], 0.5, up[:, :, 1, :], ALU.mult, ALU.mult)\
                    .then_inc(routed_h.sem, 1)
                dve.wait_ge(routed_added.sem, routed_added.at(r, 1))
                dve.wait_ge(acc_copied, r + 1)
                V.tensor_tensor(acct[:, :], acct[:, :], PS[0:64, 6, 0:HID], op=ALU.add).then_inc(acc_copied, 1)
            dve.wait_ge(acc_turned, 1)
            V.tensor_copy(accT[:, :], PS[:, 4, 0:64]).then_inc(accT_ready, 1)
            dve.wait_ge(routed_out, 1)
            dve.wait_ge(rows_loaded, 16)
            V.tensor_tensor(r8, r8, PS[0:8, 5, 0:256], op=ALU.add).then_inc(rows_ready, 1)


def tables():
    k = np.arange(P)
    t = {"ident": np.eye(P, dtype=np.float32)}
    t["block8"] = (k[:, None] // 16 == np.arange(8)[None, :]).astype(np.float32) / 16
    hd = np.arange(H)
    t["headmask"] = (hd == 8 * np.arange(C)[None, :, None] + k[:, None, None] // 16).astype(np.float32)
    col = np.arange(32)
    sel = (col[None, :] == np.arange(4)[:, None]) | (col[None, :] >= 4)
    t["sumsel"] = np.tile(sel.astype(np.float32)[None], (P, 1, 1))
    head = 2 * np.arange(8)[:, None] + (k[None, :] >= 64)
    t["sumback"] = (k[:, None, None] == 32 * (head % 4) + head // 4).astype(np.float32)
    own = hd[None, None, :] == 4 * np.arange(4)[None, :, None] + k[:, None, None] // 32
    t["collect"] = (own & (k[:, None, None] % 32 == 16)).astype(np.float32)
    tile_head = 8 * np.arange(4)[None, :, None] + k[None, None, :] // 16
    t["expand"] = (np.arange(32)[:, None, None] == tile_head).astype(np.float32)
    t["spread"] = own.transpose(2, 1, 0).astype(np.float32)
    rot = np.zeros((P, P), np.float32)
    for m in range(P):
        if m % 16 < 8:
            rot[m + 8, m] = -1.0
        else:
            rot[m - 8, m] = 1.0
    t["rotate"] = rot
    freq = np.float32(1.0) / np.float32(10000.0) ** (np.arange(8, dtype=np.float32) / np.float32(8))
    ang = (np.arange(T, dtype=np.float32)[None, :] * freq[k % 8][:, None]).astype(np.float32)
    t["cosT"], t["sinT"] = np.cos(ang).astype(np.float32), np.sin(ang).astype(np.float32)
    t["parity"] = np.stack([(k // 16) % 2 == 0, (k // 16) % 2 == 1], 1).astype(np.float32)
    relm = np.full((TT, W0), MASKED, np.float32)
    for n, ((q0, qn), c0) in enumerate(zip(QR0, QC0)):
        key, q = n * TT + np.arange(TT)[:, None], q0 + np.arange(qn)[None, :]
        ok = (key <= q) & (key >= q - WINDOW) & (key < T)
        relm[:, c0:c0 + qn] = np.where(ok, (key - q).astype(np.float32), MASKED)
    t["relm"] = relm
    relq = np.full((TT, W2), MASKED, np.float32)
    for n, ((k0, kn), c0) in enumerate(zip(KR0, KC0)):
        q, key = n * TT + np.arange(TT)[:, None], k0 + np.arange(kn)[None, :]
        ok = (key <= q) & (key >= q - WINDOW)
        relq[:, c0:c0 + kn] = np.where(ok, (key - q).astype(np.float32), MASKED)
    t["relq"] = relq
    p, col = np.arange(TT)[:, None], np.arange(NCOL)[None, :]
    token = (NB - 1 - col // 3) * T + (col % 3) * TT + p
    t["pos"] = np.stack([2 * token, 2 * token + 1], -1).astype(np.float32)
    t["valid"] = ((col % 3) * TT + p < T).astype(np.float32)
    level = np.array([8, 8, 8, 4, 4, 4, 2, 2, 2, 8], np.float32)
    t["dscale"] = np.tile(1 / level, (P, 1)).astype(np.float32)
    t["wscale"] = np.tile(1 / level ** 2, (P, 1)).astype(np.float32)
    return t


def blocks(x, rows, cols):
    lead = x.shape[:-2]
    n = len(lead)
    y = x.reshape(*lead, 32, rows, 4, cols)
    return y.transpose(*range(n), n + 2, n, n + 1, n + 3).reshape(*lead, P, rows * cols)


def halves(w):
    return w.reshape(C, P, -1).transpose(1, 0, 2)


def layout(d):
    r = {}
    r["x"] = blocks(d["x"][::-1, :, :, 0], 8, 64)
    r["wq0"] = halves(d["L0_attn_wq"].T)
    wk = d["L0_attn_wk"].T.reshape(256, KV, 1, 64)
    r["wk0"] = halves(np.repeat(wk, 2, axis=2).reshape(256, 512))
    r["wv0"] = halves(d["L0_attn_wv"].T)
    r["wo0"] = d["L0_attn_wo"].T.reshape(8, P, 256).transpose(1, 0, 2)
    kn = np.repeat(d["L0_attn_k_norm_w"].reshape(KV, 1, 64), 2, axis=1).reshape(KV, P)
    r["qkw0"] = np.concatenate([d["L0_attn_q_norm_w"].reshape(8, P), kn]).T
    r["w8"] = halves(d["L0_ffn_weight"].view(np.uint8).T)
    r["w8s"] = np.broadcast_to(d["L0_ffn_weight_scale"].reshape(1, 1), (P, 1))
    r["b8"] = d["L0_ffn_bias"].reshape(C, P).T
    r["wqk1"] = halves(d["L1_attn_w_qkv"][0:512].T)
    r["wv1"] = halves(d["L1_attn_w_qkv"][512:768].T)
    wp = np.zeros((H, 32, 256), np.float32)
    wp[:, 0:16] = d["L1_attn_w_proj"].T.reshape(H, 16, 256)
    wp[0, 16] = d["L1_attn_b_proj"]
    r["wp1"] = wp.reshape(4, P, 256).transpose(1, 0, 2)
    r["gb1"] = np.stack([np.tile(d["L1_attn_" + n], 8) for n in ("q_gamma", "k_gamma", "q_beta", "k_beta")], 1)
    r["wg"] = halves(d["L1_ffn_w_gate"].T)
    r["sw13"] = halves(np.concatenate([d["L1_ffn_sw1"].T, d["L1_ffn_sw3"].T], 1))
    r["sw2"] = halves(d["L1_ffn_sw2"].T)
    for n, name in (("ew1", "L1_ffn_w1"), ("ew3", "L1_ffn_w3")):
        r[n] = halves(d[name].transpose(1, 0, 2).reshape(256, NE * HID))
    r["ew2"] = d["L1_ffn_w2"].transpose(1, 0, 2)
    r["ebias"] = np.tile(d["L1_ffn_expert_bias"][None], (P, 1))
    r["clst"] = d["cls_tok"].reshape(C, P).T
    parts = []
    for name, n in (("L0_tok_Wd3", 128), ("L0_tok_Wd2", 64), ("L0_tok_Wd1", 32)):
        w = blocks(d[name].T.reshape(3, 3, n, n), n // 32, n // 4)
        parts.append(w.transpose(2, 0, 1, 3).reshape(P, 3, -1))
    wa = blocks(d["L0_tok_Wa"].reshape(32, 32), 1, 8)
    parts.append(np.broadcast_to(wa[:, None, :], (P, 3, 8)))
    r["wdet"] = np.concatenate(parts, 2)
    bias = np.concatenate([d["L0_tok_" + n] for n in ("bd1", "bd2", "bd3", "ba")])
    r["dbias"] = np.tile(bias[None], (P, 1))
    return r


def kernel(**inputs):
    import concourse.bacc as bacc
    from concourse.bass_utils import run_bass_kernel_spmd

    nc = bacc.Bacc("TRN2", target_bir_lowering=False, num_devices=1)
    data = layout({k: np.asarray(v) for k, v in inputs.items()})
    data.update(tables())
    arrays = {f"in_{k}": np.ascontiguousarray(v) for k, v in data.items()}
    aps = {k: nc.dram_tensor(f"in_{k}", arrays[f"in_{k}"].shape, mybir.dt.from_np(arrays[f"in_{k}"].dtype),
                             kind="ExternalInput").ap() for k in data}
    out = nc.dram_tensor("out_tokens", (NB, T, 256), F32, kind="ExternalOutput").ap()
    build_tower(nc, aps, out)
    result = run_bass_kernel_spmd(nc, [arrays], core_ids=[0])
    return result.results[0]["out_tokens"][::-1]
```

```python
from contextlib import ExitStack
from itertools import chain

import numpy as np

import concourse.bass as bass
from concourse import mybir

ALU = mybir.AluOpType
ACT = mybir.ActivationFunctionType
F32 = mybir.dt.float32
BF16 = mybir.dt.bfloat16
U8 = mybir.dt.uint8
I32 = mybir.dt.int32
AX_X = mybir.AxisListType.X
ABSMAX = bass.bass_isa.ReduceOp.absmax

P = 128
NB = 32
T = 257
TP = T + 1
C = 2
TT = 86
TILES = [(0, 86), (86, 86), (172, 85)]
H = 16
KV = 4
WINDOW = 128
NE = 8
HID = 128
NCOL = NB * 3

QR0 = [(0, 214), (86, 171), (172, 85)]
QC0 = [0, 214, 385]
W0 = 470
KR0 = [(0, 86), (0, 172), (44, 213)]
KC0 = [0, 86, 258]
W2 = 471
MASKED = -1e30
SLOPES = [float(np.float32(np.float32(2.0 ** (-8.0 / H)) ** np.float32(n + 1))) for n in range(H)]


class Signal:

    def __init__(self, sem, per):
        self.sem, self.per = sem, per

    def at(self, i, k):
        return i * self.per + k


class Chain:

    def __init__(self, eng, signal, i):
        self.eng, self.sem, self.per, self.i, self.n = eng, signal.sem, signal.per, i, 0

    def mark(self, ins):
        self.n += 1
        ins.then_inc(self.sem, 1)

    def sync(self):
        self.eng.wait_ge(self.sem, self.i * self.per + self.n)

    def step(self, ins):
        self.mark(ins)
        self.sync()

    def end(self):
        assert self.n == self.per, (self.n, self.per)


SPAN_A, SPAN_B, SPAN_C = 0.97, 1.0, 0.8
STRETCHES = {"token": 20, "first": 34, "att0": 44, "middle": 45, "att1": 40, "last": 14}


def stretches(name, part):
    n = 0
    for _ in part:
        n += 1
        yield
    assert n == STRETCHES[name], (name, n)


def weave(main, *sides):
    name, part = main
    rest = []
    for span, parts in sides:
        count = sum(STRETCHES[n] for n, _ in parts)
        rest.append([count / (span * STRETCHES[name]), 0.0, chain.from_iterable(stretches(n, p) for n, p in parts)])
    for _ in stretches(name, part):
        for side in rest:
            side[1] += side[0]
            while side[1] >= 1:
                side[1] -= 1
                next(side[2], None)
    for side in rest:
        for _ in side[2]:
            pass


def schedule(eng, parts):
    def part(name, i):
        return name, parts[name](i)

    def a_round(i):
        weave(part("att0", i), (SPAN_B, [part("middle", i - 1)]),
              (SPAN_C, [part("last", i - 2), part("token", i + 1)]))
        weave(part("att1", i - 1), (SPAN_A, [part("first", i + 1)]))

    weave(part("token", 0))
    weave(part("first", 0))
    weave(part("att0", 0), (1.0, [part("token", 1)]))
    weave(part("first", 1))
    weave(part("att0", 1), (SPAN_B, [part("middle", 0)]), (SPAN_C, [part("token", 2)]))
    weave(part("att1", 0), (SPAN_A, [part("first", 2)]))
    with eng.Fori(2, NB - 2) as i:
        a_round(i)
    a_round(NB - 2)
    weave(part("att0", NB - 1), (SPAN_B, [part("middle", NB - 2)]), (SPAN_C, [part("last", NB - 3)]))
    weave(part("att1", NB - 2))
    weave(part("middle", NB - 1), (0.5, [part("last", NB - 2)]))
    weave(part("att1", NB - 1))
    weave(part("last", NB - 1))


class Norm:

    def __init__(self, n, src, work, banks, signal):
        self.src, (self.cen, self.csq, self.small, self.xn) = src, work
        self.mean_bank, self.var_bank = banks
        self.src_ready = signal(f"h{n}_ready", 1)
        self.mean_done = signal(f"mean{n}_done", 1)
        self.centred = signal(f"centred{n}", 1)
        self.squared = signal(f"squared{n}", 1)
        self.root_done = signal(f"root{n}_done", 1)
        self.root_wide = signal(f"root{n}_wide", 1)
        self.done = signal(f"norm{n}_done", 1)


def build_tower(nc, a, out):
    with ExitStack() as ctx:
        def sb(name, shape, dt=F32):
            return ctx.enter_context(nc.sbuf_tensor("t_" + name, shape, dt))

        def sem(name):
            return ctx.enter_context(nc.semaphore(name))

        def signal(name, per):
            return Signal(sem(name), per)

        PS = ctx.enter_context(nc.psum_tensor("PS", [P, 8, 512], F32))

        loads = []

        def table(name, shape, dt=F32):
            t = sb(name, shape, dt)
            loads.append((t, a[name]))
            return t

        wq0 = table("wq0", [P, C, 1024])
        wk0 = table("wk0", [P, C, 256])
        wv0 = table("wv0", [P, C, 256])
        wo0 = table("wo0", [P, 8, 256])
        qkw0 = table("qkw0", [P, 12])
        w8 = table("w8", [P, C, 256], U8)
        w8s = table("w8s", [P, 1])
        b8 = table("b8", [P, C])
        wqk1 = table("wqk1", [P, C, 512])
        wv1 = table("wv1", [P, C, 256])
        wp1 = table("wp1", [P, 4, 256])
        gb1 = table("gb1", [P, 4])
        wg = table("wg", [P, C, NE])
        sw13 = table("sw13", [P, C, 512])
        sw2 = table("sw2", [P, C, 256])
        ebias = table("ebias", [P, NE])
        clst = table("clst", [P, C])
        wdet = table("wdet", [P, 3, 512])
        dbias = table("dbias", [P, 10])
        dscale = table("dscale", [P, 10])
        wscale = table("wscale", [P, 10])
        ident = table("ident", [P, P])
        block8 = table("block8", [P, 8])
        headmask = table("headmask", [P, C, H])
        collect = table("collect", [P, 4, H])
        spread = table("spread", [H, 4, P])
        sumsel = table("sumsel", [P, 4, 32])
        sumback = table("sumback", [P, 8, P])
        expand = table("expand", [32, 4, P])
        rotate = table("rotate", [P, P])
        cosT = table("cosT", [P, T])
        sinT = table("sinT", [P, T])
        relm = table("relm", [TT, W0])
        biasf = sb("biasq", [P, H * W2], BF16)
        biasq = biasf[:, :].rearrange("p (h n) -> p h n", h=H)
        pos = table("pos", [TT, NCOL, 2])
        valid = table("valid", [TT, NCOL])

        ones = sb("ones", [P, P])
        ones256 = sb("ones256", [P, P])
        ones1024 = sb("ones1024", [P, 1])
        onesb = sb("onesb", [P, P], BF16)
        identb = sb("identb", [P, H], BF16)
        w8b = sb("w8b", [P, C, 256], BF16)
        wmean = sb("wmean", [P, C, 32])

        img = sb("img", [P, 512])
        lohi = sb("lohi", [P, 2, 256])
        coef = sb("coef", [P, 504])
        avg = sb("avg", [P, 128 + 32 + 8])
        dots = sb("dots", [P, 10])
        z10 = sb("z10", [P, 10])
        mx3 = sb("mx3", [P, 3])
        e10 = sb("e10", [P, 10])
        s4 = sb("s4", [P, 4])
        w10 = sb("w10", [P, 10])
        rec = sb("rec", [P, 8 + 32 + 128 + 512])
        relq = rec[0:TT, 0:W2]
        loads.append((relq, a["relq"]))
        dotx = rec[:, 0:384]
        h0 = sb("h0", [P, C, T])
        h1 = sb("h1", [P, C, T])
        h2 = sb("h2", [P, C, T])
        h3 = sb("h3", [P, C, T])

        def work(name):
            return (sb("cen" + name, [P, C, T]), sb("csq" + name, [P, C, TP]), sb("small" + name, [TT, 4, 3]),
                    sb("xn" + name, [P, C, T]))

        works = [work(name) for name in "ab"]
        norms = [Norm(0, h0, works[0], (7, 4), signal), Norm(1, h1, works[1], (4, 5), signal),
                 Norm(2, h2, works[1], (4, 5), signal), Norm(3, h3, works[0], (6, 7), signal)]
        n0, n1, n2, n3 = norms
        qk = sb("qk", [P, 16, TP])
        sq = sb("sq", [P, 12, TP])
        syn = [t[:, c, 0:256] for t in (works[0][0], works[0][3]) for c in range(C)]
        qks = sb("qks", [TT, 4, 6])
        qkb = sb("qkb", [P, 16, T], BF16)
        vx = sb("vx", [TT, 3, KV, 64])
        mtok = sb("mtok", [TT, 3, H])
        shift0 = sb("shift0", [P, T], BF16)
        att = sb("att", [P, 8 * 2 * 256])
        pre = att[0:TT, 0:2 * W0].rearrange("p (b n) -> p b n", b=2)
        pr0 = att[0:TT, 2 * W0:8 * W0].rearrange("p (b n) -> p b n", b=6)
        pr1 = att[:, :].rearrange("p (h t n) -> p h t n", h=8, t=2)
        y0 = sb("y0", [P, 8, T])
        zz = y0[:, 0:4, :]
        rsum = sb("rsum", [P, T])
        fs, fy, fm = sq[:, 0:4, 0:T], sq[:, 4:6, 0:T], sq[:, 6:8, 0:T]
        fq = qkb[:, 2:4, :]
        u1 = sb("u1", [P, 4, T])
        amax = u1[:, 0:2, :]
        sq1 = sb("sq1", [P, 4, TP])
        rsin = sq[:, 8:12, 0:T]
        root32 = sb("root32", [32, T])
        root1 = sb("root1", [TT, 4, 3, 32])
        qr = sb("qr", [P, 4, T])
        km = sb("km", [P, 4, 256])
        q1b = qkb[:, 0:2, :]
        kmb = qkb[:, 4:8, 0:256]
        v1x = sb("v1x", [P, 2, H, 32])
        vlast = sb("vlast", [H, H, 32])
        qlast = sb("qlast", [P, C, H])
        klast = sb("klast", [P, C, H])
        mlast = sb("mlast", [H, 1])
        mcol1 = sb("mcol1", [P, 2, H])
        mtok1 = sb("mtok1", [P, 2, H])
        shift1 = sb("shift1", [P, T], BF16)
        slast = sb("slast", [P, H], BF16)
        pklast = sb("pklast", [H, T])
        pqlast = sb("pqlast", [P, 2, H])
        rz = rsum[0:H, :]
        half_t = n3.csq
        gate_in = rec[:, 0:C * T].rearrange("p (c t) -> p c t", c=C)
        hh = n3.cen
        osb = sb("osb", [TT, 3, 256])
        lg = sb("lg", [TT, NCOL, NE])

        tables_loaded = sem("tables_loaded")
        dve_setup = sem("dve_setup")
        act_setup = sem("act_setup")
        chain_tok = signal("chain_tok", 18)
        chain_a = signal("chain_a", 20)
        chain_b = signal("chain_b", 45)
        chain_c = signal("chain_c", 12)
        chain_pool = signal("chain_pool", 16)
        roots_due = signal("roots_due", 5)
        pool_steps = sem("pool_steps")
        factors_ready = signal("factors_ready", 1)
        image_loaded = sem("image_loaded")
        image_read = signal("image_read", 1)
        bands_ready = signal("bands_ready", 1)
        dots_ready = signal("dots_ready", 1)
        logits_summed = signal("logits_summed", 1)
        logits_shifted = signal("logits_shifted", 1)
        weights_exp = signal("weights_exp", 1)
        rec_ready = signal("rec_ready", 1)
        rec_turned = signal("rec_turned", 1)
        qk0_proj = signal("qk0_proj", 10)
        qk0_squared = signal("qk0_squared", 10)
        squares_added = signal("squares_added", 1)
        v0_proj = signal("v0_proj", 3)
        v0_ready = signal("v0_ready", 3)
        qk0_root = signal("qk0_root", 1)
        qk0_wide = signal("qk0_wide", 1)
        qk0_ready = signal("qk0_ready", 16)
        qk0_bf16 = signal("qk0_bf16", 4)
        rough0 = signal("rough0", H)
        rowmax0 = signal("rowmax0", H)
        max0_turned = signal("max0_turned", 1)
        shift0_ready = signal("shift0_ready", 1)
        scores0 = signal("scores0", H)
        biased0 = signal("biased0", H)
        probs0 = signal("probs0", H)
        pv0 = signal("pv0", 8)
        y0_copied = signal("y0_copied", 8)
        sums0 = signal("sums0", 4)
        rsum_ready = signal("rsum_ready", 1)
        rsum_wide = signal("rsum_wide", 8)
        y0_ready = signal("y0_ready", 8)
        wo0_done = signal("wo0_done", 1)
        absmax_done = signal("absmax_done", 1)
        fq_ready = signal("fq_ready", 1)
        ffn0_done = signal("ffn0_done", 1)
        qk1_proj = signal("qk1_proj", 4)
        qk1_squared = signal("qk1_squared", 4)
        v1_proj = signal("v1_proj", 3)
        v1_ready = signal("v1_ready", 2)
        vlast_ready = signal("vlast_ready", 1)
        qk1_root = signal("qk1_root", 1)
        root1_turned = signal("root1_turned", 1)
        root1_copied = signal("root1_copied", 1)
        qk1_wide = signal("qk1_wide", 4)
        qk1_normed = signal("qk1_normed", 4)
        qk1_beta = signal("qk1_beta", 4)
        qk1_turned = signal("qk1_turned", 4)
        sin_done = signal("sin_done", 4)
        rope_done = signal("rope_done", 4)
        last_ready = signal("last_ready", 1)
        q1b_ready = signal("q1b_ready", 1)
        kmb_ready = signal("kmb_ready", H)
        km_ready = signal("km_ready", H)
        rough_last = signal("rough_last", 2)
        last_max = signal("last_max", 2)
        rough1 = signal("rough1", H)
        rowmax1 = signal("rowmax1", H)
        max1_ready = signal("max1_ready", 1)
        max1_turned = signal("max1_turned", 1)
        shift1_ready = signal("shift1_ready", 2)
        slast_ready = signal("slast_ready", 1)
        last_scores = signal("last_scores", 1)
        last_probs = signal("last_probs", 2)
        scores1 = signal("scores1", H)
        probs1 = signal("probs1", H)
        pv1 = signal("pv1", 4)
        z_ready = signal("z_ready", 4)
        sums1 = signal("sums1", 1)
        rz_ready = signal("rz_ready", 1)
        rz_wide = signal("rz_wide", 4)
        y1_ready = signal("y1_ready", 4)
        proj1_done = signal("proj1_done", 1)
        gates = signal("gates", 1)
        gates_kept = signal("gates_kept", 2)
        gate_done = signal("gate_done", 2)
        gate_copied = signal("gate_copied", 2)
        value_done = signal("value_done", 2)
        hh_ready = signal("hh_ready", 2)
        out_tok = signal("out_tok", 3)
        out_copied = signal("out_copied", 3)
        out_stored = sem("out_stored")

        def inside(host, at, shape):
            names = " ".join("abcd"[:len(shape)])
            sizes = {"abcd"[n]: shape[n] for n in range(len(shape))}
            return host[0:TT, at:at + int(np.prod(shape))].rearrange(f"p ({names}) -> p {names}", **sizes)

        qkf = qk[:, :, :].rearrange("p n t -> p (n t)")
        sqf = sq[:, :, :].rearrange("p n t -> p (n t)")
        y0f = y0[:, :, :].rearrange("p n t -> p (n t)")
        N8 = NCOL * NE
        prob = inside(att, 0, [NCOL, NE])
        rt = inside(att, N8, [NCOL, NE])
        rk = inside(att, 2 * N8, [NCOL, NE])
        onehot = inside(att, 3 * N8, [NCOL, 2, NE])
        group = inside(sqf, 0, [NCOL, 2, NE])
        ge = inside(qkf, 0, [NCOL * 2, NE])
        g4 = inside(qkf, 2 * N8, [3, NCOL, 4])
        flat = [t[:, :, :].rearrange("p n t -> p (n t)") for t in (h3, n1.cen, u1, qr)]
        oh = [inside(sqf, 2 * N8, [8, 64]), inside(flat[0], 0, [8, 64])]
        ohw = [inside(sqf, 2 * N8 + 512, [8, 64]), inside(flat[1], 0, [8, 64])]
        he = inside(y0f, 0, [8, HID])
        hs = inside(y0f, 1024, [8, HID])
        u1f = flat[2]
        oht = [t[:, 0:8 * TT] for t in flat[2:4]]
        r1 = u1f[0:TT, 8 * TT:8 * TT + NCOL]
        weight = inside(u1f, 8 * TT + NCOL, [NCOL, 2])
        cnt = sb("cnt", [P, NE])
        offs = sb("offs", [TT, NE])
        u8sb = [t[0:NE, :, :].rearrange("p c n -> p (c n)").rearrange("p (g n) -> p g n", g=NE)
                for t in (wqk1, sw13)]
        ew1 = wq0
        ew3 = wo0[:, :, :].rearrange("p (c a) n -> p c (a n)", c=C)
        ew2 = biasf[:, :].bitcast(F32)[:, 0:NE * 256]\
            .rearrange("p (g n) -> p g n", g=NE)
        images_done = sem("images_done")
        experts_loaded = sem("experts_loaded")
        u64 = h1[:, 0, 0:2 * HID]
        acct = h2[0:64, 0, 0:HID]
        accT = h0[:, 0, 0:64]
        r8 = osb[0:8, 0, :]

        table_hidden = signal("table_hidden", 1)
        hidden_copied = sem("hidden_copied")
        rows_cleared = sem("rows_cleared")
        u64_loaded = sem("u64_loaded")
        pairs_stored = sem("pairs_stored")
        pair_dram = nc.dram_tensor("pair_hidden", (NE, NE, 2, HID), F32, kind="Internal").ap()
        counts_ready = sem("counts_ready")
        counts_summed = sem("counts_summed")
        onehots_ready = signal("onehots_ready", 1)
        onehots_turned = signal("onehots_turned", 1)
        turned_copied = signal("turned_copied", 1)
        routed_up = signal("routed_up", 1)
        routed_tanh = signal("routed_tanh", 1)
        routed_h = signal("routed_h", 1)
        routed_added = signal("routed_added", 1)
        acc_copied = sem("acc_copied")
        acc_turned = sem("acc_turned")
        accT_ready = sem("accT_ready")
        routed_out = sem("routed_out")
        rows_loaded = sem("rows_loaded")
        rows_ready = sem("rows_ready")
        rows_stored = sem("rows_stored")
        tail_chain = sem("tail_chain")

        SETUP_DVE = 48
        SETUP_ACT = 4
        ROUNDS = NCOL // 4

        def wait_next(eng, count, signal):
            eng.reg_add(count, count, 1)
            eng.wait_ge(tables_loaded, 16 * len(loads))
            eng.wait_ge(signal.sem, count)

        block = ctx.enter_context(nc.Block())

        @block.sync
        def _(sp):
            for t, src in loads:
                sp.dma_start(t if isinstance(t, bass.AP) else t[:], src).then_inc(tables_loaded, 16)
            with sp.Fori(0, NB) as i:
                sp.wait_ge(image_read.sem, image_read.at(i, 1))
                sp.dma_start(img[:, :], a["x"][bass.ds(i, 1), :, :].rearrange("a p n -> (a p) n"))\
                    .then_inc(image_loaded, 16)
            sp.wait_ge(images_done, 1)
            sp.dma_start(ew1[:, :, :], a["ew1"]).then_inc(experts_loaded, 16)
            sp.dma_start(ew3, a["ew3"].rearrange("p c n -> p c n")).then_inc(experts_loaded, 16)
            sp.dma_start(ew2, a["ew2"]).then_inc(experts_loaded, 16)
            sp.wait_ge(hidden_copied, 2)
            for s in range(2):
                sp.dma_start(pair_dram[:, :, s, :], u8sb[s]).then_inc(pairs_stored, 16)
            sp.wait_ge(pairs_stored, 32)
            sp.dma_start(u64[0:64, :], pair_dram.rearrange("e g s n -> (e g) (s n)")).then_inc(u64_loaded, 16)
            sp.wait_ge(out_stored, 32 * NB + 32)
            sp.dma_start(r8, out[NB - 1, 0:8, :]).then_inc(rows_loaded, 16)
            sp.wait_ge(rows_ready, 1)
            sp.dma_start(out[NB - 1, 0:8, :], r8).then_inc(rows_stored, 16)
            sp.wait_ge(rows_stored, 16)

        @block.gpsimd
        def _(pool):
            G = nc.gpsimd
            n_ln = pool.alloc_register("n_ln")
            pool.reg_mov(n_ln, 0)

            def nothing(name, count=None):
                def part(i):
                    for _ in range(count or STRETCHES[name]):
                        yield
                return part

            def analyse(i):
                ch = Chain(pool, chain_pool, i)
                pool.wait_ge(image_loaded, i * 16 + 16)
                pool.wait_ge(rec_ready.sem, rec_ready.at(i, 1))
                x0 = img[:, :]
                rows = 8
                for lev in range(3):
                    n = [128, 32, 8][lev]
                    half = rows // 2
                    v = x0.rearrange("p (n e) -> p n e", e=2)
                    lo, hi = lohi[:, 0, 0:2 * n], lohi[:, 1, 0:2 * n]
                    ch.mark(G.tensor_tensor(lo, v[:, :, 0], v[:, :, 1], op=ALU.add))
                    sub = G.tensor_tensor(hi, v[:, :, 0], v[:, :, 1], op=ALU.subtract)
                    if lev == 0:
                        sub.then_inc(image_read.sem, 1)
                        ch.sync()
                        pool.wait_ge(image_read.sem, image_read.at(i, 2))
                    else:
                        ch.step(sub)
                    c0 = [0, 384, 480][lev]
                    a0 = [0, 128, 160][lev]
                    lo = lo.rearrange("p (r e n) -> p r e n", r=half, e=2)
                    hi = hi.rearrange("p (r e n) -> p r e n", r=half, e=2)

                    def sub_of(t, at):
                        return t[:, at:at + n].rearrange("p (r n) -> p r n", r=half)

                    ch.mark(G.tensor_tensor(sub_of(coef, c0), lo[:, :, 0], lo[:, :, 1], op=ALU.subtract))
                    ch.mark(G.tensor_tensor(sub_of(coef, c0 + n), hi[:, :, 0], hi[:, :, 1], op=ALU.add))
                    ch.mark(G.tensor_tensor(sub_of(coef, c0 + 2 * n), hi[:, :, 0], hi[:, :, 1], op=ALU.subtract))
                    av = G.tensor_tensor(sub_of(avg, a0), lo[:, :, 0], lo[:, :, 1], op=ALU.add)
                    if lev < 2:
                        ch.step(av)
                    else:
                        av.then_inc(bands_ready.sem, 1)
                    x0 = avg[:, a0:a0 + n]
                    rows = half
                ch.end()

            n_factors = pool.alloc_register("n_factors")
            pool.reg_mov(n_factors, 0)
            n_steps = pool.alloc_register("n_steps")
            pool.reg_mov(n_steps, 0)
            marked = [0]

            def mark(ins):
                ins.then_inc(pool_steps, 1)
                marked[0] += 1

            def sync():
                pool.reg_add(n_steps, n_steps, marked[0])
                marked[0] = 0
                pool.wait_ge(tables_loaded, 16 * len(loads))
                pool.wait_ge(pool_steps, n_steps)

            def step(ins):
                mark(ins)
                sync()

            def first(i):
                yield from nothing("", 2)(i)
                yield from nothing("", 5)(i)
                if isinstance(i, int) and i < 2:
                    analyse(i + 1)
                for n in range(10):
                    if n not in (0, 8):
                        into = sq[:, 0 if n < 8 else 8, :]
                        pool.wait_ge(qk0_squared.sem, qk0_squared.at(i, n + 1))
                        add = G.tensor_tensor(into, into, sq[:, n, :], op=ALU.add)
                        if n < 9:
                            step(add)
                        else:
                            add.then_inc(squares_added.sem, 1)
                    yield
                yield from nothing("", 17)(i)

            def token(i):
                if isinstance(i, int) and i == 0:
                    analyse(0)
                yield from nothing("", 12)(i)
                wait_next(pool, n_factors, factors_ready)
                step(G.tensor_scalar(rec[:, 0:8], avg[:, 160:168], w10[:, 9:10], None, ALU.mult))
                for k, (c0, n, rows, at) in enumerate([(480, 8, 1, 0), (384, 32, 2, 8), (0, 128, 4, 40)]):
                    cur = rec[:, at:at + n].rearrange("p (r n) -> p r n", r=rows)

                    def band(s):
                        return coef[:, c0 + s * n:c0 + (s + 1) * n]

                    def weighed(s):
                        return syn[2][:, s * n:(s + 1) * n] if s < 2 else syn[3][:, 0:n]

                    lo = syn[0][:, 0:2 * n].rearrange("p (r e n) -> p r e n", r=rows, e=2)
                    hi = syn[1][:, 0:2 * n].rearrange("p (r e n) -> p r e n", r=rows, e=2)
                    for s in range(3):
                        mark(G.tensor_scalar(weighed(s), band(s), w10[:, 3 * k + s:3 * k + s + 1], None, ALU.mult))
                    sync()
                    if k:
                        yield
                    wh, wv, wd = [weighed(s).rearrange("p (r n) -> p r n", r=rows) for s in range(3)]
                    for s, op in enumerate((ALU.add, ALU.subtract)):
                        mark(G.tensor_tensor(lo[:, :, s], cur, wh, op=op))
                        mark(G.tensor_tensor(hi[:, :, s], wv, wd, op=op))
                    sync()
                    if k == 2:
                        yield
                    o = rec[:, at + n:at + 5 * n].rearrange("p (n e) -> p n e", e=2)
                    mark(G.tensor_tensor(o[:, :, 0], syn[0][:, 0:2 * n], syn[1][:, 0:2 * n], op=ALU.add))
                    odd = G.tensor_tensor(o[:, :, 1], syn[0][:, 0:2 * n], syn[1][:, 0:2 * n], op=ALU.subtract)
                    if k < 2:
                        step(odd)
                    else:
                        odd.then_inc(rec_ready.sem, 1)
                    yield
                yield
                yield

            def att1(i):
                yield from nothing("", 10)(i)
                if not (isinstance(i, int) and i + 3 >= NB):
                    analyse(i + 3)
                yield from nothing("", STRETCHES["att1"] - 10)(i)

            def middle(i):
                yield from nothing("", 5)(i)
                wait_next(pool, n_ln, n1.done)
                pool.partition_all_reduce(amax, n1.xn[:, :, :], P, ABSMAX).then_inc(absmax_done.sem, 1)
                yield from nothing("", STRETCHES["middle"] - 5)(i)

            schedule(pool, {"token": token, "first": first, "att0": nothing("att0"), "middle": middle,
                            "att1": att1, "last": nothing("last")})

        @block.tensor
        def _(pe):
            def mm(o, l, r, start=True, stop=True, loose=False):
                return pe.matmul(o, l, r, start=start, stop=stop, skip_group_check=loose)

            pe.wait_ge(tables_loaded, 16 * len(loads))
            pe.wait_ge(dve_setup, SETUP_DVE)
            pe.wait_ge(act_setup, SETUP_ACT)

            n_rec = pe.alloc_register("n_rec")
            pe.reg_mov(n_rec, 1)

            def layernorm(nm, i):
                pe.wait_ge(nm.src_ready.sem, nm.src_ready.at(i, 1))
                for c in range(C):
                    m = mm(PS[:, nm.mean_bank, 0:T], ones256[:, :], nm.src[:, c, :], c == 0, c == C - 1)
                m.then_inc(nm.mean_done.sem, 1)
                yield
                yield
                pe.wait_ge(nm.squared.sem, nm.squared.at(i, 1))
                for t in range(3):
                    for c in range(C):
                        m = mm(PS[0:TT, nm.var_bank, t:t + 1], nm.csq[:, c, t * TT:(t + 1) * TT],
                               ones256[:, 0:1], c == 0, c == C - 1)
                m.then_inc(roots_due.sem, 1)
                yield
                yield
                pe.wait_ge(nm.root_done.sem, nm.root_done.at(i, 1))
                for t, (t0, tn) in enumerate(TILES):
                    m = mm(PS[:, nm.mean_bank, t0:t0 + tn], nm.small[:, 0, t:t + 1].broadcast_to([TT, P]),
                           ident[0:TT, 0:tn])
                m.then_inc(nm.root_wide.sem, 1)
                yield
                pe.wait_ge(nm.done.sem, nm.done.at(i, 1))

            def token(i):
                for _ in range(10):
                    yield
                pe.wait_ge(dots_ready.sem, dots_ready.at(i, 1))
                mm(PS[:, 6, 0:10], ones[:, :], dots[:, :]).then_inc(logits_summed.sem, 1)
                yield
                pe.wait_ge(logits_shifted.sem, logits_shifted.at(i, 1))
                for _ in range(9):
                    yield

            def first(i):
                wait_next(pe, n_rec, rec_ready)
                for r in range(8):
                    m = pe.transpose(PS[0:64, 5 + r // 4, (r % 4) * P:(r % 4 + 1) * P],
                                     rec[:, 168 + 64 * r:168 + 64 * (r + 1)], ident[:, :])
                m.then_inc(rec_turned.sem, 1)
                yield
                yield
                yield from layernorm(n0, i)
                for n in range(10):
                    w, j = (wq0, n) if n < 8 else (wk0, n - 8)
                    if n >= 3:
                        pe.wait_ge(qk0_squared.sem, qk0_squared.at(i, n - 2))
                    for c in range(C):
                        m = mm(PS[:, 4 + n % 3, 0:T], w[:, c, j * P:(j + 1) * P], n0.xn[:, c, :],
                               c == 0, c == C - 1)
                    m.then_inc(qk0_proj.sem, 1)
                    yield
                for t, (t0, tn) in enumerate(TILES):
                    pe.wait_ge(qk0_squared.sem, qk0_squared.at(i, 8 + t))
                    for c in range(C):
                        m = mm(PS[0:tn, 4 + (t + 1) % 3, 0:256], n0.xn[:, c, t0:t0 + tn], wv0[:, c, :], c == 0, c == C - 1)
                    m.then_inc(v0_proj.sem, 1)
                    yield
                pe.wait_ge(squares_added.sem, squares_added.at(i, 1))
                for t in range(3):
                    for b, n, col in ((0, 0, ones1024), (1, 8, ones256)):
                        m = mm(PS[0:TT, 7, 2 * t + b:2 * t + b + 1], sq[:, n, t * TT:(t + 1) * TT],
                               col[:, 0:1])
                m.then_inc(roots_due.sem, 1)
                yield
                pe.wait_ge(v0_ready.sem, v0_ready.at(i, 3))
                pe.wait_ge(qk0_root.sem, qk0_root.at(i, 1))
                for b in range(2):
                    for t, (t0, tn) in enumerate(TILES):
                        m = mm(PS[:, 4 + b, t0:t0 + tn],
                               qks[:, 0, 2 * t + b:2 * t + b + 1].broadcast_to([TT, P]), ident[0:TT, 0:tn])
                m.then_inc(qk0_wide.sem, 1)
                yield
                yield
                yield
                for h in range(H):
                    if h % 8 == 0:
                        pe.wait_ge(qk0_bf16.sem, qk0_bf16.at(i, 3 + h // 8))
                    j, g = h // 2, h // 4
                    if h >= 3:
                        pe.wait_ge(rowmax0.sem, rowmax0.at(i, h - 2))
                    for (t0, tn), (k0, kn), kc in zip(TILES, KR0, KC0):
                        m = mm(PS[0:tn, 5 + h % 3, kc:kc + kn], qkb[:, j, t0:t0 + tn],
                               qkb[:, 8 + 4 * (h % 2) + g, k0:k0 + kn])
                    m.then_inc(rough0.sem, 1)
                    if h % 2:
                        yield
                pe.wait_ge(rowmax0.sem, rowmax0.at(i, H))
                for t, (t0, tn) in enumerate(TILES):
                    m = pe.transpose(PS[0:H, 4, t0:t0 + tn], mtok[0:tn, t, :], ident[0:tn, 0:tn])
                m.then_inc(max0_turned.sem, 1)
                yield
                pe.wait_ge(shift0_ready.sem, shift0_ready.at(i, 1))
                yield

            def att0(i):
                def score(h):
                    j, g = h // 2, h // 4
                    if h >= 2:
                        pe.wait_ge(biased0.sem, biased0.at(i, h - 1))
                    for t in range(3):
                        (q0, qn), c0 = QR0[t], QC0[t]
                        o = PS[0:TT, h % 2, c0:c0 + qn]
                        mm(o, qk[:, 8 + 4 * (h % 2) + g, t * TT:(t + 1) * TT], qk[:, j, q0:q0 + qn], True, False)
                        m = mm(o, identb[:, h:h + 1].broadcast_to([P, TT]), shift0[:, q0:q0 + qn], False, True)
                    m.then_inc(scores0.sem, 1)

                score(0)
                score(1)
                yield
                for j in range(8):
                    if j < 7:
                        score(2 * j + 2)
                    yield
                    if j < 7:
                        score(2 * j + 3)
                    yield
                    pe.wait_ge(probs0.sem, probs0.at(i, 2 * j + 2))
                    if j:
                        pe.wait_ge(y0_copied.sem, y0_copied.at(i, j))
                    for t in range(3):
                        (q0, qn), c0 = QR0[t], QC0[t]
                        for h in (2 * j, 2 * j + 1):
                            k = 64 * (h % 2)
                            m = mm(PS[k:k + 64, 2, q0:q0 + qn], vx[:, t, h // 4, :], pr0[:, h % 6, c0:c0 + qn],
                                   t == 0, t == 2, loose=True)
                    m.then_inc(pv0.sem, 1)
                    yield
                    if j % 2:
                        g = j // 2
                        for t in range(3):
                            (q0, qn), c0 = QR0[t], QC0[t]
                            for k in range(4):
                                h = 4 * g + k
                                m = mm(PS[32 * k:32 * k + 32, 3, q0:q0 + qn], sumsel[0:TT, g, :],
                                       pr0[:, h % 6, c0:c0 + qn], t == 0 and g == 0, t == 2 and g == 3,
                                       loose=True)
                        m.then_inc(sums0.sem, 1)
                    yield
                pe.wait_ge(y0_copied.sem, y0_copied.at(i, 8))
                yield
                pe.wait_ge(rsum_ready.sem, rsum_ready.at(i, 1))
                for j in range(8):
                    if j >= 2:
                        pe.wait_ge(y0_ready.sem, y0_ready.at(i, j - 1))
                    mm(PS[:, j % 2, 0:T], sumback[:, j, :], rsum[:, :]).then_inc(rsum_wide.sem, 1)
                    if j >= 1:
                        yield
                        pe.wait_ge(y0_ready.sem, y0_ready.at(i, j))
                        for c in range(C):
                            mm(PS[:, 2 + c, 0:T], wo0[:, j - 1, c * P:(c + 1) * P], y0[:, j - 1, :], j == 1,
                               False, loose=True)
                yield
                pe.wait_ge(y0_ready.sem, y0_ready.at(i, 8))
                for c in range(C):
                    m = mm(PS[:, 2 + c, 0:T], wo0[:, 7, c * P:(c + 1) * P], y0[:, 7, :], False, True, loose=True)
                m.then_inc(wo0_done.sem, 1)
                yield
                pe.wait_ge(n1.src_ready.sem, n1.src_ready.at(i, 1))
                yield

            def middle(i):
                yield from layernorm(n1, i)
                yield
                yield
                yield
                yield
                yield
                pe.wait_ge(fq_ready.sem, fq_ready.at(i, 1))
                for o in range(C):
                    for c in range(C):
                        m = mm(PS[:, 4 + o, 0:T], w8b[:, c, o * P:(o + 1) * P], fq[:, c, :], c == 0, c == C - 1)
                m.then_inc(ffn0_done.sem, 1)
                yield
                yield from layernorm(n2, i)
                for n in range(4):
                    if n >= 2:
                        pe.wait_ge(qk1_squared.sem, qk1_squared.at(i, n - 1))
                    for c in range(C):
                        m = mm(PS[:, 4 + n % 2, 0:T], wqk1[:, c, n * P:(n + 1) * P], n2.xn[:, c, :],
                               c == 0, c == C - 1)
                    m.then_inc(qk1_proj.sem, 1)
                    yield
                for t in range(2):
                    pe.wait_ge(qk1_squared.sem, qk1_squared.at(i, 3 + t))
                    for c in range(C):
                        m = mm(PS[:, 4 + t, 0:256], n2.xn[:, c, t * P:(t + 1) * P], wv1[:, c, :],
                               c == 0, c == C - 1)
                    m.then_inc(v1_proj.sem, 1)
                yield
                pe.wait_ge(v1_ready.sem, v1_ready.at(i, 1))
                for c in range(C):
                    m = mm(PS[0:H, 4, 0:256], n2.xn[:, c, 256:257].broadcast_to([P, H]), wv1[:, c, :],
                           c == 0, c == C - 1)
                m.then_inc(v1_proj.sem, 1)
                pe.wait_ge(v1_ready.sem, v1_ready.at(i, 2))
                for t in range(3):
                    for n in range(4):
                        m = mm(PS[0:TT, 5, 32 * t + 8 * n:32 * t + 8 * n + 8], sq1[:, n, t * TT:(t + 1) * TT],
                               block8[:, :])
                m.then_inc(roots_due.sem, 1)
                yield
                yield
                pe.wait_ge(qk1_root.sem, qk1_root.at(i, 1))
                pe.wait_ge(vlast_ready.sem, vlast_ready.at(i, 1))
                for t, (t0, tn) in enumerate(TILES):
                    m = mm(PS[0:32, 4, t0:t0 + tn], root1[:, 0, t, :], ident[0:TT, 0:tn])
                m.then_inc(root1_turned.sem, 1)
                yield
                pe.wait_ge(root1_copied.sem, root1_copied.at(i, 1))
                for n in range(4):
                    if n >= 2:
                        pe.wait_ge(qk1_normed.sem, qk1_normed.at(i, n - 1))
                    mm(PS[:, 4 + n % 2, 0:T], expand[:, n, :], root32[:, :]).then_inc(qk1_wide.sem, 1)
                    yield
                for n in range(4):
                    pe.wait_ge(qk1_beta.sem, qk1_beta.at(i, n + 1))
                    if n >= 2:
                        pe.wait_ge(sin_done.sem, sin_done.at(i, n - 1))
                    else:
                        pe.wait_ge(qk1_normed.sem, qk1_normed.at(i, n + 3))
                    mm(PS[:, 4 + n % 2, 0:T], rotate[:, :], u1[:, n, :]).then_inc(qk1_turned.sem, 1)
                    yield
                yield
                pe.wait_ge(sin_done.sem, sin_done.at(i, 4))
                pe.wait_ge(last_ready.sem, last_ready.at(i, 1))
                for c in range(C):
                    m = mm(PS[0:H, 4, 0:T], qlast[:, c, :], qr[:, 2 + c, :], c == 0, c == C - 1)
                m.then_inc(rough_last.sem, 1)
                for t in range(2):
                    for c in range(C):
                        m = mm(PS[:, 5, H * t:H * t + H], qr[:, c, t * P:(t + 1) * P], klast[:, c, :],
                               c == 0, c == C - 1)
                m.then_inc(rough_last.sem, 1)
                yield
                pe.wait_ge(q1b_ready.sem, q1b_ready.at(i, 1))
                for h in range(H):
                    if h >= 2:
                        pe.wait_ge(rowmax1.sem, rowmax1.at(i, h - 1))
                    else:
                        pe.wait_ge(last_max.sem, last_max.at(i, h + 1))
                    pe.wait_ge(kmb_ready.sem, kmb_ready.at(i, h + 1))
                    for t in range(2):
                        m = mm(PS[:, 4 + h % 2, 256 * t:256 * t + 256], q1b[:, h // 8, t * P:(t + 1) * P],
                               kmb[:, h % 4, :])
                    m.then_inc(rough1.sem, 1)
                    if h % 2:
                        yield
                pe.wait_ge(max1_ready.sem, max1_ready.at(i, 1))
                for t in range(2):
                    m = mm(PS[0:H, 4, t * P:(t + 1) * P], mtok1[:, t, :], ident[:, :])
                m.then_inc(max1_turned.sem, 1)
                yield
                pe.wait_ge(shift1_ready.sem, shift1_ready.at(i, 2))
                for c in range(C):
                    mm(PS[0:H, 5, 0:T], klast[:, c, :], qr[:, c, :], c == 0, False)
                mm(PS[0:H, 5, 0:T], identb[:, :], shift1[:, :], False, True)
                pe.wait_ge(slast_ready.sem, slast_ready.at(i, 1))
                for t in range(2):
                    for c in range(C):
                        mm(PS[:, 4, H * t:H * t + H], qr[:, 2 + c, t * P:(t + 1) * P], qlast[:, c, :],
                           c == 0, False)
                    m = mm(PS[:, 4, H * t:H * t + H], onesb[:, :], slast[:, :], False, True)
                m.then_inc(last_scores.sem, 1)
                yield
                pe.wait_ge(last_probs.sem, last_probs.at(i, 2))
                yield

            def att1(i):
                def context(g):
                    pe.wait_ge(probs1.sem, probs1.at(i, 4 * g + 4))
                    if g >= 2:
                        pe.wait_ge(z_ready.sem, z_ready.at(i, g - 1))
                    heads = range(4 * g, 4 * g + 4)
                    for t in range(2):
                        for h in heads:
                            k = 32 * (h % 4)
                            mm(PS[k:k + 32, 2 + g % 2, 0:256], v1x[:, t, h, :], pr1[:, h % 8, t, :], t == 0,
                               False, loose=True)
                        for h in heads:
                            k = 32 * (h % 4)
                            mm(PS[k:k + 32, 2 + g % 2, 256:257], v1x[:, t, h, :], pqlast[:, t, h:h + 1], False,
                               False, loose=True)
                    mm(PS[:, 2 + g % 2, 0:T], vlast[:, 4 * g:4 * g + 4, :], pklast[:, :], False, True,
                       loose=True).then_inc(pv1.sem, 1)

                for h in range(H):
                    c = h // 8
                    if h >= 2:
                        pe.wait_ge(probs1.sem, probs1.at(i, h - 1))
                    pe.wait_ge(km_ready.sem, km_ready.at(i, h + 1))
                    for t in range(2):
                        o = PS[:, h % 2, 256 * t:256 * t + 256]
                        mm(o, km[:, h % 4, t * P:(t + 1) * P], qr[:, c, 0:256], True, False)
                        m = mm(o, identb[:, h:h + 1].broadcast_to([P, P]), shift1[:, 0:256], False, True)
                    m.then_inc(scores1.sem, 1)
                    yield
                    if h % 4 == 1 and h > 4:
                        context(h // 4 - 1)
                    yield
                context(3)
                yield
                pe.wait_ge(z_ready.sem, z_ready.at(i, 4))
                for g in range(4):
                    m = mm(PS[0:H, 0, 0:T], collect[:, g, :], zz[:, g, :], g == 0, g == 3)
                m.then_inc(sums1.sem, 1)
                yield
                pe.wait_ge(rz_ready.sem, rz_ready.at(i, 1))
                for n in range(4):
                    if n >= 2:
                        pe.wait_ge(y1_ready.sem, y1_ready.at(i, n - 1))
                    mm(PS[:, n % 2, 0:T], spread[:, n, :], rz[:, :]).then_inc(rz_wide.sem, 1)
                    if n >= 1:
                        yield
                        pe.wait_ge(y1_ready.sem, y1_ready.at(i, n))
                        for c in range(C):
                            mm(PS[:, 2 + c, 0:T], wp1[:, n - 1, c * P:(c + 1) * P], zz[:, n - 1, :], n == 1,
                               False, loose=True)
                yield
                pe.wait_ge(y1_ready.sem, y1_ready.at(i, 4))
                for c in range(C):
                    m = mm(PS[:, 2 + c, 0:T], wp1[:, 3, c * P:(c + 1) * P], zz[:, 3, :], False, True, loose=True)
                m.then_inc(proj1_done.sem, 1)
                yield
                pe.wait_ge(n3.src_ready.sem, n3.src_ready.at(i, 1))
                yield

            def last(i):
                yield from layernorm(n3, i)
                for t, (t0, tn) in enumerate(TILES):
                    for c in range(C):
                        m = mm(PS[0:tn, 7, t * NE:(t + 1) * NE], n3.xn[:, c, t0:t0 + tn], wg[:, c, :],
                               c == 0, c == C - 1)
                m.then_inc(gates.sem, 1)
                yield
                for n in range(2):
                    if n:
                        pe.wait_ge(gate_copied.sem, gate_copied.at(i, 1))
                    for c in range(C):
                        m = mm(PS[:, 6, 0:T], sw13[:, c, n * P:(n + 1) * P], n3.xn[:, c, :], c == 0, c == C - 1)
                    m.then_inc(gate_done.sem, 1)
                    yield
                    if n:
                        pe.wait_ge(hh_ready.sem, hh_ready.at(i, 1))
                    else:
                        pe.wait_ge(gates_kept.sem, gates_kept.at(i, 2))
                    for c in range(C):
                        m = mm(PS[:, 7, 0:T], sw13[:, c, (2 + n) * P:(3 + n) * P], n3.xn[:, c, :],
                               c == 0, c == C - 1)
                    m.then_inc(value_done.sem, 1)
                    yield
                pe.wait_ge(gate_copied.sem, gate_copied.at(i, 2))
                pe.wait_ge(hh_ready.sem, hh_ready.at(i, 2))
                for t, (t0, tn) in enumerate(TILES):
                    bank = 6 + t % 2
                    if t == 2:
                        pe.wait_ge(out_copied.sem, out_copied.at(i, 1))
                    for c in range(C):
                        mm(PS[0:tn, bank, 0:256], hh[:, c, t0:t0 + tn], sw2[:, c, :], c == 0, False, loose=True)
                    for c in range(C):
                        m = mm(PS[0:tn, bank, c * P:(c + 1) * P], h3[:, c, t0:t0 + tn], ident[:, :],
                               False, c == C - 1, loose=True)
                    m.then_inc(out_tok.sem, 1)
                    yield
                pe.wait_ge(out_copied.sem, out_copied.at(i, 3))
                yield

            schedule(pe, {"token": token, "first": first, "att0": att0, "middle": middle, "att1": att1, "last": last})
            pe.wait_ge(gates_kept.sem, gates_kept.at(NB - 1, 2))
            pe.transpose(PS[0:64, 0, 0:P], ident[:, 0:64], ident[:, :]).then_inc(images_done, 1)

            pe.wait_ge(experts_loaded, 48)
            for s, w in enumerate((ew1, ew3)):
                for b in range(2):
                    for c in range(C):
                        m = mm(PS[0:8, 2 * s + b, 0:512], n3.xn[:, c, 0:8], w[:, c, 512 * b:512 * (b + 1)],
                               c == 0, c == C - 1)
            m.then_inc(table_hidden.sem, 1)
            pe.wait_ge(counts_ready, 1)
            mm(PS[:, 4, 0:NE], ones[0:TT, :], cnt[0:TT, :]).then_inc(counts_summed, 1)
            pe.wait_ge(u64_loaded, 16)
            pe.wait_ge(rows_cleared, 3)
            pe.wait_ge(hidden_copied, 2)
            n_onehots = pe.alloc_register("n_onehots")
            pe.reg_mov(n_onehots, 0)

            def turn_round(k):
                wait_next(pe, n_onehots, onehots_ready)
                for n in range(8):
                    m = pe.transpose(PS[0:64, 4 + n // 4, (n % 4) * TT:(n % 4 + 1) * TT], ohw[k][:, n, :],
                                     ident[0:TT, 0:TT])
                m.then_inc(onehots_turned.sem, 1)

            def routed_round(r, k, more):
                pe.wait_ge(turned_copied.sem, turned_copied.at(r, 1))
                for n in range(8):
                    m = mm(PS[0:TT, n // 2, 256 * (n % 2):256 * (n % 2) + 256], oht[k][:, n * TT:(n + 1) * TT],
                           u64[:, :])
                m.then_inc(routed_up.sem, 1)
                if more:
                    turn_round(1 - k)
                pe.wait_ge(routed_h.sem, routed_h.at(r, 1))
                for n in range(8):
                    m = mm(PS[0:64, 6, 0:HID], oh[k][:, n, :], hs[:, n, :], n == 0, n == 7)
                m.then_inc(routed_added.sem, 1)

            turn_round(0)
            with pe.Fori(0, ROUNDS // 2 - 1) as pair:
                for k in range(2):
                    routed_round(pair * 2 + k, k, True)
            for k in range(2):
                routed_round(ROUNDS - 2 + k, k, k == 0)
            pe.wait_ge(acc_copied, ROUNDS + 1)
            pe.transpose(PS[:, 4, 0:64], acct[:, :], ident[0:64, 0:64]).then_inc(acc_turned, 1)
            pe.wait_ge(accT_ready, 1)
            turned = accT[:, :].rearrange("p (e g) -> p g e", g=NE)
            for g in range(NE):
                m = mm(PS[0:8, 5, 0:256], turned[:, g, :], ew2[:, g, :], g == 0, g == NE - 1)
            m.then_inc(routed_out, 1)

        @block.scalar
        def _(act):
            A = nc.scalar.activation
            act.wait_ge(tables_loaded, 16 * len(loads))
            A(h0[:, :, 0:1], clst[:, :].rearrange("p (c a) -> p c a", a=1), ACT.Copy).then_inc(act_setup, 1)
            A(osb[0:1, 0, 0:4], ident[0:1, 0:4], ACT.Copy).then_inc(out_stored, 32)
            A(gb1[:, 0:1], gb1[:, 0:1], ACT.Copy, scale=0.25).then_inc(act_setup, 1)
            A(gb1[:, 2:3], gb1[:, 2:3], ACT.Copy, scale=0.25).then_inc(act_setup, 1)
            A(qkw0[:, 0:8], qkw0[:, 0:8], ACT.Copy, scale=0.125).then_inc(act_setup, 1)
            act.wait_ge(act_setup, SETUP_ACT)
            act.wait_ge(dve_setup, SETUP_DVE)

            def idle(n):
                for _ in range(n):
                    yield

            def layernorm(nm, i):
                yield
                act.wait_ge(nm.centred.sem, nm.centred.at(i, 1))
                A(nm.csq[:, :, 0:T], nm.cen[:, :, :], ACT.Square).then_inc(nm.squared.sem, 1)
                yield
                yield
                yield
                yield

            def token(i):
                yield from idle(11)
                act.wait_ge(logits_shifted.sem, logits_shifted.at(i, 1))
                A(e10[:, :], z10[:, :], ACT.Exp).then_inc(weights_exp.sem, 1)
                yield from idle(9)

            def first(i):
                yield
                act.wait_ge(rec_turned.sem, rec_turned.at(i, 1))
                for cg in range(4):
                    src = PS[0:64, 5:7, :].rearrange("p b (r q n) -> p b r q n", r=4, q=4)[:, :, :, cg, :]
                    dst = h0[64 * (cg % 2):64 * (cg % 2) + 64, cg // 2, 1:T]\
                        .rearrange("p (n b r) -> p b r n", b=2, r=4)
                    cp = A(dst, src, ACT.Copy)
                cp.then_inc(n0.src_ready.sem, 1)
                yield
                yield from layernorm(n0, i)
                for n in range(10):
                    act.wait_ge(qk0_proj.sem, qk0_proj.at(i, n + 1))
                    if n < 8:
                        A(qk[:, n, 0:T], PS[:, 4 + n % 3, 0:T], ACT.Copy)
                    else:
                        for half in range(2):
                            g, src = 2 * (n - 8) + half, PS[64 * half:64 * half + 64, 4 + n % 3, 0:T]
                            A(qk[0:64, 8 + g, 0:T], src, ACT.Copy)
                            A(qk[64:P, 12 + g, 0:T], src, ACT.Copy)
                    A(sq[:, n, 0:T], PS[:, 4 + n % 3, 0:T], ACT.Square).then_inc(qk0_squared.sem, 1)
                    yield
                for t, (_, tn) in enumerate(TILES):
                    act.wait_ge(v0_proj.sem, v0_proj.at(i, t + 1))
                    A(vx[0:tn, t, :, :], PS[0:tn, 4 + (t + 1) % 3, 0:256].rearrange("p (g d) -> p g d", g=KV), ACT.Copy)\
                        .then_inc(v0_ready.sem, 1)
                    yield
                yield
                act.wait_ge(qk0_ready.sem, qk0_ready.at(i, 8))
                for r0, n in ((0, 8), (64, 12)):
                    A(qkb[r0:r0 + 64, n:n + 4, :], qk[r0:r0 + 64, n:n + 4, 0:T], ACT.Copy).then_inc(qk0_bf16.sem, 1)
                yield
                for n in range(2):
                    act.wait_ge(qk0_ready.sem, qk0_ready.at(i, 4 * n + 12))
                    A(qkb[:, 4 * n:4 * n + 4, :], qk[:, 4 * n:4 * n + 4, 0:T], ACT.Copy).then_inc(qk0_bf16.sem, 1)
                    yield
                yield from idle(8)
                act.wait_ge(max0_turned.sem, max0_turned.at(i, 1))
                A(shift0[0:H, :], PS[0:H, 4, 0:T], ACT.Copy, scale=-1.0).then_inc(shift0_ready.sem, 1)
                yield
                yield

            def att0(i):
                def prob0(h):
                    act.wait_ge(biased0.sem, biased0.at(i, h + 1))
                    if h >= 6:
                        act.wait_ge(sums0.sem, sums0.at(i, (h - 6) // 4 + 1))
                    A(pr0[:, h % 6, :], pre[:, h % 2, :], ACT.Exp).then_inc(probs0.sem, 1)

                prob0(0)
                yield
                for j in range(8):
                    prob0(2 * j + 1)
                    yield
                    yield
                    if j < 7:
                        prob0(2 * j + 2)
                    yield
                    act.wait_ge(pv0.sem, pv0.at(i, j + 1))
                    A(y0[:, j, :], PS[:, 2, 0:T], ACT.Copy).then_inc(y0_copied.sem, 1)
                    yield
                yield from idle(11)

            def middle(i):
                yield from layernorm(n1, i)
                yield from idle(6)
                yield from layernorm(n2, i)
                for n in range(4):
                    act.wait_ge(qk1_proj.sem, qk1_proj.at(i, n + 1))
                    A(u1[:, n, :], PS[:, 4 + n % 2, 0:T], ACT.Copy, scale=gb1[:, n // 2:n // 2 + 1])
                    A(sq1[:, n, 0:T], PS[:, 4 + n % 2, 0:T], ACT.Square).then_inc(qk1_squared.sem, 1)
                    yield
                for t in range(2):
                    act.wait_ge(v1_proj.sem, v1_proj.at(i, t + 1))
                    A(v1x[:, t, :, 0:16], PS[:, 4 + t, 0:256].rearrange("p (h d) -> p h d", h=H), ACT.Copy)\
                        .then_inc(v1_ready.sem, 1)
                yield
                yield
                yield from idle(3)
                for n in range(4):
                    act.wait_ge(qk1_normed.sem, qk1_normed.at(i, n + 1))
                    A(u1[:, n, :], u1[:, n, :], ACT.Identity, bias=gb1[:, 2 + n // 2:3 + n // 2])\
                        .then_inc(qk1_beta.sem, 1)
                    yield
                yield from idle(3)
                act.wait_ge(rope_done.sem, rope_done.at(i, 4))
                A(q1b[:, :, :], qr[:, 0:2, :], ACT.Copy).then_inc(q1b_ready.sem, 1)
                yield
                yield
                yield from idle(8)
                act.wait_ge(max1_turned.sem, max1_turned.at(i, 1))
                A(shift1[0:H, 0:256], PS[0:H, 4, 0:256], ACT.Copy, scale=-1.0).then_inc(shift1_ready.sem, 1)
                yield
                act.wait_ge(last_scores.sem, last_scores.at(i, 1))
                A(pklast[:, :], PS[0:H, 5, 0:T], ACT.Exp).then_inc(last_probs.sem, 1)
                A(pqlast[:, :, :], PS[:, 4, 0:2 * H].rearrange("p (t h) -> p t h", t=2), ACT.Exp)\
                    .then_inc(last_probs.sem, 1)
                yield
                yield

            def att1(i):
                def keep(g):
                    act.wait_ge(pv1.sem, pv1.at(i, g + 1))
                    A(zz[:, g, :], PS[:, 2 + g % 2, 0:T], ACT.Copy).then_inc(z_ready.sem, 1)

                for h in range(H):
                    if h % 4 == 2 and h > 4:
                        keep(h // 4 - 1)
                    yield
                    act.wait_ge(scores1.sem, scores1.at(i, h + 1))
                    if h >= 8:
                        act.wait_ge(pv1.sem, pv1.at(i, h // 4 - 1))
                    A(pr1[:, h % 8, :, :], PS[:, h % 2, :].rearrange("p (t n) -> p t n", t=2), ACT.Exp)\
                        .then_inc(probs1.sem, 1)
                    yield
                keep(3)
                yield
                yield from idle(7)

            def last(i):
                yield from layernorm(n3, i)
                yield
                for n in range(2):
                    act.wait_ge(gate_done.sem, gate_done.at(i, n + 1))
                    A(half_t[:, n, 0:T], PS[:, 6, 0:T], ACT.Tanh, scale=0.5)
                    A(gate_in[:, n, :], PS[:, 6, 0:T], ACT.Copy, scale=0.5).then_inc(gate_copied.sem, 1)
                    yield
                    yield
                act.wait_ge(out_stored, i * 32 + 32)
                for t, (_, tn) in enumerate(TILES):
                    act.wait_ge(out_tok.sem, out_tok.at(i, t + 1))
                    A(osb[0:tn, t, :], PS[0:tn, 6 + t % 2, 0:256], ACT.Copy).then_inc(out_copied.sem, 1)
                    yield
                act.wait_ge(out_copied.sem, out_copied.at(i, 3))
                o = out[bass.ds(i, 1), :, :]
                act.dma_start(o[:, 0:2 * TT, :].rearrange("a (t p) d -> p (a t) d", p=TT), osb[:, 0:2, :])\
                    .then_inc(out_stored, 16)
                act.dma_start(o[:, 2 * TT:T, :].rearrange("a p d -> p (a d)"), osb[0:85, 2, :])\
                    .then_inc(out_stored, 16)
                yield

            schedule(act, {"token": token, "first": first, "att0": att0, "middle": middle, "att1": att1, "last": last})

            act.wait_ge(table_hidden.sem, table_hidden.at(0, 1))
            for s in range(2):
                A(u8sb[s], PS[0:8, 2 * s:2 * s + 2, :].rearrange("p b (g n) -> p (b g) n", n=HID), ACT.Copy)\
                    .then_inc(hidden_copied, 1)
            act.wait_ge(logits_shifted.sem, logits_shifted.at(NB, 1))
            A(prob[:, :, :], rt[:, :, :], ACT.Exp).then_inc(weights_exp.sem, 1)
            with act.Fori(0, ROUNDS) as r:
                act.wait_ge(routed_up.sem, routed_up.at(r, 1))
                A(he[:, :, :], PS[0:TT, 0:4, :].rearrange("p b (n s d) -> p (b n) s d", n=2, s=2)[:, :, 0, :],
                  ACT.Tanh, scale=0.5).then_inc(routed_tanh.sem, 1)

        @block.vector
        def _(dve):
            V = nc.vector
            n_setup = [0]

            def setup(ins):
                n_setup[0] += 1
                ins.then_inc(dve_setup, 1)

            def settled():
                dve.wait_ge(dve_setup, n_setup[0])

            V.memset(img[:, :], 0.0).then_inc(image_read.sem, 1)
            V.memset(coef[:, :], 0.0).then_inc(rec_ready.sem, 1)
            setup(V.memset(ones[:, :], 1.0))
            setup(V.memset(onesb[:, :], 1.0))
            setup(V.memset(ones256[:, :], 1.0 / 256))
            setup(V.memset(ones1024[:, :], 1.0 / 1024))
            setup(V.memset(vx[:, :, :, :], 0.0))
            setup(V.memset(v1x[:, :, :, :], 1.0))
            setup(V.memset(shift0[:, :], 0.0))
            setup(V.memset(shift1[:, :], 0.0))
            setup(V.memset(qk[:, 0:8, T:TP], 0.0))
            setup(V.memset(qk[:, 8:16, :], 0.0))
            setup(V.memset(qkb[:, 8:16, :], 0.0))
            setup(V.memset(sq[:, :, T:TP], 0.0))
            setup(V.memset(sq1[:, :, T:TP], 0.0))
            for w in works:
                setup(V.memset(w[1][:, :, T:TP], 0.0))
            setup(V.memset(lg[:, :, :], 0.0))
            settled()
            dve.wait_ge(tables_loaded, 16 * len(loads))
            w8x = [sq[:, 2 * n:2 * n + 2, 0:256] for n in range(4)]
            w8i, w8m, w8f, w8g = w8x[0].bitcast(I32), w8x[1].bitcast(I32), w8x[2], w8x[3]
            for h in range(H):
                setup(V.tensor_scalar(biasq[0:TT, h, :], relq, SLOPES[h], None, ALU.mult))
            setup(V.tensor_copy(identb[:, :], ident[:, 0:H]))
            setup(V.tensor_copy(vlast[:, :, 16:32], ident[0:H, 0:H].unsqueeze(2).broadcast_to([H, H, 16])))
            setup(V.tensor_copy(w8i[:, :, :], w8[:, :, :]))
            settled()
            setup(V.tensor_scalar(w8m[:, :, :], w8i[:, :, :], 127, None, ALU.bitwise_and))
            settled()
            setup(V.tensor_scalar(w8i[:, :, :], w8i[:, :, :], 128, 24, ALU.bitwise_and, ALU.logical_shift_left))
            setup(V.tensor_copy(w8f[:, :, :], w8m[:, :, :]))
            settled()
            setup(V.tensor_scalar(w8m[:, :, :], w8m[:, :, :], 20, None, ALU.logical_shift_left))
            setup(V.tensor_scalar(w8f[:, :, :], w8f[:, :, :], 8.0, 2.0 ** -9, ALU.min, ALU.mult))
            settled()
            setup(V.tensor_scalar(w8g[:, :, :], w8m[:, :, :].bitcast(F32), 2.0 ** 120, None, ALU.mult))
            settled()
            setup(V.tensor_tensor(w8f[:, :, :], w8f[:, :, :], w8g[:, :, :], op=ALU.max))
            settled()
            setup(V.tensor_tensor(w8m[:, :, :], w8f[:, :, :].bitcast(I32), w8i[:, :, :], op=ALU.bitwise_or))
            settled()
            setup(V.tensor_copy(w8b[:, :, :], w8m[:, :, :].bitcast(F32)))
            wh = wqk1[:, :, :].rearrange("p c (h d) -> p c h d", d=16)
            setup(V.tensor_reduce(wmean[:, :, :], wh, axis=AX_X, op=ALU.add))
            settled()
            setup(V.tensor_scalar(wmean[:, :, :], wmean[:, :, :], 1.0 / 16, None, ALU.mult))
            settled()
            for c in range(C):
                setup(V.tensor_tensor(wh[:, c], wh[:, c],
                                      wmean[:, c, :].unsqueeze(2).broadcast_to([P, 32, 16]), op=ALU.subtract))
            assert n_setup[0] == SETUP_DVE, n_setup
            settled()
            dve.wait_ge(act_setup, SETUP_ACT)

            n_rough = dve.alloc_register("n_rough")
            dve.reg_mov(n_rough, 0)

            def over(row, n):
                return row.unsqueeze(1).broadcast_to([P, n, T])

            def idle(n):
                for _ in range(n):
                    yield

            n_due = dve.alloc_register("n_due")
            dve.reg_mov(n_due, 0)

            def root(ch, y, v, w, x, sums, eps, done):
                wait_next(dve, n_due, roots_due)
                ch.step(V.tensor_scalar(v, sums, eps, None, ALU.add))
                ch.step(V.tensor_scalar(y.bitcast(I32), v.bitcast(I32), -0.5, 1597463007.0, ALU.mult, ALU.add))
                for n in range(3):
                    ch.step(V.scalar_tensor_tensor(w, v, -0.5, y, ALU.mult, ALU.mult))
                    ch.step(V.tensor_tensor(x, w, y, op=ALU.mult))
                    y_next = V.scalar_tensor_tensor(y, x, 1.5, y, ALU.add, ALU.mult)
                    if n < 2:
                        ch.step(y_next)
                    else:
                        y_next.then_inc(done.sem, 1)

            def layernorm(nm, i, ch):
                dve.wait_ge(nm.mean_done.sem, nm.mean_done.at(i, 1))
                V.tensor_tensor(nm.cen[:, :, :], nm.src[:, :, :], over(PS[:, nm.mean_bank, 0:T], C),
                                op=ALU.subtract).then_inc(nm.centred.sem, 1)
                yield
                yield
                yield
                root(ch, *[nm.small[:, k, :] for k in range(4)], PS[0:TT, nm.var_bank, 0:3], 1e-5, nm.root_done)
                yield
                dve.wait_ge(nm.root_wide.sem, nm.root_wide.at(i, 1))
                V.tensor_tensor(nm.xn[:, :, :], nm.cen[:, :, :], over(PS[:, nm.mean_bank, 0:T], C),
                                op=ALU.mult).then_inc(nm.done.sem, 1)
                yield

            def token(i):
                ch = Chain(dve, chain_tok, i)
                dve.wait_ge(bands_ready.sem, bands_ready.at(i, 1))
                for k, (c0, n) in enumerate([(480, 24), (384, 96), (0, 384)]):
                    for o in range(3):
                        ch.step(V.tensor_tensor_reduce(
                            out=dotx[:, 0:n], in0=coef[:, c0:c0 + n], in1=wdet[:, o, c0:c0 + n], scale=1.0,
                            scalar=0.0, op0=ALU.mult, op1=ALU.add, accum_out=dots[:, 3 * k + o:3 * k + o + 1]))
                        yield
                V.tensor_tensor_reduce(out=dotx[:, 0:8], in0=avg[:, 160:168], in1=wdet[:, 0, 504:512], scale=1.0,
                                       scalar=0.0, op0=ALU.mult, op1=ALU.add, accum_out=dots[:, 9:10])\
                    .then_inc(dots_ready.sem, 1)
                yield
                dve.wait_ge(logits_summed.sem, logits_summed.at(i, 1))
                ch.step(V.tensor_tensor(z10[:, :], PS[:, 6, 0:10], dscale[:, :], op=ALU.mult))
                ch.step(V.tensor_tensor(z10[:, :], z10[:, :], dbias[:, :], op=ALU.add))
                z9 = z10[:, 0:9].rearrange("p (l o) -> p l o", o=3)
                ch.mark(V.tensor_reduce(mx3[:, :], z9, axis=AX_X, op=ALU.max))
                ch.step(V.tensor_scalar(z10[:, 9:10], z10[:, 9:10], -1.0, None, ALU.mult))
                V.tensor_tensor(z9, z9, mx3[:, :].unsqueeze(2).broadcast_to([P, 3, 3]), op=ALU.subtract)\
                    .then_inc(logits_shifted.sem, 1)
                yield
                dve.wait_ge(weights_exp.sem, weights_exp.at(i, 1))
                e9 = e10[:, 0:9].rearrange("p (l o) -> p l o", o=3)
                ch.mark(V.tensor_reduce(s4[:, 0:3], e9, axis=AX_X, op=ALU.add))
                ch.step(V.tensor_scalar(s4[:, 3:4], e10[:, 9:10], 1.0, None, ALU.add))
                ch.step(V.reciprocal(s4[:, :], s4[:, :]))
                ch.mark(V.tensor_copy(e10[:, 9:10], s4[:, 3:4]))
                ch.step(V.tensor_tensor(e9, e9, s4[:, 0:3].unsqueeze(2).broadcast_to([P, 3, 3]), op=ALU.mult))
                V.tensor_tensor(w10[:, :], e10[:, :], wscale[:, :], op=ALU.mult).then_inc(factors_ready.sem, 1)
                yield
                ch.end()
                yield from idle(8)

            def first(i):
                ch = Chain(dve, chain_a, i)
                yield from idle(2)
                yield from layernorm(n0, i, ch)
                yield from idle(13)
                root(ch, *[qks[:, k, :] for k in range(4)], PS[0:TT, 7, 0:6], 1e-6, qk0_root)
                ch.end()
                yield
                dve.wait_ge(qk0_wide.sem, qk0_wide.at(i, 1))
                for n in (8, 9, 10, 11, 0, 1, 2, 3, 4, 5, 6, 7):
                    for r, m in ((slice(0, P), n),) if n < 8 else ((slice(0, 64), n), (slice(64, P), n + 4)):
                        V.scalar_tensor_tensor(qk[r, m, 0:T], qk[r, m, 0:T], qkw0[r, n:n + 1],
                                               PS[r, 4 + n // 8, 0:T], ALU.mult, ALU.mult)\
                            .then_inc(qk0_ready.sem, 1)
                    if n % 4 == 3:
                        yield
                for h in range(H):
                    wait_next(dve, n_rough, rough0)
                    for t, ((_, tn), (_, kn), kc) in enumerate(zip(TILES, KR0, KC0)):
                        o = PS[0:tn, 5 + h % 3, kc:kc + kn]
                        m = V.tensor_tensor_reduce(out=o, in0=o, in1=biasq[0:tn, h, kc:kc + kn], scale=1.0,
                                                   scalar=-3e38, op0=ALU.add, op1=ALU.max,
                                                   accum_out=mtok[0:tn, t, h:h + 1])
                    m.then_inc(rowmax0.sem, 1)
                    if h % 2:
                        yield
                yield
                yield

            def att0(i):
                def bias(h):
                    dve.wait_ge(scores0.sem, scores0.at(i, h + 1))
                    if h >= 2:
                        dve.wait_ge(probs0.sem, probs0.at(i, h - 1))
                    V.scalar_tensor_tensor(pre[:, h % 2, :], relm[:, :], SLOPES[h], PS[0:TT, h % 2, 0:W0],
                                           ALU.mult, ALU.add).then_inc(biased0.sem, 1)

                def scale(j):
                    dve.wait_ge(rsum_wide.sem, rsum_wide.at(i, j + 1))
                    V.tensor_tensor(y0[:, j, :], y0[:, j, :], PS[:, j % 2, 0:T], op=ALU.mult)\
                        .then_inc(y0_ready.sem, 1)

                bias(0)
                bias(1)
                yield
                for h in range(2, 18):
                    yield
                    if h < H:
                        bias(h)
                    yield
                dve.wait_ge(sums0.sem, sums0.at(i, 4))
                dve.wait_ge(y0_copied.sem, y0_copied.at(i, 8))
                V.reciprocal(rsum[:, :], PS[:, 3, 0:T]).then_inc(rsum_ready.sem, 1)
                yield
                for j in range(8):
                    scale(j)
                    yield
                dve.wait_ge(wo0_done.sem, wo0_done.at(i, 1))
                V.tensor_tensor(h1[:, :, :], h0[:, :, :], PS[:, 2:4, 0:T], op=ALU.add).then_inc(n1.src_ready.sem, 1)
                yield
                yield

            def middle(i):
                ch = Chain(dve, chain_b, i)
                yield from layernorm(n1, i, ch)
                yield
                yield
                dve.wait_ge(absmax_done.sem, absmax_done.at(i, 1))
                ch.step(V.tensor_tensor(fs[:, 0, :], amax[:, 0, :], amax[:, 1, :], op=ALU.max))
                ch.step(V.tensor_scalar(fs[:, 1, :], fs[:, 0, :], 1e-12, 1.0 / 448.0, ALU.max, ALU.mult))
                ch.mark(V.tensor_scalar(fs[:, 3, :], fs[:, 1, :], w8s[:, 0:1], None, ALU.mult))
                ch.step(V.reciprocal(fs[:, 2, :], fs[:, 1, :]))
                yield
                ch.step(V.tensor_tensor(fy[:, :, :], n1.xn[:, :, :], over(fs[:, 2, :], C), op=ALU.mult))
                yield
                ch.step(V.tensor_scalar(fm[:, :, :].bitcast(I32), fy[:, :, :].bitcast(I32), 0x7F800000, None,
                                        ALU.bitwise_and))
                ch.step(V.tensor_scalar(fm[:, :, :], fm[:, :, :], 2.0 ** -6, 1.5 * 2.0 ** 20, ALU.max, ALU.mult))
                ch.step(V.tensor_tensor(fy[:, :, :], fy[:, :, :], fm[:, :, :], op=ALU.add))
                V.tensor_tensor(fq[:, :, :], fy[:, :, :], fm[:, :, :], op=ALU.subtract).then_inc(fq_ready.sem, 1)
                yield
                dve.wait_ge(ffn0_done.sem, ffn0_done.at(i, 1))
                ch.step(V.tensor_tensor(fy[:, :, :], PS[:, 4:6, 0:T], over(fs[:, 3, :], C), op=ALU.mult))
                ch.mark(V.scalar_tensor_tensor(h2[:, 0, :], fy[:, 0, :], b8[:, 0:1], h1[:, 0, :], ALU.add, ALU.add))
                V.scalar_tensor_tensor(h2[:, 1, :], fy[:, 1, :], b8[:, 1:2], h1[:, 1, :], ALU.add, ALU.add)\
                    .then_inc(n2.src_ready.sem, 1)
                yield

                yield from layernorm(n2, i, ch)
                yield from idle(5)
                dve.wait_ge(v1_proj.sem, v1_proj.at(i, 3))
                V.tensor_tensor(vlast[:, :, 0:16], PS[0:H, 4, 0:256].rearrange("p (h d) -> p h d", h=H),
                                ident[0:H, 0:H].unsqueeze(2).broadcast_to([H, H, 16]), op=ALU.mult)\
                    .then_inc(vlast_ready.sem, 1)
                yield
                root(ch, *[root1[:, k, :, :] for k in range(4)],
                     PS[0:TT, 5, 0:96].rearrange("p (t n) -> p t n", t=3), 1e-6, qk1_root)
                yield
                dve.wait_ge(root1_turned.sem, root1_turned.at(i, 1))
                V.tensor_copy(root32[:, :], PS[0:32, 4, 0:T]).then_inc(root1_copied.sem, 1)
                yield
                for n in range(4):
                    dve.wait_ge(qk1_wide.sem, qk1_wide.at(i, n + 1))
                    V.tensor_tensor(u1[:, n, :], u1[:, n, :], PS[:, 4 + n % 2, 0:T], op=ALU.mult)\
                        .then_inc(qk1_normed.sem, 1)
                    yield
                for n in range(4):
                    dve.wait_ge(qk1_turned.sem, qk1_turned.at(i, n + 1))
                    V.tensor_tensor(rsin[:, n, :], PS[:, 4 + n % 2, 0:T], sinT[:, :], op=ALU.mult)\
                        .then_inc(sin_done.sem, 1)
                    ch.step(V.tensor_tensor(qr[:, n, :], u1[:, n, :], cosT[:, :], op=ALU.mult))
                    dve.wait_ge(sin_done.sem, sin_done.at(i, n + 1))
                    V.tensor_tensor(qr[:, n, :], qr[:, n, :], rsin[:, n, :], op=ALU.add).then_inc(rope_done.sem, 1)
                    yield
                dve.wait_ge(rope_done.sem, rope_done.at(i, 4))
                ch.mark(V.tensor_tensor(qlast[:, :, :], headmask[:, :, :],
                                        qr[:, 0:2, 256:257].broadcast_to([P, C, H]), op=ALU.mult))
                V.tensor_tensor(klast[:, :, :], headmask[:, :, :], qr[:, 2:4, 256:257].broadcast_to([P, C, H]),
                                op=ALU.mult).then_inc(last_ready.sem, 1)
                yield
                def rough_keys(h):
                    V.tensor_scalar(kmb[:, h % 4, :], qr[:, 2 + h // 8, 0:256], headmask[:, h // 8, h:h + 1], None,
                                    ALU.mult).then_inc(kmb_ready.sem, 1)

                rough_keys(0)
                rough_keys(1)
                dve.wait_ge(rough_last.sem, rough_last.at(i, 1))
                V.tensor_reduce(mlast[:, :], PS[0:H, 4, 0:T], axis=AX_X, op=ALU.max).then_inc(last_max.sem, 1)
                dve.wait_ge(rough_last.sem, rough_last.at(i, 2))
                V.tensor_copy(mcol1[:, :, :], PS[:, 5, 0:2 * H].rearrange("p (t h) -> p t h", t=2))\
                    .then_inc(last_max.sem, 1)
                yield
                for h in range(H):
                    if h + 2 < H:
                        rough_keys(h + 2)
                    dve.wait_ge(rough1.sem, rough1.at(i, h + 1))
                    V.tensor_reduce(mtok1[:, :, h:h + 1], PS[:, 4 + h % 2, :].rearrange("p (t n) -> p t n", t=2),
                                    axis=AX_X, op=ALU.max).then_inc(rowmax1.sem, 1)
                    if h % 2:
                        yield
                dve.wait_ge(rowmax1.sem, rowmax1.at(i, H))
                V.tensor_tensor(mtok1[:, :, :], mtok1[:, :, :], mcol1[:, :, :], op=ALU.max)\
                    .then_inc(max1_ready.sem, 1)
                V.tensor_scalar(shift1[0:H, 256:257], mlast[:, :], -1.0, None, ALU.mult)\
                    .then_inc(shift1_ready.sem, 1)
                dve.wait_ge(shift1_ready.sem, shift1_ready.at(i, 2))
                V.tensor_tensor(slast[:, :], identb[:, :], shift1[:, 256:257].broadcast_to([P, H]), op=ALU.mult)\
                    .then_inc(slast_ready.sem, 1)
                yield
                yield
                yield
                ch.end()

            def att1(i):
                def scale(n):
                    dve.wait_ge(rz_wide.sem, rz_wide.at(i, n + 1))
                    V.tensor_tensor(zz[:, n, :], zz[:, n, :], PS[:, n % 2, 0:T], op=ALU.mult)\
                        .then_inc(y1_ready.sem, 1)

                def keys(h):
                    if h >= 4:
                        dve.wait_ge(scores1.sem, scores1.at(i, h - 3))
                    c = h // 8
                    V.tensor_scalar(km[:, h % 4, :], qr[:, 2 + c, 0:256], headmask[:, c, h:h + 1], None,
                                    ALU.mult).then_inc(km_ready.sem, 1)

                dve.wait_ge(rope_done.sem, rope_done.at(i, 4))
                keys(0)
                keys(1)
                for h in range(H):
                    if h + 2 < H:
                        keys(h + 2)
                    yield
                    yield
                yield
                dve.wait_ge(sums1.sem, sums1.at(i, 1))
                V.reciprocal(rz[:, :], PS[0:H, 0, 0:T]).then_inc(rz_ready.sem, 1)
                yield
                for n in range(4):
                    scale(n)
                    yield
                dve.wait_ge(proj1_done.sem, proj1_done.at(i, 1))
                V.tensor_tensor(h3[:, :, :], h2[:, :, :], PS[:, 2:4, 0:T], op=ALU.add).then_inc(n3.src_ready.sem, 1)
                yield
                yield

            def last(i):
                ch = Chain(dve, chain_c, i)
                yield from layernorm(n3, i, ch)
                dve.wait_ge(gates.sem, gates.at(i, 1))
                V.tensor_copy(lg[:, bass.ds(i * 3, 2), :], PS[0:TT, 7, 0:2 * NE].rearrange("p (t e) -> p t e", e=NE))\
                    .then_inc(gates_kept.sem, 1)
                V.tensor_copy(lg[0:85, bass.ds(i * 3 + 2, 1), :],
                              PS[0:85, 7, 2 * NE:3 * NE].rearrange("p (t e) -> p t e", e=NE))\
                    .then_inc(gates_kept.sem, 1)
                yield
                for n in range(2):
                    dve.wait_ge(gate_copied.sem, gate_copied.at(i, n + 1))
                    ch.step(V.scalar_tensor_tensor(gate_in[:, n, :], half_t[:, n, 0:T], 1.0, gate_in[:, n, :],
                                                   ALU.add, ALU.mult))
                    yield
                    dve.wait_ge(value_done.sem, value_done.at(i, n + 1))
                    V.tensor_tensor(hh[:, n, :], gate_in[:, n, :], PS[:, 7, 0:T], op=ALU.mult)\
                        .then_inc(hh_ready.sem, 1)
                    yield
                ch.end()
                yield from idle(4)

            schedule(dve, {"token": token, "first": first, "att0": att0, "middle": middle, "att1": att1, "last": last})

            steps = [0]

            def mark(ins):
                steps[0] += 1
                ins.then_inc(tail_chain, 1)

            def step(ins):
                mark(ins)
                dve.wait_ge(tail_chain, steps[0])

            def per_expert(x):
                return x.unsqueeze(2).broadcast_to([TT, NCOL, NE])

            dve.wait_ge(gates_kept.sem, gates_kept.at(NB - 1, 2))
            step(V.tensor_reduce(r1[:, :], lg[:, :, :], axis=AX_X, op=ALU.max))
            V.tensor_tensor(rt[:, :, :], lg[:, :, :], per_expert(r1[:, :]), op=ALU.subtract)\
                .then_inc(logits_shifted.sem, 1)
            dve.wait_ge(weights_exp.sem, weights_exp.at(NB, 1))
            step(V.tensor_reduce(r1[:, :], prob[:, :, :], axis=AX_X, op=ALU.add))
            step(V.reciprocal(r1[:, :], r1[:, :]))
            step(V.tensor_tensor(prob[:, :, :], prob[:, :, :], per_expert(r1[:, :]), op=ALU.mult))
            step(V.tensor_tensor(rt[:, :, :], prob[:, :, :], ebias[0:TT, :].unsqueeze(1)
                                 .broadcast_to([TT, NCOL, NE]), op=ALU.add))
            s2 = rt[:, :, :].rearrange("p n (g e) -> p n g e", e=2)
            gs, beat, tmp = g4[:, 0], g4[:, 1], g4[:, 2]
            step(V.tensor_tensor(gs, s2[:, :, :, 0], s2[:, :, :, 1], op=ALU.add))
            step(V.memset(beat, 0.0))

            def rank(score, count, scratch, width):
                for k in range(width):
                    for lo, hi, op in ((0, k, ALU.is_gt), (k + 1, width, ALU.is_ge)):
                        if lo < hi:
                            rival = score[:, :, k:k + 1].broadcast_to([TT, NCOL, hi - lo])
                            step(V.tensor_tensor(scratch[:, :, lo:hi], rival, score[:, :, lo:hi], op=op))
                            step(V.tensor_tensor(count[:, :, lo:hi], count[:, :, lo:hi], scratch[:, :, lo:hi],
                                                 op=ALU.add))

            rank(gs, beat, tmp, 4)
            step(V.tensor_scalar(tmp, beat, 1.5, None, ALU.is_lt))
            step(V.tensor_scalar(beat, tmp, -MASKED, MASKED, ALU.mult, ALU.add))
            for e in range(2):
                step(V.tensor_tensor(s2[:, :, :, e], s2[:, :, :, e], tmp, op=ALU.mult))
                step(V.tensor_tensor(s2[:, :, :, e], s2[:, :, :, e], beat, op=ALU.add))
            step(V.memset(rk[:, :, :], 0.0))
            scratch = ge[:, 0:NCOL, :]
            rank(rt, rk, scratch, NE)
            for s in range(2):
                step(V.tensor_scalar(onehot[:, :, s, :], rk[:, :, :], float(s), None, ALU.is_equal))
                step(V.tensor_tensor(scratch, onehot[:, :, s, :], prob[:, :, :], op=ALU.mult))
                step(V.tensor_reduce(weight[:, :, s:s + 1], scratch, axis=AX_X, op=ALU.add))
                step(V.tensor_tensor(onehot[:, :, s, :], onehot[:, :, s, :], per_expert(valid[:, :]), op=ALU.mult))
            step(V.tensor_tensor(scratch, onehot[:, :, 0, :], onehot[:, :, 1, :], op=ALU.add))
            V.tensor_reduce(cnt[0:TT, :], scratch.rearrange("p n e -> p e n"), axis=AX_X, op=ALU.add)\
                .then_inc(counts_ready, 1)
            dve.wait_ge(counts_summed, 1)
            step(V.tensor_copy(offs[:, :], PS[0:TT, 4, 0:NE]))
            for e in range(1, NE):
                step(V.tensor_tensor(offs[:, e:e + 1], offs[:, e:e + 1], offs[:, e - 1:e], op=ALU.add))
            flat = pos[:, :, :].rearrange("p n s -> p (n s)").unsqueeze(2).broadcast_to([TT, NCOL * 2, NE])
            step(V.tensor_tensor(ge[:, :, :], flat, offs[:, :].unsqueeze(1).broadcast_to([TT, NCOL * 2, NE]),
                                 op=ALU.is_lt))
            gr = group[:, :, :, :].rearrange("p n s g -> p (n s) g")
            step(V.tensor_copy(gr[:, :, 0:1], ge[:, :, 0:1]))
            step(V.tensor_tensor(gr[:, :, 1:NE], ge[:, :, 1:NE], ge[:, :, 0:NE - 1], op=ALU.subtract))

            V.memset(acct[:, :], 0.0).then_inc(acc_copied, 1)

            n_steps = steps[0]
            ONES = onehot[:, :, :, :].rearrange("p n s e -> p (n s) e")
            WGT = weight[:, :, :].rearrange("p n s -> p (n s)")
            for t in (u64, *oht):
                V.memset(t[64:P, :], 0.0).then_inc(rows_cleared, 1)

            def one_hots(r, k, first=False):
                at = bass.ds(r * 8, 8)
                o4 = oh[k][:, :, :].rearrange("p n (e g) -> p n e g", g=NE)
                V.tensor_tensor(o4, ONES[:, at, :].unsqueeze(3).broadcast_to([TT, 8, NE, NE]),
                                gr[:, at, :].unsqueeze(2).broadcast_to([TT, 8, NE, NE]), op=ALU.mult)\
                    .then_inc(tail_chain, 1)
                dve.wait_ge(tail_chain, n_steps + 1 if first else r * 2 + n_steps)
                V.tensor_tensor(ohw[k][:, :, :], oh[k][:, :, :], WGT[:, at].unsqueeze(2).broadcast_to([TT, 8, 64]),
                                op=ALU.mult).then_inc(onehots_ready.sem, 1)

            def copy_turned(r, k):
                dve.wait_ge(onehots_turned.sem, onehots_turned.at(r, 1))
                V.tensor_copy(oht[k][0:64, :].rearrange("p (b n) -> p b n", b=2), PS[0:64, 4:6, 0:4 * TT])\
                    .then_inc(turned_copied.sem, 1)

            def routed_round(r, k, more):
                if more:
                    one_hots(r + 1, 1 - k)
                    copy_turned(r + 1, 1 - k)
                dve.wait_ge(routed_tanh.sem, routed_tanh.at(r, 1))
                up = PS[0:TT, 0:4, :].rearrange("p b (n s d) -> p (b n) s d", n=2, s=2)
                V.scalar_tensor_tensor(he[:, :, :], he[:, :, :], 1.0, up[:, :, 0, :], ALU.add, ALU.mult)\
                    .then_inc(tail_chain, 1)
                dve.wait_ge(tail_chain, r * 2 + (n_steps + (3 if more else 2)))
                V.scalar_tensor_tensor(hs[:, :, :], he[:, :, :], 0.5, up[:, :, 1, :], ALU.mult, ALU.mult)\
                    .then_inc(routed_h.sem, 1)
                dve.wait_ge(routed_added.sem, routed_added.at(r, 1))
                dve.wait_ge(acc_copied, r + 1)
                V.tensor_tensor(acct[:, :], acct[:, :], PS[0:64, 6, 0:HID], op=ALU.add).then_inc(acc_copied, 1)

            one_hots(0, 0, True)
            copy_turned(0, 0)
            with dve.Fori(0, ROUNDS // 2 - 1) as pair:
                for k in range(2):
                    routed_round(pair * 2 + k, k, True)
            for k in range(2):
                routed_round(ROUNDS - 2 + k, k, k == 0)
            dve.wait_ge(acc_turned, 1)
            V.tensor_copy(accT[:, :], PS[:, 4, 0:64]).then_inc(accT_ready, 1)
            dve.wait_ge(routed_out, 1)
            dve.wait_ge(rows_loaded, 16)
            V.tensor_tensor(r8, r8, PS[0:8, 5, 0:256], op=ALU.add).then_inc(rows_ready, 1)


def tables():
    k = np.arange(P)
    t = {"ident": np.eye(P, dtype=np.float32)}
    t["block8"] = (k[:, None] // 16 == np.arange(8)[None, :]).astype(np.float32) / 16
    hd = np.arange(H)
    t["headmask"] = (hd == 8 * np.arange(C)[None, :, None] + k[:, None, None] // 16).astype(np.float32)
    col = np.arange(32)
    sel = (col[None, :] == np.arange(4)[:, None]) | (col[None, :] >= 4)
    t["sumsel"] = np.tile(sel.astype(np.float32)[None], (P, 1, 1))
    head = 2 * np.arange(8)[:, None] + (k[None, :] >= 64)
    t["sumback"] = (k[:, None, None] == 32 * (head % 4) + head // 4).astype(np.float32)
    own = hd[None, None, :] == 4 * np.arange(4)[None, :, None] + k[:, None, None] // 32
    t["collect"] = (own & (k[:, None, None] % 32 == 16)).astype(np.float32)
    tile_head = 8 * np.arange(4)[None, :, None] + k[None, None, :] // 16
    t["expand"] = (np.arange(32)[:, None, None] == tile_head).astype(np.float32)
    t["spread"] = own.transpose(2, 1, 0).astype(np.float32)
    rot = np.zeros((P, P), np.float32)
    for m in range(P):
        if m % 16 < 8:
            rot[m + 8, m] = -1.0
        else:
            rot[m - 8, m] = 1.0
    t["rotate"] = rot
    freq = np.float32(1.0) / np.float32(10000.0) ** (np.arange(8, dtype=np.float32) / np.float32(8))
    ang = (np.arange(T, dtype=np.float32)[None, :] * freq[k % 8][:, None]).astype(np.float32)
    t["cosT"], t["sinT"] = np.cos(ang).astype(np.float32), np.sin(ang).astype(np.float32)
    relm = np.full((TT, W0), MASKED, np.float32)
    for n, ((q0, qn), c0) in enumerate(zip(QR0, QC0)):
        key, q = n * TT + np.arange(TT)[:, None], q0 + np.arange(qn)[None, :]
        ok = (key <= q) & (key >= q - WINDOW) & (key < T)
        relm[:, c0:c0 + qn] = np.where(ok, (key - q).astype(np.float32), MASKED)
    t["relm"] = relm
    relq = np.full((TT, W2), MASKED, np.float32)
    for n, ((k0, kn), c0) in enumerate(zip(KR0, KC0)):
        q, key = n * TT + np.arange(TT)[:, None], k0 + np.arange(kn)[None, :]
        ok = (key <= q) & (key >= q - WINDOW)
        relq[:, c0:c0 + kn] = np.where(ok, (key - q).astype(np.float32), MASKED)
    t["relq"] = relq
    p, col = np.arange(TT)[:, None], np.arange(NCOL)[None, :]
    token = (NB - 1 - col // 3) * T + (col % 3) * TT + p
    t["pos"] = np.stack([2 * token, 2 * token + 1], -1).astype(np.float32)
    t["valid"] = ((col % 3) * TT + p < T).astype(np.float32)
    level = np.array([8, 8, 8, 4, 4, 4, 2, 2, 2, 8], np.float32)
    t["dscale"] = np.tile(1 / level, (P, 1)).astype(np.float32)
    t["wscale"] = np.tile(1 / level ** 2, (P, 1)).astype(np.float32)
    return t


def blocks(x, rows, cols):
    lead = x.shape[:-2]
    n = len(lead)
    y = x.reshape(*lead, 32, rows, 4, cols)
    return y.transpose(*range(n), n + 2, n, n + 1, n + 3).reshape(*lead, P, rows * cols)


def halves(w):
    return w.reshape(C, P, -1).transpose(1, 0, 2)


def layout(d):
    r = {}
    r["x"] = blocks(d["x"][::-1, :, :, 0], 8, 64)
    r["wq0"] = halves(d["L0_attn_wq"].T)
    r["wk0"] = halves(d["L0_attn_wk"].T)
    r["wv0"] = halves(d["L0_attn_wv"].T)
    r["wo0"] = d["L0_attn_wo"].T.reshape(8, P, 256).transpose(1, 0, 2)
    kn = np.repeat(d["L0_attn_k_norm_w"].reshape(KV, 1, 64), 2, axis=1).reshape(KV, P)
    r["qkw0"] = np.concatenate([d["L0_attn_q_norm_w"].reshape(8, P), kn]).T
    r["w8"] = halves(d["L0_ffn_weight"].view(np.uint8).T)
    r["w8s"] = np.broadcast_to(d["L0_ffn_weight_scale"].reshape(1, 1), (P, 1))
    r["b8"] = d["L0_ffn_bias"].reshape(C, P).T
    r["wqk1"] = halves(d["L1_attn_w_qkv"][0:512].T)
    r["wv1"] = halves(d["L1_attn_w_qkv"][512:768].T)
    wp = np.zeros((H, 32, 256), np.float32)
    wp[:, 0:16] = d["L1_attn_w_proj"].T.reshape(H, 16, 256)
    wp[0, 16] = d["L1_attn_b_proj"]
    r["wp1"] = wp.reshape(4, P, 256).transpose(1, 0, 2)
    r["gb1"] = np.stack([np.tile(d["L1_attn_" + n], 8) for n in ("q_gamma", "k_gamma", "q_beta", "k_beta")], 1)
    r["wg"] = halves(d["L1_ffn_w_gate"].T)
    r["sw13"] = halves(np.concatenate([d["L1_ffn_sw1"].T, d["L1_ffn_sw3"].T], 1))
    r["sw2"] = halves(d["L1_ffn_sw2"].T)
    for n, name in (("ew1", "L1_ffn_w1"), ("ew3", "L1_ffn_w3")):
        r[n] = halves(d[name].transpose(1, 0, 2).reshape(256, NE * HID))
    r["ew2"] = d["L1_ffn_w2"].transpose(1, 0, 2)
    r["ebias"] = np.tile(d["L1_ffn_expert_bias"][None], (P, 1))
    r["clst"] = d["cls_tok"].reshape(C, P).T
    parts = []
    for name, n in (("L0_tok_Wd3", 128), ("L0_tok_Wd2", 64), ("L0_tok_Wd1", 32)):
        w = blocks(d[name].T.reshape(3, 3, n, n), n // 32, n // 4)
        parts.append(w.transpose(2, 0, 1, 3).reshape(P, 3, -1))
    wa = blocks(d["L0_tok_Wa"].reshape(32, 32), 1, 8)
    parts.append(np.broadcast_to(wa[:, None, :], (P, 3, 8)))
    r["wdet"] = np.concatenate(parts, 2)
    bias = np.concatenate([d["L0_tok_" + n] for n in ("bd1", "bd2", "bd3", "ba")])
    r["dbias"] = np.tile(bias[None], (P, 1))
    return r


def kernel(**inputs):
    import concourse.bacc as bacc
    from concourse.bass_utils import run_bass_kernel_spmd

    nc = bacc.Bacc("TRN2", target_bir_lowering=False, num_devices=1)
    data = layout({k: np.asarray(v) for k, v in inputs.items()})
    data.update(tables())
    arrays = {f"in_{k}": np.ascontiguousarray(v) for k, v in data.items()}
    aps = {k: nc.dram_tensor(f"in_{k}", arrays[f"in_{k}"].shape, mybir.dt.from_np(arrays[f"in_{k}"].dtype),
                             kind="ExternalInput").ap() for k in data}
    out = nc.dram_tensor("out_tokens", (NB, T, 256), F32, kind="ExternalOutput").ap()
    build_tower(nc, aps, out)
    result = run_bass_kernel_spmd(nc, [arrays], core_ids=[0])
    return result.results[0]["out_tokens"][::-1]
```
